# Optimizing a Trainium2 kernel written in Bass

```python
import numpy as np
import jax
import jax.numpy as jnp

def _softmax(x, axis=-1):
    return jax.nn.softmax(x, axis=axis)

def _gelu(x):
    return jax.nn.gelu(x, approximate=True)

def _silu(x):
    return jax.nn.silu(x)

def _sigmoid(x):
    return jax.nn.sigmoid(x)

def _layernorm(x, axis=-1, eps=1e-05):
    m = jnp.mean(x, axis=axis, keepdims=True)
    v = jnp.var(x, axis=axis, keepdims=True)
    return (x - m) / jnp.sqrt(v + eps)

def _scatter_add(tgt, idx, src, axis=0):
    return tgt.at[idx].add(src)

def _segment_sum(src, seg, n):
    return jax.ops.segment_sum(src, seg, n)
kernel_name = 'mk_gnn_ffn_d2_gnn_r8_56684d'

def setup_inputs(seed: int=0):
    np.random.seed(seed)
    _w = jnp.asarray

    def _rec_inputs():
        import jax
        import jax.numpy as jnp
        _gk = jax.random.key(seed)
        x = -8.776e-05 + 1 * jax.random.normal(jax.random.fold_in(_gk, 1), (2500, 256), jnp.float32)
        src = jax.random.randint(jax.random.fold_in(_gk, 2), (40000,), 0, 2500, jnp.int32)
        dst = jax.random.randint(jax.random.fold_in(_gk, 3), (40000,), 0, 2500, jnp.int32)
        _o = jnp.argsort(dst, stable=True)
        src = src[_o]
        dst = dst[_o]
        edge_attr_64 = 1.36993e-05 + 0.999972 * jax.random.normal(jax.random.fold_in(_gk, 12), (40000, 64), jnp.float32)
        edge_type_8 = jax.random.randint(jax.random.fold_in(_gk, 14), (40000,), 0, 8, jnp.int32)
        edge_weight = jax.random.uniform(jax.random.fold_in(_gk, 15), (40000,), jnp.float32, 0.0, 0.999998)
        return (x, src, dst, edge_attr_64, edge_type_8, edge_weight)
    x, src, dst, edge_attr_64, edge_type_8, edge_weight = _rec_inputs()

    def _L0_gnn_setup():
        import jax, jax.numpy as jnp
        import numpy as np
        N_NODES = 2500
        N_EDGES = 37500
        D = 256
        NUM_RELS = 8
        NUM_BASES = 4
        key = jax.random.key(seed)
        ks = jax.random.split(key, 8)
        x = jax.random.normal(ks[0], (N_NODES, D), dtype=jnp.float32)
        src = jax.random.randint(ks[1], (N_EDGES,), 0, N_NODES, dtype=jnp.int32)
        dst = jax.random.randint(ks[2], (N_EDGES,), 0, N_NODES, dtype=jnp.int32)
        etypes = jax.random.randint(ks[3], (N_EDGES,), 0, NUM_RELS, dtype=jnp.int32)
        scale = 1.0 / np.sqrt(D)
        basis = jax.random.normal(ks[4], (NUM_BASES, D, D), dtype=jnp.float32) * scale
        comp = jax.random.normal(ks[5], (NUM_RELS, NUM_BASES), dtype=jnp.float32)
        loop_weight = jax.random.normal(ks[6], (D, D), dtype=jnp.float32) * scale
        bias_param = jnp.zeros((D,), dtype=jnp.float32)
        return {'x': x, 'src': src, 'dst': dst, 'etypes': etypes, 'basis': basis, 'comp': comp, 'loop_weight': loop_weight, 'bias_param': bias_param}
    _L0_gnn_all = _L0_gnn_setup()
    _L0_gnn_in = {k: v for k, v in _L0_gnn_all.items() if k in ('basis', 'comp', 'loop_weight', 'bias_param')}
    del _L0_gnn_all

    def _L0_ffn_setup():
        import jax, jax.numpy as jnp
        import numpy as np
        E, D, H, TOP_K = (6, 256, 256, 2)
        ROUTER_H = D // 2
        key = jax.random.key(seed)
        ks = jax.random.split(key, 12)
        s = 1.0 / np.sqrt(D)
        sh = 1.0 / np.sqrt(H)
        sr = 1.0 / np.sqrt(ROUTER_H)
        return {'features': jax.random.normal(ks[0], (8, 512, D), dtype=jnp.float32), 'router_w1': jax.random.uniform(ks[1], (D, ROUTER_H), jnp.float32, -s, s), 'router_b1': jnp.zeros((ROUTER_H,), jnp.float32), 'router_w2': jax.random.uniform(ks[2], (ROUTER_H, E), jnp.float32, -sr, sr), 'router_b2': jnp.zeros((E,), jnp.float32), 'expert_w1': jax.random.uniform(ks[3], (E, D, H), jnp.float32, -s, s), 'expert_b1': jnp.zeros((E, H), jnp.float32), 'expert_w2': jax.random.uniform(ks[4], (E, H, H), jnp.float32, -sh, sh), 'expert_b2': jnp.zeros((E, H), jnp.float32), 'expert_w3': jax.random.uniform(ks[5], (E, H, D), jnp.float32, -sh, sh), 'expert_b3': jnp.zeros((E, D), jnp.float32)}
    _L0_ffn_all = _L0_ffn_setup()
    _L0_ffn_in = {k: v for k, v in _L0_ffn_all.items() if k in ('router_w1', 'router_b1', 'router_w2', 'router_b2', 'expert_w1', 'expert_b1', 'expert_w2', 'expert_b2', 'expert_w3', 'expert_b3')}
    del _L0_ffn_all

    def _L1_gnn_setup():
        import jax, jax.numpy as jnp
        import numpy as np
        N = 2500
        E = 40000
        D = 256
        H = 8
        DH = D // H
        ED = 64
        FF = 4 * D
        EPS = 1e-05

        def _layernorm(x, g, b):
            m = jnp.mean(x, axis=-1, keepdims=True)
            v = jnp.var(x, axis=-1, keepdims=True)
            return (x - m) * jax.lax.rsqrt(v + EPS) * g + b

        def _edge_attention(xn, edge_index, ef, ew, Wq, bq, Wk, bk, Wv, bv, We, be, Wo, bo):
            n = xn.shape[0]
            scale = DH ** (-0.5)
            q = (xn @ Wq + bq).reshape(n, H, DH)
            k = (xn @ Wk + bk).reshape(n, H, DH)
            v = (xn @ Wv + bv).reshape(n, H, DH)
            src, dst = (edge_index[0], edge_index[1])
            ep = ef @ We + be
            scores = jnp.einsum('ehd,ehd->eh', q[dst], k[src] + ep[:, None, :]) * scale
            scores = scores * ew[:, None]
            m = jax.ops.segment_max(scores, dst, num_segments=n)
            m = jnp.where(jnp.isfinite(m), m, 0.0)
            ex = jnp.exp(scores - m[dst])
            s = jax.ops.segment_sum(ex, dst, num_segments=n)
            attn = ex / s[dst]
            out = jax.ops.segment_sum(attn[:, :, None] * v[src], dst, num_segments=n)
            out = out.reshape(n, D) @ Wo + bo
            return out
        key = jax.random.key(seed)
        ks = jax.random.split(key, 32)

        def lin_w(k, i, o):
            return (jax.random.normal(k, (i, o), jnp.float32) / np.sqrt(i)).astype(jnp.float32)
        return {'x': jax.random.normal(ks[0], (N, D), jnp.float32), 'edge_features': jax.random.normal(ks[1], (E, ED), jnp.float32), 'edge_weights': jax.random.uniform(ks[2], (E,), jnp.float32), 'edge_index': jax.random.randint(ks[3], (2, E), 0, N, dtype=jnp.int32), 'Wq': lin_w(ks[4], D, D), 'bq': jnp.zeros((D,), jnp.float32), 'Wk': lin_w(ks[5], D, D), 'bk': jnp.zeros((D,), jnp.float32), 'Wv': lin_w(ks[6], D, D), 'bv': jnp.zeros((D,), jnp.float32), 'We': lin_w(ks[7], ED, DH), 'be': jnp.zeros((DH,), jnp.float32), 'Wo': lin_w(ks[8], D, D), 'bo': jnp.zeros((D,), jnp.float32), 'ln1_g': jnp.ones((D,), jnp.float32), 'ln1_b': jnp.zeros((D,), jnp.float32), 'ln2_g': jnp.ones((D,), jnp.float32), 'ln2_b': jnp.zeros((D,), jnp.float32), 'W1': lin_w(ks[9], D, FF), 'b1': jnp.zeros((FF,), jnp.float32), 'W2': lin_w(ks[10], FF, D), 'b2': jnp.zeros((D,), jnp.float32), 'alpha': jnp.ones((1,), jnp.float32), 'beta': jnp.ones((1,), jnp.float32)}
    _L1_gnn_all = _L1_gnn_setup()
    _L1_gnn_in = {k: v for k, v in _L1_gnn_all.items() if k in ('Wq', 'bq', 'Wk', 'bk', 'Wv', 'bv', 'We', 'be', 'Wo', 'bo', 'ln1_g', 'ln1_b', 'ln2_g', 'ln2_b', 'W1', 'b1', 'W2', 'b2', 'alpha', 'beta')}
    del _L1_gnn_all

    def _L1_ffn_setup():
        import jax, jax.numpy as jnp
        import numpy as np
        NUM_EXPERTS = 8
        TOP_K = 2
        B, S, D = (8, 1024, 256)

        def _moe(tokens, router_w, w1, b1, w2, b2):
            N = tokens.shape[0]
            E = router_w.shape[0]
            logits = tokens.astype(jnp.float32) @ router_w.astype(jnp.float32).T
            probs = jax.nn.softmax(logits, axis=-1)
            rw, re = jax.lax.top_k(probs, TOP_K)
            if TOP_K > 1:
                rw = rw / jnp.maximum(rw.sum(-1, keepdims=True), 1e-12)
            rw = rw.astype(tokens.dtype)
            combine = jnp.zeros((N, E), tokens.dtype).at[jnp.arange(N)[:, None], re].set(rw)
            out = tokens
            for e in range(E):
                h = jax.nn.gelu(tokens @ w1[e] + b1[e], approximate=False)
                y = h @ w2[e] + b2[e]
                out = out + combine[:, e:e + 1] * y
            return out
        key = jax.random.key(seed)
        ks = jax.random.split(key, 4)
        scale = 1.0 / np.sqrt(D).astype(np.float32)
        return {'input_embeddings': jax.random.normal(ks[0], (B, S, D), jnp.float32), 'router_w': jax.random.normal(ks[1], (NUM_EXPERTS, D), jnp.float32) * scale, 'w1': jax.random.normal(ks[2], (NUM_EXPERTS, D, D), jnp.float32) * scale, 'b1': jnp.zeros((NUM_EXPERTS, D), jnp.float32), 'w2': jax.random.normal(ks[3], (NUM_EXPERTS, D, D), jnp.float32) * scale, 'b2': jnp.zeros((NUM_EXPERTS, D), jnp.float32)}
    _L1_ffn_all = _L1_ffn_setup()
    _L1_ffn_in = {k: v for k, v in _L1_ffn_all.items() if k in ('router_w', 'w1', 'b1', 'w2', 'b2')}
    del _L1_ffn_all
    return {'x': x, 'src': src, 'dst': dst, 'edge_attr_64': edge_attr_64, 'edge_type_8': edge_type_8, 'edge_weight': edge_weight, 'L0_gnn_basis': _L0_gnn_in['basis'], 'L0_gnn_comp': _L0_gnn_in['comp'], 'L0_gnn_loop_weight': _L0_gnn_in['loop_weight'], 'L0_gnn_bias_param': _L0_gnn_in['bias_param'], 'L0_ffn_router_w1': _L0_ffn_in['router_w1'], 'L0_ffn_router_b1': _L0_ffn_in['router_b1'], 'L0_ffn_router_w2': _L0_ffn_in['router_w2'], 'L0_ffn_router_b2': _L0_ffn_in['router_b2'], 'L0_ffn_expert_w1': _L0_ffn_in['expert_w1'], 'L0_ffn_expert_b1': _L0_ffn_in['expert_b1'], 'L0_ffn_expert_w2': _L0_ffn_in['expert_w2'], 'L0_ffn_expert_b2': _L0_ffn_in['expert_b2'], 'L0_ffn_expert_w3': _L0_ffn_in['expert_w3'], 'L0_ffn_expert_b3': _L0_ffn_in['expert_b3'], 'L1_gnn_Wq': _L1_gnn_in['Wq'], 'L1_gnn_bq': _L1_gnn_in['bq'], 'L1_gnn_Wk': _L1_gnn_in['Wk'], 'L1_gnn_bk': _L1_gnn_in['bk'], 'L1_gnn_Wv': _L1_gnn_in['Wv'], 'L1_gnn_bv': _L1_gnn_in['bv'], 'L1_gnn_We': _L1_gnn_in['We'], 'L1_gnn_be': _L1_gnn_in['be'], 'L1_gnn_Wo': _L1_gnn_in['Wo'], 'L1_gnn_bo': _L1_gnn_in['bo'], 'L1_gnn_ln1_g': _L1_gnn_in['ln1_g'], 'L1_gnn_ln1_b': _L1_gnn_in['ln1_b'], 'L1_gnn_ln2_g': _L1_gnn_in['ln2_g'], 'L1_gnn_ln2_b': _L1_gnn_in['ln2_b'], 'L1_gnn_W1': _L1_gnn_in['W1'], 'L1_gnn_b1': _L1_gnn_in['b1'], 'L1_gnn_W2': _L1_gnn_in['W2'], 'L1_gnn_b2': _L1_gnn_in['b2'], 'L1_gnn_alpha': _L1_gnn_in['alpha'], 'L1_gnn_beta': _L1_gnn_in['beta'], 'L1_ffn_router_w': _L1_ffn_in['router_w'], 'L1_ffn_w1': _L1_ffn_in['w1'], 'L1_ffn_b1': _L1_ffn_in['b1'], 'L1_ffn_w2': _L1_ffn_in['w2'], 'L1_ffn_b2': _L1_ffn_in['b2']}

def reference(x, src, dst, edge_attr_64, edge_type_8, edge_weight, L0_gnn_basis, L0_gnn_comp, L0_gnn_loop_weight, L0_gnn_bias_param, L0_ffn_router_w1, L0_ffn_router_b1, L0_ffn_router_w2, L0_ffn_router_b2, L0_ffn_expert_w1, L0_ffn_expert_b1, L0_ffn_expert_w2, L0_ffn_expert_b2, L0_ffn_expert_w3, L0_ffn_expert_b3, L1_gnn_Wq, L1_gnn_bq, L1_gnn_Wk, L1_gnn_bk, L1_gnn_Wv, L1_gnn_bv, L1_gnn_We, L1_gnn_be, L1_gnn_Wo, L1_gnn_bo, L1_gnn_ln1_g, L1_gnn_ln1_b, L1_gnn_ln2_g, L1_gnn_ln2_b, L1_gnn_W1, L1_gnn_b1, L1_gnn_W2, L1_gnn_b2, L1_gnn_alpha, L1_gnn_beta, L1_ffn_router_w, L1_ffn_w1, L1_ffn_b1, L1_ffn_w2, L1_ffn_b2):
    import jax
    import jax.numpy as jnp

    def _L0_gnn_ref(x, src, dst, etypes, basis, comp, loop_weight, bias_param):
        import jax, jax.numpy as jnp
        import numpy as np
        N_NODES = 2500
        N_EDGES = 37500
        D = 256
        NUM_RELS = 8
        NUM_BASES = 4
        W = jnp.einsum('rb,bio->rio', comp, basis)
        H = jnp.einsum('ni,rio->nro', x, W)
        msg = H[src, etypes]
        agg = jax.ops.segment_sum(msg, dst, num_segments=N_NODES)
        out = agg + x @ loop_weight + bias_param
        return out

    def _L0_ffn_ref(features, router_w1, router_b1, router_w2, router_b2, expert_w1, expert_b1, expert_w2, expert_b2, expert_w3, expert_b3):
        import jax, jax.numpy as jnp
        import numpy as np
        E, D, H, TOP_K = (6, 256, 256, 2)
        ROUTER_H = D // 2
        rh = jax.nn.relu(features @ router_w1 + router_b1)
        expert_logits = jax.nn.softmax(rh @ router_w2 + router_b2, axis=-1)
        top_w, top_i = jax.lax.top_k(expert_logits, TOP_K)
        routing_weights = jax.nn.softmax(top_w, axis=-1)
        h1 = jax.nn.relu(jnp.einsum('bsd,edh->bseh', features, expert_w1) + expert_b1)
        h2 = jax.nn.relu(jnp.einsum('bseh,ehf->bsef', h1, expert_w2) + expert_b2)
        expert_out = jnp.einsum('bsef,efo->bseo', h2, expert_w3) + expert_b3
        sel = jnp.take_along_axis(expert_out, top_i[:, :, :, None], axis=2)
        combined = jnp.sum(sel * routing_weights[..., None], axis=2)
        return combined

    def _L1_gnn_ref(x, edge_features, edge_weights, edge_index, Wq, bq, Wk, bk, Wv, bv, We, be, Wo, bo, ln1_g, ln1_b, ln2_g, ln2_b, W1, b1, W2, b2, alpha, beta):
        import jax, jax.numpy as jnp
        import numpy as np
        N = 2500
        E = 40000
        D = 256
        H = 8
        DH = D // H
        ED = 64
        FF = 4 * D
        EPS = 1e-05

        def _layernorm(x, g, b):
            m = jnp.mean(x, axis=-1, keepdims=True)
            v = jnp.var(x, axis=-1, keepdims=True)
            return (x - m) * jax.lax.rsqrt(v + EPS) * g + b

        def _edge_attention(xn, edge_index, ef, ew, Wq, bq, Wk, bk, Wv, bv, We, be, Wo, bo):
            n = xn.shape[0]
            scale = DH ** (-0.5)
            q = (xn @ Wq + bq).reshape(n, H, DH)
            k = (xn @ Wk + bk).reshape(n, H, DH)
            v = (xn @ Wv + bv).reshape(n, H, DH)
            src, dst = (edge_index[0], edge_index[1])
            ep = ef @ We + be
            scores = jnp.einsum('ehd,ehd->eh', q[dst], k[src] + ep[:, None, :]) * scale
            scores = scores * ew[:, None]
            m = jax.ops.segment_max(scores, dst, num_segments=n)
            m = jnp.where(jnp.isfinite(m), m, 0.0)
            ex = jnp.exp(scores - m[dst])
            s = jax.ops.segment_sum(ex, dst, num_segments=n)
            attn = ex / s[dst]
            out = jax.ops.segment_sum(attn[:, :, None] * v[src], dst, num_segments=n)
            out = out.reshape(n, D) @ Wo + bo
            return out
        xn = _layernorm(x, ln1_g, ln1_b)
        attn_out = _edge_attention(xn, edge_index, edge_features, edge_weights, Wq, bq, Wk, bk, Wv, bv, We, be, Wo, bo)
        x = x + alpha * attn_out
        xn = _layernorm(x, ln2_g, ln2_b)
        ff = jax.nn.gelu(xn @ W1 + b1, approximate=False) @ W2 + b2
        x = x + beta * ff
        return x

    def _L1_ffn_ref(input_embeddings, router_w, w1, b1, w2, b2):
        import jax, jax.numpy as jnp
        import numpy as np
        NUM_EXPERTS = 8
        TOP_K = 2
        B, S, D = (8, 1024, 256)

        def _moe(tokens, router_w, w1, b1, w2, b2):
            N = tokens.shape[0]
            E = router_w.shape[0]
            logits = tokens.astype(jnp.float32) @ router_w.astype(jnp.float32).T
            probs = jax.nn.softmax(logits, axis=-1)
            rw, re = jax.lax.top_k(probs, TOP_K)
            if TOP_K > 1:
                rw = rw / jnp.maximum(rw.sum(-1, keepdims=True), 1e-12)
            rw = rw.astype(tokens.dtype)
            combine = jnp.zeros((N, E), tokens.dtype).at[jnp.arange(N)[:, None], re].set(rw)
            out = tokens
            for e in range(E):
                h = jax.nn.gelu(tokens @ w1[e] + b1[e], approximate=False)
                y = h @ w2[e] + b2[e]
                out = out + combine[:, e:e + 1] * y
            return out
        b, s, d = input_embeddings.shape
        tokens = input_embeddings.reshape(b * s, d)
        return _moe(tokens, router_w, w1, b1, w2, b2).reshape(b, s, d)
    edge_index = jnp.stack([src, dst])
    x = x + _L0_gnn_ref(_layernorm(x, axis=-1), src, dst, edge_type_8, L0_gnn_basis, L0_gnn_comp, L0_gnn_loop_weight, L0_gnn_bias_param)
    x = x + _L0_ffn_ref(_layernorm(x, axis=-1)[None], L0_ffn_router_w1, L0_ffn_router_b1, L0_ffn_router_w2, L0_ffn_router_b2, L0_ffn_expert_w1, L0_ffn_expert_b1, L0_ffn_expert_w2, L0_ffn_expert_b2, L0_ffn_expert_w3, L0_ffn_expert_b3)[0]
    x = x + _L1_gnn_ref(_layernorm(x, axis=-1), edge_attr_64, edge_weight, edge_index, L1_gnn_Wq, L1_gnn_bq, L1_gnn_Wk, L1_gnn_bk, L1_gnn_Wv, L1_gnn_bv, L1_gnn_We, L1_gnn_be, L1_gnn_Wo, L1_gnn_bo, L1_gnn_ln1_g, L1_gnn_ln1_b, L1_gnn_ln2_g, L1_gnn_ln2_b, L1_gnn_W1, L1_gnn_b1, L1_gnn_W2, L1_gnn_b2, L1_gnn_alpha, L1_gnn_beta)
    x = x + _L1_ffn_ref(_layernorm(x, axis=-1)[None], L1_ffn_router_w, L1_ffn_w1, L1_ffn_b1, L1_ffn_w2, L1_ffn_b2)[0]
    return x

_drawn_inputs = setup_inputs


def setup_inputs(seed=0):
    import zlib

    import numpy as np

    out = dict(_drawn_inputs(seed))
    spreads = {'L0_gnn_bias_param': (0.0, 0.648),
     'L0_ffn_router_b1': (0.0, 0.8),
     'L0_ffn_router_b2': (0.0, 0.8),
     'L0_ffn_expert_b1': (0.0, 0.8),
     'L0_ffn_expert_b2': (0.0, 0.8),
     'L0_ffn_expert_b3': (0.0, 2.0),
     'L1_gnn_bq': (0.0, 2.0),
     'L1_gnn_bk': (0.0, 2.0),
     'L1_gnn_bv': (0.0, 1.91),
     'L1_gnn_be': (0.0, 2.0),
     'L1_gnn_bo': (0.0, 2.0),
     'L1_gnn_ln1_g': (1.0, 0.6),
     'L1_gnn_ln1_b': (0.0, 1.82),
     'L1_gnn_ln2_g': (1.0, 0.6),
     'L1_gnn_ln2_b': (0.0, 2.0),
     'L1_gnn_b1': (0.0, 2.0),
     'L1_gnn_b2': (0.0, 2.0),
     'L1_ffn_b1': (0.0, 2.0),
     'L1_ffn_b2': (0.0, 2.0)}
    factors = {'L0_ffn_router_w1': 5.668,
     'L0_ffn_router_w2': 5.637,
     'L0_ffn_expert_w1': 8.0,
     'L0_ffn_expert_w2': 7.512,
     'L0_ffn_expert_w3': 5.934,
     'edge_attr_64': 3.419,
     'edge_weight': 3.402,
     'L1_gnn_We': 3.353,
     'L1_ffn_w1': 3.648,
     'L1_gnn_Wk': 3.146}
    for name, (base, spread) in spreads.items():
        noise = np.random.default_rng([zlib.crc32(name.encode()), seed]).standard_normal(out[name].shape)
        drawn = base * np.exp(spread * noise) if base else spread * noise
        out[name] = jnp.asarray(drawn.astype(out[name].dtype))
    for name, factor in factors.items():
        out[name] = (out[name] * factor).astype(out[name].dtype)
    return out
```

```python
from contextlib import ExitStack

import concourse.bass as bass
from concourse import mybir

P = 128
N = 2500
NT = -(-N // P)
NP = NT * P
BT = 4
BLK = BT * P
NB = NP // BLK
D = 256
DK = D // P
E = 40000
G = 8
ET = -(-E // (P * G)) * G
EP = ET * P
W = 32
XS = NP // W
KS = ET + XS
ACCW = NP + W
NBASE = 4
NREL = 8
RH = 128
E0 = 6
E1 = 8
H = 8
DH = D // H
ED = 64
FF = 4 * D
FK = FF // P
EPS = 1e-5
VG = 88
BIG = 3.0e38
LINE = EP // P

F32 = mybir.dt.float32
BF16 = mybir.dt.bfloat16
I32 = mybir.dt.int32
ALU = mybir.AluOpType
ACT = mybir.ActivationFunctionType
AX = mybir.AxisListType

COLS = {"rb1": 1, "eb1": 2 * E0, "eb2": 2 * E0, "ln1_g": 2, "ln1_b": 2, "ln2_g": 2, "ln2_b": 2,
        "bo": 2, "gb1": FK, "mb1": 2 * E1}
ROWS = {"bias0": D, "rb2": E0, "qkvb": 3 * D, "b2": D, "alpha": 1, "beta": 1, "comp": NREL * NBASE}


def places(widths):
    at, out = 0, {}
    for name, w in widths.items():
        out[name] = (at, at + w)
        at += w
    return out, at


COL, NCOL = places(COLS)
ROW, NROW = places(ROWS)


class Tally:

    def __init__(self, sem, i=0, per=0, base=0):
        self.sem, self.i, self.per, self.n, self.base = sem, i, per, 0, base

    def at(self, n):
        return self.i * self.per + (self.base + n)

    def mark(self, ins):
        ins.then_inc(self.sem, 1)
        self.n += 1

    def wait(self, eng):
        eng.wait_ge(self.sem, self.at(self.n))

    def close(self):
        assert self.n == self.per, (self.n, self.per)


def settle(eng):
    eng.nop(nofuse=True)


def windows(nc, engine, g, i, first=0):
    _, at = nc.values_load_multi_w_load_instructions(
        g.win[0:1, ds(i * G + first, G)], engines=[engine], min_val=0, max_val=NP,
        skip_runtime_bounds_check_because="a window starts at an edge's node, or at NP")
    return at


def ds(a, n):
    return bass.ds(a, n)


class Mem:

    def __init__(self, nc, ctx, prefix):
        self.nc, self.ctx, self.prefix, self.cleared = nc, ctx, prefix, []

    def sb(self, name, shape, dt=F32):
        return self.ctx.enter_context(self.nc.sbuf_tensor(f"{self.prefix}_{name}", list(shape), dt))

    def ps(self, name, shape, dt=F32):
        return self.ctx.enter_context(self.nc.psum_tensor(f"{self.prefix}_{name}", list(shape), dt))

    def cleared_sem(self, name):
        self.cleared.append(self.nc.alloc_semaphore(name=f"{self.prefix}_{name}"))
        return self.cleared[-1]

    def clear(self):
        self.nc.clear_and_free_semaphores(self.cleared)

    def sem(self, name):
        return self.ctx.enter_context(self.nc.semaphore(f"{self.prefix}_{name}"))



def stage_load(nc, d, g):
    with ExitStack() as ctx:
        m = Mem(nc, ctx, "load")
        ahead = m.sb("ahead", [P, LINE + 1], I32)
        down = m.sb("down", [P, LINE])
        downs = m.sb("downs", [P, 1])
        ones = m.sb("ones", [P, 1])
        count = m.sb("count", [1, 1])
        diag = m.sb("diag", [P, P])
        psC = m.ps("psC", [P, 512])
        loaded, line_loaded, chain = m.cleared_sem("loaded"), m.cleared_sem("line_loaded"), m.cleared_sem("chain")
        diag_ready, downs_ready, counted = m.cleared_sem("diag_ready"), m.cleared_sem("downs_ready"), m.cleared_sem("counted")
        with nc.Block() as block:
            @block.sync
            def _(sp):
                sp.dma_start(ahead[:, :], d.line).then_inc(line_loaded, 16)
                for dst, src in ((g.dstI[:, :], d.dst), (g.typI[:, :], d.typ), (g.srcI[:, 0:ET], d.src),
                                 (g.ew[:, :], d.ew), (g.cols[:, :], d.cols),
                                 (g.rows[:, :], d.rows.to_broadcast([P, NROW]))):
                    sp.dma_start(dst, src).then_inc(loaded, 16)
                for b in range(NB):
                    sp.dma_start(g.x[:, b * BT:(b + 1) * BT, :],
                                 d.x[b * BLK:(b + 1) * BLK, :].rearrange("(t p) c -> p t c", p=P)).then_inc(loaded, 16)
                sp.dma_start(g.basis[:, :, :, :], d.basis.rearrange("b (k p) o -> p b k o", p=P)).then_inc(loaded, 16)
                sp.dma_start(g.loopw[:, :, :], d.loopw.rearrange("(k p) o -> p k o", p=P)).then_inc(loaded, 16)
                sp.dma_start(g.rw1[:, :, :], d.rw1.rearrange("(k p) o -> p k o", p=P)).then_inc(loaded, 16)
                sp.dma_start(g.rw2[:, :], d.rw2).then_inc(loaded, 16)
                sp.dma_start(g.b3[:, :], d.b3).then_inc(loaded, 16)
                for w_sb, w in ((g.w1, d.w1), (g.w2, d.w2), (g.w3, d.w3)):
                    for e in range(E0):
                        sp.dma_start(w_sb[:, e, :, :], w[e].rearrange("(k p) o -> p k o", p=P)).then_inc(g.weights0, 16)
                sp.wait_ge(line_loaded, 16)
                sp.wait_ge(loaded, 16 * (6 + NB + 5))

            @block.gpsimd
            def _(pool):
                nc.gpsimd.iota(diag[:, :], [[-1, P]], base=0, channel_multiplier=1,
                               allow_small_or_imprecise_dtypes=True).then_inc(diag_ready, 1)

            @block.vector
            def _(dve):
                t = Tally(chain)
                nc.vector.memset(ones[:, :], 1.0)
                nc.vector.memset(g.eps[:, :], EPS)
                dve.wait_ge(diag_ready, 1)
                nc.vector.tensor_scalar(g.ident[:, :], diag[:, :], 0.0, None, ALU.is_equal)
                nc.vector.tensor_scalar(g.identb[:, :], diag[:, :], 0.0, None, ALU.is_equal)
                dve.wait_ge(line_loaded, 16)
                t.mark(nc.vector.tensor_tensor(down[:, :], ahead[:, 0:LINE], ahead[:, 1:LINE + 1], ALU.is_gt))
                t.wait(dve)
                nc.vector.tensor_reduce(downs[:, :], down[:, :], AX.X, ALU.add).then_inc(downs_ready, 1)
                dve.wait_ge(counted, 1)
                t.mark(nc.vector.tensor_copy(count[:, :], psC[0:1, 0:1]))
                t.wait(dve)
                nc.vector.tensor_scalar(g.flags[:, 0:1], count[:, :], 0.0, None, ALU.is_gt)
                nc.vector.tensor_scalar(g.flags[:, 1:2], count[:, :], 0.0, None, ALU.is_equal)

            @block.tensor
            def _(pe):
                pe.wait_ge(downs_ready, 1)
                nc.tensor.matmul(psC[0:1, 0:1], downs[:, :], ones[:, :], start=True, stop=True).then_inc(counted, 1)
        m.clear()
        nc.all_engine_barrier()



def stage_sort(nc, d, g):
    RN = 512
    with ExitStack() as ctx:
        m = Mem(nc, ctx, "sort")
        nodes = m.sb("nodes", [P, NP])
        oh = m.sb("oh", [P, NP], BF16)
        junk = m.sb("junk", [P, NP])
        base = m.sb("base", [P, NP])
        hist = m.sb("hist", [P, NP])
        onesb = m.sb("onesb", [P, P], BF16)
        below = m.sb("below", [P, P])
        same = m.sb("same", [P, P])
        wide = m.sb("wide", [P, P])
        dstF = m.sb("dstF", [P, ET])
        col = m.sb("col", [P, 1])
        part = m.sb("part", [P, 3])
        rank = m.sb("rank", [P, ET])
        place = m.sb("place", [P, 1], I32)
        rec = m.sb("rec", [P, 4 + P])
        efT = m.sb("efT", [ED, P])
        psR = m.ps("psR", [P, NP])
        psD = m.ps("psD", [P, 512])
        shapes_ready, chain, zeroed = m.cleared_sem("shapes_ready"), m.cleared_sem("chain"), m.cleared_sem("zeroed")
        wide_ready, spread, seen, counted = m.cleared_sem("wide_ready"), m.cleared_sem("spread"), m.cleared_sem("seen"), m.cleared_sem("counted")
        ef_got, rec_ready, scattered = m.cleared_sem("ef_got"), m.cleared_sem("rec_ready"), m.cleared_sem("scattered")
        chain2, chain3, back, turned, efT_ready, stored = (m.cleared_sem(n) for n in
                                                           ("chain2", "chain3", "back", "turned", "efT_ready", "stored"))
        with nc.Block() as block:
            @block.gpsimd
            def _(pool):
                with pool.If(pool.value_load(g.flags[0:1, 0:1], min_val=0, max_val=1)):
                    kw = dict(allow_small_or_imprecise_dtypes=True)
                    nc.gpsimd.iota(nodes[:, :], [[1, NP]], base=0, channel_multiplier=0, **kw)
                    nc.gpsimd.iota(below[:, :], [[-1, P]], base=0, channel_multiplier=1, **kw).then_inc(shapes_ready, 1)
                    with pool.Fori(0, ET) as t:
                        pool.wait_ge(rec_ready, t + 1)
                        settle(pool)
                        nc.gpsimd.indirect_dma_start(d.sorted[:, :], bass.IndirectOffsetOnAxis(ap=place[:, 0:1], axis=0),
                                                     rec[:, 0:4 + ED], None).then_inc(scattered, 16)
                    pool.wait_ge(scattered, 16 * ET)

            @block.sync
            def _(sp):
                with sp.If(sp.value_load(g.flags[0:1, 0:1], min_val=0, max_val=1)):
                    sp.wait_ge(zeroed, 1)
                    sp.dma_start(rec[:, 4:4 + ED], d.ef[0:P, :]).then_inc(ef_got, 16)
                    with sp.Fori(1, ET) as t:
                        sp.wait_ge(scattered, t * 16)
                        settle(sp)
                        sp.dma_start(rec[:, 4:4 + ED], d.ef[ds(t * P, P), :]).then_inc(ef_got, 16)
                    sp.wait_ge(ef_got, 16 * ET)
                    sp.wait_ge(scattered, 16 * ET)
                    with sp.Fori(0, ET) as t:
                        sp.wait_ge(chain3, t + 1)
                        settle(sp)
                        sp.dma_start(rec[:, 0:4 + ED], d.sorted[ds(t * P, P), :]).then_inc(back, 16)
                        sp.wait_ge(efT_ready, t + 1)
                        settle(sp)
                        sp.dma_start(d.efs[:, ds(t * P, P)], efT[:, :]).then_inc(stored, 16)
                    sp.wait_ge(back, 16 * ET)
                    sp.wait_ge(stored, 16 * ET)

            @block.vector
            def _(dve):
                with dve.If(dve.value_load(g.flags[0:1, 0:1], min_val=0, max_val=1)):
                    nc.vector.memset(onesb[:, :], 1.0)
                    nc.vector.memset(rec[:, :], 0.0).then_inc(zeroed, 1)
                    nc.vector.memset(hist[:, :], 0.0)
                    nc.vector.memset(g.spare[0:1, 0:1], 0.0).then_inc(chain, 1)
                    dve.wait_ge(shapes_ready, 1)
                    nc.vector.tensor_scalar(junk[:, 0:P], below[:, :], 0.0, None, ALU.is_gt).then_inc(zeroed, 1)
                    dve.wait_ge(zeroed, 2)
                    nc.vector.tensor_copy(below[:, :], junk[:, 0:P])
                    nc.vector.tensor_copy(dstF[:, :], g.dstI[:, :]).then_inc(zeroed, 1)
                    dve.wait_ge(zeroed, 3)
                    with dve.Fori(0, ET) as i:
                        t = Tally(chain, i, 5, 1)
                        t.wait(dve)
                        t.mark(nc.vector.tensor_copy(col[:, :], dstF[:, ds(i, 1)]))
                        t.wait(dve)
                        nc.vector.tensor_copy(wide[:, :], col[:, :].to_broadcast([P, P])).then_inc(wide_ready, 1)
                        t.mark(nc.vector.tensor_scalar(oh[:, :], nodes[:, :], col[:, 0:1], None, ALU.is_equal))
                        t.wait(dve)
                        nc.vector.scalar_tensor_tensor(out=junk[:, :], in0=nodes[:, :], scalar=col[:, 0:1], in1=hist[:, :],
                                                       op0=ALU.is_equal, op1=ALU.mult, accum_out=part[:, 0:1]).then_inc(seen, 1)
                        dve.wait_ge(spread, i + 1)
                        t.mark(nc.vector.scalar_tensor_tensor(out=same[:, :], in0=psD[:, 0:P], scalar=col[:, 0:1], in1=below[:, :],
                                                              op0=ALU.is_equal, op1=ALU.mult, accum_out=part[:, 1:2]))
                        t.wait(dve)
                        dve.wait_ge(seen, i + 1)
                        t.mark(nc.vector.tensor_tensor(rank[:, ds(i, 1)], part[:, 0:1], part[:, 1:2], ALU.add))
                        dve.wait_ge(counted, i + 1)
                        t.mark(nc.vector.tensor_tensor(hist[:, :], hist[:, :], psR[:, :], ALU.add))
                        t.close()
                    dve.wait_ge(chain, 5 * ET + 1)
                    t = Tally(chain2)
                    t.mark(nc.vector.memset(base[:, :], 0.0))
                    t.wait(dve)
                    t.mark(nc.vector.tensor_tensor_scan(junk[:, :], hist[:, :], base[:, :], 0.0, ALU.add, ALU.add))
                    t.wait(dve)
                    t.mark(nc.vector.tensor_tensor(base[:, :], junk[:, :], hist[:, :], ALU.subtract))
                    with dve.Fori(0, ET) as i:
                        t = Tally(chain2, i, 3, 3)
                        t.wait(dve)
                        t.mark(nc.vector.tensor_copy(col[:, :], dstF[:, ds(i, 1)]))
                        t.wait(dve)
                        t.mark(nc.vector.scalar_tensor_tensor(out=junk[:, :], in0=nodes[:, :], scalar=col[:, 0:1], in1=base[:, :],
                                                              op0=ALU.is_equal, op1=ALU.mult, accum_out=part[:, 0:1]))
                        t.wait(dve)
                        dve.wait_ge(ef_got, i * 16 + 16)
                        nc.vector.tensor_tensor(place[:, :], part[:, 0:1], rank[:, ds(i, 1)], ALU.add)
                        for c, from_ in enumerate((g.srcI, g.dstI, g.typI, g.ew)):
                            ins = nc.vector.tensor_copy(rec[:, c:c + 1], from_[:, ds(i, 1)])
                        ins.then_inc(rec_ready, 1)
                        dve.wait_ge(rec_ready, i + 1)
                        t.mark(nc.vector.tensor_copy(g.spare[0:1, 5:6], g.eps[0:1, 0:1]))
                        t.close()
                    nc.vector.memset(g.spare[0:1, 1:2], 0.0).then_inc(chain3, 1)
                    with dve.Fori(0, ET) as i:
                        dve.wait_ge(back, i * 16 + 16)
                        for c, to in enumerate((g.srcI, g.dstI, g.typI, g.ew)):
                            nc.vector.tensor_copy(to[:, ds(i, 1)], rec[:, c:c + 1])
                        dve.wait_ge(turned, i + 1)
                        nc.vector.tensor_copy(efT[:, :], psD[0:ED, 0:P]).then_inc(efT_ready, 1)
                        dve.wait_ge(stored, i * 16 + 16)
                        nc.vector.memset(g.spare[0:1, 2:3], 0.0).then_inc(chain3, 1)

            @block.tensor
            def _(pe):
                with pe.If(pe.value_load(g.flags[0:1, 0:1], min_val=0, max_val=1)):
                    pe.wait_ge(zeroed, 1)
                    with pe.Fori(0, ET) as i:
                        pe.wait_ge(wide_ready, i + 1)
                        nc.tensor.matmul(psD[:, 0:P], wide[:, :], g.ident[:, :], start=True, stop=True).then_inc(spread, 1)
                        pe.wait_ge(seen, i + 1)
                        for j in range(NP // RN):
                            ins = nc.tensor.matmul(psR[:, j * RN:(j + 1) * RN], onesb[:, :], oh[:, j * RN:(j + 1) * RN],
                                                   start=True, stop=True)
                        ins.then_inc(counted, 1)
                    with pe.Fori(0, ET) as i:
                        pe.wait_ge(back, i * 16 + 16)
                        nc.tensor.transpose(psD[:, 0:P], rec[:, 4:4 + P], g.ident[:, :]).then_inc(turned, 1)
        m.clear()
        nc.all_engine_barrier()



def stage_tables(nc, d, g):
    with ExitStack() as ctx:
        m = Mem(nc, ctx, "tab")
        dstF = g.dstF
        typF = m.sb("typF", [P, ET])
        hit = m.sb("hit", [P, ET])
        pick0 = m.sb("pick0", [P, P])
        pickl = m.sb("pickl", [P, P])
        firstS = m.sb("firstS", [P, ET])
        lastS = m.sb("lastS", [P, ET])
        spanF = m.sb("spanF", [P, ET])
        spanI = m.sb("spanI", [P, ET], I32)
        moreI = m.sb("moreI", [P, ET], I32)
        more = m.sb("more", [P, ET])
        upto = m.sb("upto", [P, ET])
        past = m.sb("past", [P, ET])
        sel = m.sb("sel", [P, ET])
        pidx = m.sb("pidx", [P, 1])
        tidx = m.sb("tidx", [P, ET])
        xt = m.sb("xt", [P, 8])
        winx = m.sb("winx", [P, XS])
        psF = m.ps("psF", [P, 512])
        psL = m.ps("psL", [P, 512])
        psX = m.ps("psX", [P, 512])
        shapes_ready = m.sem("shapes_ready")
        ch = m.sem("chain")
        picks_ready = m.sem("picks_ready")
        ends_ready = m.sem("ends_ready")
        extra_ready = m.sem("extra_ready")
        extra_turned = m.sem("extra_turned")
        dst_ready = m.sem("dst_ready")
        moved = m.sem("moved")
        with nc.Block() as block:
            @block.gpsimd
            def _(pool):
                kw = dict(allow_small_or_imprecise_dtypes=True)
                nc.gpsimd.iota(g.iota[:, :], [[1, W]], base=0, channel_multiplier=0, **kw)
                nc.gpsimd.iota(g.iota3[:, :], [[1, W], [0, 3]], base=0, channel_multiplier=0, **kw)
                nc.gpsimd.iota(pidx[:, :], [[0, 1]], base=0, channel_multiplier=1, **kw)
                nc.gpsimd.iota(tidx[:, :], [[1, ET]], base=0, channel_multiplier=0, **kw)
                nc.gpsimd.iota(g.rev[:, :], [[-1, E1]], base=E1, channel_multiplier=0, **kw)
                nc.gpsimd.iota(g.tile[:, 0:ET], [[1, ET]], base=0, channel_multiplier=0)
                nc.gpsimd.memset(g.srcI[:, ET:KS + G], 0).then_inc(shapes_ready, 1)

            @block.vector
            def _(dve):
                t = Tally(ch)
                nc.vector.memset(g.none[:, :], 0.0)
                nc.vector.memset(g.coef[:, :, :], 0.0)
                t.mark(nc.vector.memset(g.dstrel[:, ET:KS + G], -1.0))
                dve.wait_ge(shapes_ready, 1)
                nc.vector.tensor_copy(pick0[:, :], g.ident[:, 0:1].to_broadcast([P, P]))
                nc.vector.tensor_copy(pickl[:, :], g.ident[:, P - 1:P].to_broadcast([P, P])).then_inc(picks_ready, 1)
                nc.vector.tensor_copy(dstF[:, :], g.dstI[:, :]).then_inc(dst_ready, 1)
                t.mark(nc.vector.tensor_copy(typF[:, :], g.typI[:, :]))
                t.wait(dve)
                for r in range(NREL):
                    t.mark(nc.vector.tensor_scalar(hit[:, :], typF[:, :], float(r), None, ALU.is_equal))
                    t.wait(dve)
                    for b in range(NBASE):
                        c = ROW["comp"][0] + r * NBASE + b
                        ins = nc.vector.scalar_tensor_tensor(out=g.coef[:, 0:ET, b], in0=hit[:, :], scalar=g.rows[:, c:c + 1],
                                                             in1=g.coef[:, 0:ET, b], op0=ALU.mult, op1=ALU.add)
                    t.mark(ins)
                    t.wait(dve)
                dve.wait_ge(ends_ready, 1)
                nc.vector.tensor_copy(firstS[:, :], psF[:, 0:ET])
                nc.vector.tensor_copy(g.win[:, 0:ET], psF[0:1, 0:ET])
                t.mark(nc.vector.tensor_copy(lastS[:, :], psL[:, 0:ET]))
                t.wait(dve)
                nc.vector.tensor_tensor(g.dstrel[:, 0:ET], dstF[:, :], firstS[:, :], ALU.subtract)
                t.mark(nc.vector.tensor_tensor(spanI[:, :], lastS[:, :], firstS[:, :], ALU.subtract))
                t.wait(dve)
                t.mark(nc.vector.tensor_scalar(moreI[:, :], spanI[:, :], 5, None, ALU.arith_shift_right))
                t.wait(dve)
                t.mark(nc.vector.tensor_scalar(more[:, :], moreI[:, :], 0.0, None, ALU.max))
                t.wait(dve)
                nc.vector.memset(past[:, :], 0.0)
                t.mark(nc.vector.memset(xt[:, :], 0.0))
                t.wait(dve)
                t.mark(nc.vector.tensor_tensor_scan(upto[:, :], more[:, :], past[:, :], 0.0, ALU.add, ALU.add))
                t.wait(dve)
                t.mark(nc.vector.tensor_scalar(past[:, :], upto[:, :], pidx[:, 0:1], None, ALU.is_le))
                t.wait(dve)
                nc.vector.tensor_reduce(xt[:, 0:1], past[:, :], AX.X, ALU.add)
                t.mark(nc.vector.tensor_tensor(sel[:, :], past[:, :], more[:, :], ALU.mult))
                t.wait(dve)
                nc.vector.tensor_reduce(xt[:, 1:2], sel[:, :], AX.X, ALU.add)
                t.mark(nc.vector.tensor_scalar(spanF[:, :], tidx[:, :], xt[:, 0:1], None, ALU.is_equal))
                t.wait(dve)
                t.mark(nc.vector.tensor_tensor(sel[:, :], spanF[:, :], firstS[:, :], ALU.mult))
                t.wait(dve)
                t.mark(nc.vector.tensor_reduce(xt[:, 2:3], sel[:, :], AX.X, ALU.add))
                t.wait(dve)
                t.mark(nc.vector.tensor_scalar(xt[:, 3:4], pidx[:, :], xt[:, 1:2], 1.0, ALU.subtract, ALU.add))
                t.wait(dve)
                t.mark(nc.vector.tensor_scalar(xt[:, 3:4], xt[:, 3:4], float(W), xt[:, 2:3], ALU.mult, ALU.add))
                t.wait(dve)
                t.mark(nc.vector.tensor_scalar(xt[:, 4:5], xt[:, 0:1], float(ET), None, ALU.is_ge))
                t.wait(dve)
                t.mark(nc.vector.tensor_scalar(xt[:, 5:6], xt[:, 4:5], float(2 * NP), xt[:, 3:4], ALU.mult, ALU.add))
                t.wait(dve)
                nc.vector.tensor_scalar(xt[:, 6:7], xt[:, 5:6], float(NP), None, ALU.min)
                t.mark(nc.vector.tensor_scalar(xt[:, 7:8], xt[:, 0:1], float(ET - 1), None, ALU.min))
                t.wait(dve)
                nc.vector.tensor_copy(pick0[:, :], xt[:, 6:7].to_broadcast([P, P]))
                nc.vector.tensor_copy(pickl[:, :], xt[:, 7:8].to_broadcast([P, P])).then_inc(extra_ready, 1)
                dve.wait_ge(extra_turned, 1)
                nc.vector.tensor_copy(winx[:, :], psX[:, 0:XS])
                nc.vector.tensor_copy(g.win[:, ET:KS], psX[0:1, 0:XS])
                nc.vector.tensor_copy(g.tile[:, ET:KS], psX[0:1, P:P + XS])
                t.mark(nc.vector.tensor_copy(g.over[:, :], upto[0:1, ET - 1:ET]))
                t.wait(dve)
                over = dve.value_load(g.over[0:1, 0:1], min_val=0, max_val=2 * NP)
                with dve.If(over):
                    with dve.Fori(0, XS) as k:
                        tl = dve.value_load(g.tile[0:1, ds(k + ET, 1)], min_val=0, max_val=ET - 1)
                        nc.vector.tensor_tensor(g.dstrel[:, ds(k + ET, 1)], dstF[:, ds(tl, 1)], winx[:, ds(k, 1)], ALU.subtract)
                        nc.vector.tensor_copy(g.coef[:, ds(k + ET, 1), :], g.coef[:, ds(tl, 1), :])
                        nc.vector.tensor_copy(g.srcI[:, ds(k + ET, 1)], g.srcI[:, ds(tl, 1)]).then_inc(moved, 1)
                    dve.wait_ge(moved, XS)

            @block.tensor
            def _(pe):
                pe.wait_ge(picks_ready, 1)
                pe.wait_ge(dst_ready, 1)
                nc.tensor.matmul(psF[:, 0:ET], pick0[:, :], dstF[:, :], start=True, stop=True)
                nc.tensor.matmul(psL[:, 0:ET], pickl[:, :], dstF[:, :], start=True, stop=True).then_inc(ends_ready, 1)
                pe.wait_ge(extra_ready, 1)
                nc.tensor.matmul(psX[:, 0:P], pick0[:, :], g.ident[:, :], start=True, stop=True)
                nc.tensor.matmul(psX[:, P:2 * P], pickl[:, :], g.ident[:, :], start=True, stop=True).then_inc(extra_turned, 1)



class Norm:

    def __init__(self, m, i, per):
        self.stat = m.sb("stat", [P, BT, 6])
        self.mv = m.sb("mv", [P, BT, 2])
        self.std = m.sb("std", [P, BT])
        self.rstd = m.sb("rstd", [P, BT])
        self.var_ready = m.sem("var_ready")
        self.std_ready = m.sem("std_ready")


def norm_dve(nc, dve, g, nm, t, i, per, k, src, dst, done=None):
    t.wait(dve)
    settle(dve)
    for q in range(BT):
        ins = nc.vector.bn_stats(nm.stat[:, q, :], src(q))
    t.mark(ins)
    t.wait(dve)
    settle(dve)
    for q in range(BT):
        ins = nc.vector.bn_aggr(nm.mv[:, q, :], nm.stat[:, q, :])
    ins.then_inc(nm.var_ready, 1)
    dve.wait_ge(nm.std_ready, i * per + k + 1)
    t.mark(nc.vector.reciprocal(nm.rstd[:, :], nm.std[:, :]))
    t.wait(dve)
    for q in range(BT):
        ins = nc.vector.tensor_scalar(dst(q), src(q), nm.mv[:, q, 0:1], nm.rstd[:, q:q + 1], ALU.subtract, ALU.mult)
    if done is None:
        t.mark(ins)
    else:
        ins.then_inc(done, 1)


def norm_act(nc, act, g, nm, i, per, k):
    act.wait_ge(nm.var_ready, i * per + k + 1)
    nc.scalar.activation(nm.std[:, :], nm.mv[:, :, 1], ACT.Sqrt, bias=g.eps[:, 0:1]).then_inc(nm.std_ready, 1)


def turn(nc, g, out, src):
    for q in range(BT):
        for k in range(DK):
            ins = nc.tensor.transpose(out[:, k, q * P:(q + 1) * P], src(q)[:, k * P:(k + 1) * P], g.ident[:, :])
    return ins



def stage_self_loop(nc, d, g):
    with ExitStack() as ctx:
        m = Mem(nc, ctx, "self")
        nm = Norm(m, 0, 1)
        xn = m.sb("xn", [P, BT, D])
        xnT = m.sb("xnT", [P, DK, BLK])
        psT = m.ps("psT", [P, DK, BLK])
        psY = m.ps("psY", [P, BT, D])
        ch = m.sem("chain")
        xn_ready = m.sem("xn_ready")
        turned = m.sem("turned")
        xnT_ready = m.sem("xnT_ready")
        y_ready = m.sem("y_ready")
        stored = m.sem("stored")
        with nc.Block() as block:
            @block.vector
            def _(dve):
                nc.vector.memset(g.spare[0:1, 1:2], 0.0).then_inc(ch, 1)
                with dve.Fori(0, NB) as i:
                    t = Tally(ch, i, 4, 1)
                    norm_dve(nc, dve, g, nm, t, i, 1, 0, lambda q: g.x[:, ds(i * BT + q, 1), :].rearrange("p a c -> p (a c)"),
                             lambda q: xn[:, q, :], xn_ready)
                    dve.wait_ge(y_ready, i + 1)
                    xb = g.x[:, ds(i * BT, BT), :]
                    r = g.rows[:, ROW["bias0"][0]:ROW["bias0"][1]].unsqueeze(1).to_broadcast([P, BT, D])
                    t.mark(nc.vector.tensor_tensor(xb, psY[:, :, :], xb, ALU.add))
                    t.wait(dve)
                    t.mark(nc.vector.tensor_tensor(xb, xb, r, ALU.add))
                    t.close()
                    dve.wait_ge(stored, i * 16 + 16)

            @block.scalar
            def _(act):
                with act.Fori(0, NB) as i:
                    norm_act(nc, act, g, nm, i, 1, 0)
                    act.wait_ge(turned, i + 1)
                    nc.scalar.copy(xnT[:, :, :], psT[:, :, :]).then_inc(xnT_ready, 1)

            @block.tensor
            def _(pe):
                with pe.Fori(0, NB) as i:
                    pe.wait_ge(xn_ready, i + 1)
                    turn(nc, g, psT, lambda q: xn[:, q, :]).then_inc(turned, 1)
                    pe.wait_ge(xnT_ready, i + 1)
                    for q in range(BT):
                        for k in range(DK):
                            ins = nc.tensor.matmul(psY[:, q, :], xnT[:, k, q * P:(q + 1) * P], g.loopw[:, k, :],
                                                   start=(k == 0), stop=(k == DK - 1))
                    ins.then_inc(y_ready, 1)

            @block.sync
            def _(sp):
                with sp.Fori(0, NB) as i:
                    sp.wait_ge(xn_ready, i + 1)
                    sp.dma_start(d.xn[ds(i * BLK, BLK), :].rearrange("(t p) c -> p t c", p=P), xn[:, :, :]).then_inc(stored, 16)
                sp.wait_ge(stored, 16 * NB)



def index_copies(nc, act, g, ixs, got, copied, i, slots=range(G)):
    for b in slots:
        act.wait_ge(got[b], i * 16 + 16)
        settle(act)
        nc.scalar.copy(ixs[:, b:b + 1], g.srcI[:, ds(i * G + (G + b), 1)]).then_inc(copied, 1)


def first_indices(nc, g, ixs, copied):
    for b in range(G):
        nc.scalar.copy(ixs[:, b:b + 1], g.srcI[:, b:b + 1]).then_inc(copied, 1)


def gathers(nc, pool, g, ring, ixs, table, got, copied, free, per, i):
    for b in range(G):
        pool.wait_ge(copied, i * G + (b + 1))
        pool.wait_ge(free, i * (G // per) + (b // per + 1))
        settle(pool)
        nc.gpsimd.indirect_dma_start(ring[:, b, :], None, table[:, :],
                                     bass.IndirectOffsetOnAxis(ap=ixs[:, b:b + 1], axis=0)).then_inc(got[b], 16)


def free_at_first(nc, g, out, sem, n):
    nc.tensor.transpose(out, g.ident[0:32, 0:32], g.ident[0:32, 0:32]).then_inc(sem, n)


def edge_loops(nc, eng, g, body):
    with eng.Fori(0, ET // G) as i:
        body(i)
    over = eng.value_load(g.over[0:1, 0:1], min_val=0, max_val=2 * NP)
    with eng.If(over):
        with eng.Fori(ET // G, KS // G) as i:
            body(i)


def stage_gather0(nc, d, g):
    with ExitStack() as ctx:
        m = Mem(nc, ctx, "ga0")
        ixs = m.sb("ixs", [P, G], I32)
        xg = m.sb("xg", [P, G, D])
        oh = m.sb("oh", [P, 2, 4, W])
        M = m.sb("M", [P, 2, 4, NBASE, W])
        psZ = m.ps("psZ", [P, 4, 512])
        got = [m.sem(f"got{b}") for b in range(G)]
        copied = m.sem("copied")
        oh_ready = m.sem("oh_ready")
        M_ready = m.sem("M_ready")
        z_ready = m.sem("z_ready")
        z_added = m.sem("z_added")
        cleared = m.sem("cleared")
        with nc.Block() as block:
            @block.scalar
            def _(act):
                first_indices(nc, g, ixs, copied)
                edge_loops(nc, act, g, lambda i: index_copies(nc, act, g, ixs, got, copied, i))

            @block.gpsimd
            def _(pool):
                edge_loops(nc, pool, g, lambda i: gathers(nc, pool, g, xg, ixs, d.xn, got, copied, z_ready, 1, i))

            @block.vector
            def _(dve):
                nc.vector.memset(g.spare[0:1, 0:1], 0.0).then_inc(z_added, 4)
                nc.vector.memset(g.ZT[:, :, :, :], 0.0).then_inc(cleared, 1)
                dve.wait_ge(cleared, 1)

                def build(i, h):
                    dve.wait_ge(z_ready, i * G + 4 * (h + 1))
                    at = ds(i * G + 4 * h, 4)
                    nc.vector.tensor_tensor(oh[:, h, :, :], g.iota[:, :].unsqueeze(1).to_broadcast([P, 4, W]),
                                            g.dstrel[:, at].unsqueeze(2).to_broadcast([P, 4, W]),
                                            ALU.is_equal).then_inc(oh_ready, 1)
                    dve.wait_ge(oh_ready, i * 2 + (h + 1))
                    nc.vector.tensor_tensor(M[:, h, :, :, :],
                                            oh[:, h, :, :].unsqueeze(2).to_broadcast([P, 4, NBASE, W]),
                                            g.coef[:, at, :].unsqueeze(3).to_broadcast([P, 4, NBASE, W]),
                                            ALU.mult).then_inc(M_ready, 1)

                def body(i):
                    at = windows(nc, mybir.EngineType.DVE, g, i)
                    for b in range(G):
                        dve.wait_ge(z_ready, i * G + (G + b + 1))
                        dve.wait_ge(z_added, i * G + (b + 4))
                        z = g.ZT[:, :, :, ds(at[b], W)]
                        nc.vector.tensor_tensor(z, psZ[:, b % 4, 0:DK * NBASE * W].rearrange("p (k b w) -> p k b w", k=DK, b=NBASE),
                                                z, ALU.add).then_inc(z_added, 1)
                        if b % 4 == 3:
                            build(i + 1, b // 4)

                for h in range(2):
                    build(0, h)
                edge_loops(nc, dve, g, body)

            @block.tensor
            def _(pe):
                free_at_first(nc, g, psZ[0:32, 0, 0:32], z_ready, G)

                def body(i):
                    for h in range(2):
                        pe.wait_ge(M_ready, i * 2 + (h + 1))
                        for j in range(4):
                            b = 4 * h + j
                            pe.wait_ge(got[b], i * 16 + 16)
                            pe.wait_ge(z_added, i * G + (b + 1))
                            for k in range(DK):
                                ins = nc.tensor.matmul(psZ[:, j, k * NBASE * W:(k + 1) * NBASE * W],
                                                       xg[:, b, k * P:(k + 1) * P],
                                                       M[:, h, j, :, :].rearrange("p b w -> p (b w)"), start=True, stop=True)
                            ins.then_inc(z_ready, 1)

                edge_loops(nc, pe, g, body)




def stage_bases(nc, d, g):
    with ExitStack() as ctx:
        m = Mem(nc, ctx, "bas")
        aT = m.sb("aT", [P, DK, BLK])
        psA = m.ps("psA", [P, DK, BLK])
        psB = m.ps("psB", [P, BT, D])
        sums_ready = m.sem("sums_ready")
        aT_ready = m.sem("aT_ready")
        turned = m.sem("turned")
        added = m.sem("added")
        with nc.Block() as block:
            @block.tensor
            def _(pe):
                free_at_first(nc, g, psA[0:32, 0, 0:32], turned, 1)
                with pe.Fori(0, NB) as i:
                    pe.wait_ge(turned, i + 1)
                    for o in range(DK):
                        for b in range(NBASE):
                            for k in range(DK):
                                ins = nc.tensor.matmul(psA[:, o, :], g.basis[:, b, k, o * P:(o + 1) * P],
                                                       g.ZT[:, k, b, ds(i * BLK, BLK)],
                                                       start=(b == 0 and k == 0), stop=(b == NBASE - 1 and k == DK - 1))
                        ins.then_inc(sums_ready, 1)
                    pe.wait_ge(aT_ready, i * 2 + 2)
                    pe.wait_ge(added, i + 1)
                    for q in range(BT):
                        for k in range(DK):
                            ins = nc.tensor.transpose(psB[:, q, k * P:(k + 1) * P], aT[:, k, q * P:(q + 1) * P], g.ident[:, :])
                    ins.then_inc(turned, 1)

            @block.scalar
            def _(act):
                with act.Fori(0, NB) as i:
                    for o in range(DK):
                        act.wait_ge(sums_ready, i * 2 + (o + 1))
                        act.wait_ge(turned, i + 1)
                        nc.scalar.copy(aT[:, o, :], psA[:, o, :]).then_inc(aT_ready, 1)

            @block.vector
            def _(dve):
                nc.vector.memset(g.spare[0:1, 2:3], 0.0).then_inc(added, 1)
                with dve.Fori(0, NB) as i:
                    dve.wait_ge(turned, i + 2)
                    xb = g.x[:, ds(i * BT, BT), :]
                    nc.vector.tensor_tensor(xb, psB[:, :, :], xb, ALU.add).then_inc(added, 1)



def gates_dve(nc, dve, g, r, t, i, n, psL, bias, last):
    def red(out, op):
        t.mark(nc.vector.tensor_reduce(out, r.p[:, :, 0:n], AX.X, op))
        t.wait(dve)

    def spread(v):
        return v.unsqueeze(2).to_broadcast([P, BT, n])

    if bias is None:
        t.mark(nc.vector.tensor_copy(r.p[:, :, :], psL))
    else:
        t.mark(nc.vector.tensor_tensor(r.p[:, :, :], psL, bias.unsqueeze(1).to_broadcast([P, BT, n]), ALU.add))
    t.wait(dve)
    red(r.m[:, :, 0], ALU.max)
    nc.vector.tensor_tensor(r.p[:, :, :], r.p[:, :, :], spread(r.m[:, :, 0]), ALU.subtract).then_inc(r.shifted, 1)
    dve.wait_ge(r.p_ready, last * i + 1)
    red(r.m[:, :, 0], ALU.add)
    t.mark(nc.vector.reciprocal(r.m[:, :, 1], r.m[:, :, 0]))
    t.wait(dve)
    t.mark(nc.vector.tensor_tensor(r.p[:, :, :], r.p[:, :, :], spread(r.m[:, :, 1]), ALU.mult))
    t.wait(dve)
    for j in range(2):
        red(r.m[:, :, j], ALU.max)
        t.mark(nc.vector.tensor_tensor(r.k[:, j, :, :], r.p[:, :, :], spread(r.m[:, :, j]), ALU.is_equal))
        t.wait(dve)
        t.mark(nc.vector.tensor_tensor(r.k[:, j, :, :], r.k[:, j, :, :], g.rev[:, 0:n].unsqueeze(1).to_broadcast([P, BT, n]), ALU.mult))
        t.wait(dve)
        t.mark(nc.vector.tensor_reduce(r.m[:, :, 2], r.k[:, j, :, :], AX.X, ALU.max))
        t.wait(dve)
        t.mark(nc.vector.tensor_tensor(r.k[:, j, :, :], r.k[:, j, :, :], spread(r.m[:, :, 2]), ALU.is_equal))
        t.wait(dve)
        if j == 0:
            t.mark(nc.vector.scalar_tensor_tensor(out=r.p[:, :, :], in0=r.k[:, 0, :, :], scalar=-2.0, in1=r.p[:, :, :],
                                                  op0=ALU.mult, op1=ALU.add))
            t.wait(dve)


def mix_dve(nc, dve, r, t, n, g1, g2, done):
    def spread(v):
        return v.unsqueeze(2).to_broadcast([P, BT, n])
    nc.vector.tensor_tensor(r.k[:, 0, :, :], r.k[:, 0, :, :], spread(g1), ALU.mult)
    t.mark(nc.vector.tensor_tensor(r.k[:, 1, :, :], r.k[:, 1, :, :], spread(g2), ALU.mult))
    t.wait(dve)
    nc.vector.tensor_tensor(r.gate[:, :, :], r.k[:, 0, :, :], r.k[:, 1, :, :], ALU.add).then_inc(done, 1)


class Router:
    def __init__(self, m, n):
        self.p = m.sb("r_p", [P, BT, n])
        self.m = m.sb("r_m", [P, BT, 4])
        self.k = m.sb("r_k", [P, 2, BT, n])
        self.gate = m.sb("gate", [P, BT, n])
        self.gateT = m.sb("gateT", [n, BLK])
        self.shifted = m.sem("shifted")
        self.p_ready = m.sem("p_ready")


def vec(g, name, k=0):
    c = COL[name][0] + k
    return g.cols[:, c:c + 1]


def row(g, name):
    return g.rows[:, ROW[name][0]:ROW[name][1]]


def stage_experts0(nc, d, g):
    order = []
    for e in range(-1, E0 + 1):
        order += [(s, x) for s, x in (("A", e + 1), ("B", e), ("C", e - 1)) if 0 <= x < E0]
    with ExitStack() as ctx:
        m = Mem(nc, ctx, "ex0")
        nm = Norm(m, 0, 3)
        r = Router(m, E0)
        xn = m.sb("xn", [P, BT, D])
        xT = m.sb("xT", [P, DK, BLK])
        rhT = m.sb("rhT", [P, BLK])
        h1 = m.sb("h1", [P, 2, DK, BLK])
        h2 = m.sb("h2", [P, 2, DK, BLK])
        acc = m.sb("acc", [P, BT, D])
        qkv = m.sb("qkv", [P, BT, 3 * D])
        q3 = m.sb("q3", [P, BT, 3, D], BF16)
        rest = m.sb("rest", [P, BT, D])
        psW = m.ps("psW", [P, 2, 512])
        psA = m.ps("psA", [P, 2, 512])
        psB = m.ps("psB", [P, 2, 512])
        psC = m.ps("psC", [P, BT, D])
        names = ("chain", "xn_ready", "turned", "xT_ready", "hidden", "rhT_ready", "logits", "gate_ready", "gate_turned",
                 "gateT_ready", "bias_mixed", "acc_ready", "a_ready", "h1_ready", "b_ready", "h2_ready", "c_ready", "c_used",
                 "qkv_made", "qkv_ready", "part_made", "rest_made", "q3_ready", "stored")
        s = Names()
        (s.chain, s.xn_ready, s.turned, s.xT_ready, s.hidden, s.rhT_ready, s.logits, s.gate_ready, s.gate_turned,
         s.gateT_ready, s.bias_mixed, s.acc_ready, s.a_ready, s.h1_ready, s.b_ready, s.h2_ready, s.c_ready, s.c_used,
         s.qkv_made, s.qkv_ready, s.part_made, s.rest_made, s.q3_ready, s.stored) = (m.sem(n) for n in names)
        with nc.Block() as block:
            @block.vector
            def _(dve):
                nc.vector.memset(g.spare[0:1, 1:2], 0.0).then_inc(s.c_used, BT)
                nc.vector.memset(g.spare[0:1, 2:3], 0.0).then_inc(s.qkv_ready, BT)
                nc.vector.memset(g.spare[0:1, 3:4], 0.0).then_inc(s.chain, 1)
                dve.wait_ge(g.weights0, 16 * 3 * E0)
                with dve.Fori(0, NB) as i:
                    t = Tally(s.chain, i, 28, 1)
                    norm_dve(nc, dve, g, nm, t, i, 3, 0, lambda q: g.x[:, ds(i * BT + q, 1), :].rearrange("p a c -> p (a c)"),
                             lambda q: xn[:, q, :], s.xn_ready)
                    dve.wait_ge(s.logits, i + 1)
                    gates_dve(nc, dve, g, r, t, i, E0, psW[:, 1, 0:BT * E0].rearrange("p (t e) -> p t e", t=BT), row(g, "rb2"), 2)
                    nc.vector.tensor_tensor(r.m[:, :, 2], r.m[:, :, 1], r.m[:, :, 0], ALU.subtract).then_inc(r.shifted, 1)
                    dve.wait_ge(r.p_ready, i * 2 + 2)
                    t.mark(nc.vector.tensor_scalar(r.m[:, :, 2], r.m[:, :, 3], 1.0, None, ALU.add))
                    t.wait(dve)
                    t.mark(nc.vector.reciprocal(r.m[:, :, 0], r.m[:, :, 2]))
                    t.wait(dve)
                    t.mark(nc.vector.tensor_tensor(r.m[:, :, 1], r.m[:, :, 3], r.m[:, :, 0], ALU.mult))
                    t.wait(dve)
                    mix_dve(nc, dve, r, t, E0, r.m[:, :, 0], r.m[:, :, 1], s.gate_ready)
                    dve.wait_ge(s.gate_ready, i + 1)
                    dve.wait_ge(s.acc_ready, i + 1)
                    for e in range(E0):
                        for q in range(BT):
                            if q % 2 == 0:
                                dve.wait_ge(s.c_ready, i * (E0 * BT) + (e * BT + q + 2))
                            dve.wait_ge(s.c_used, i * (E0 * BT) + (e * BT + q + 1))
                            nc.vector.scalar_tensor_tensor(out=acc[:, q, :], in0=psC[:, q, :], scalar=r.gate[:, q, e:e + 1],
                                                           in1=acc[:, q, :], op0=ALU.mult, op1=ALU.add).then_inc(s.c_used, 1)
                    dve.wait_ge(s.c_used, i * (E0 * BT) + (E0 * BT + BT))
                    xb = g.x[:, ds(i * BT, BT), :]
                    t.mark(nc.vector.tensor_tensor(xb, xb, acc[:, :, :], ALU.add))
                    ub = lambda q: g.u[:, ds(i * BT + q, 1), :].rearrange("p a c -> p (a c)")
                    norm_dve(nc, dve, g, nm, t, i, 3, 1, lambda q: g.x[:, ds(i * BT + q, 1), :].rearrange("p a c -> p (a c)"), ub)
                    norm_dve(nc, dve, g, nm, t, i, 3, 2, ub, lambda q: xn[:, q, :], s.xn_ready)
                    dve.wait_ge(s.stored, i * 48 + 16)
                    for q in range(BT):
                        dve.wait_ge(s.qkv_made, i * BT + (q + 1))
                        R = (psA if q % 2 == 0 else psB)[:, :, :].rearrange("p a c -> p (a c)")
                        nc.vector.tensor_tensor(qkv[:, q, :], R[:, 0:3 * D], row(g, "qkvb"), ALU.add).then_inc(s.qkv_ready, 1)
                    dve.wait_ge(s.part_made, i * 2 + 1)
                    nc.vector.tensor_tensor(rest[:, :, :], qkv[:, :, 0:D], q3[:, :, 0, :], ALU.subtract).then_inc(s.rest_made, 1)
                    dve.wait_ge(s.part_made, i * 2 + 2)
                    nc.vector.tensor_tensor(q3[:, :, 2, :], rest[:, :, :], q3[:, :, 1, :], ALU.subtract).then_inc(s.q3_ready, 1)
                    t.close()

            @block.scalar
            def _(act):
                with act.Fori(0, NB) as i:
                    norm_act(nc, act, g, nm, i, 3, 0)
                    act.wait_ge(s.turned, i * 2 + 1)
                    nc.scalar.copy(xT[:, :, :], psW[:, :, :]).then_inc(s.xT_ready, 1)
                    act.wait_ge(s.hidden, i + 1)
                    nc.scalar.activation(rhT[:, :], psW[:, 0, :], ACT.Relu, bias=vec(g, "rb1")).then_inc(s.rhT_ready, 1)
                    for n, (what, e) in enumerate(order):
                        if what == "C":
                            continue
                        for o in range(DK):
                            src, ready, h, done, b = (psA, s.a_ready, h1, s.h1_ready, "eb1") if what == "A" else \
                                                     (psB, s.b_ready, h2, s.h2_ready, "eb2")
                            act.wait_ge(ready, i * (2 * E0) + (2 * e + o + 1))
                            nc.scalar.activation(h[:, e % 2, o, :], src[:, o, :], ACT.Relu, bias=vec(g, b, 2 * e + o)).then_inc(done, 1)
                        if (what, e) == ("A", 1):
                            act.wait_ge(r.shifted, i * 2 + 1)
                            nc.scalar.activation(r.p[:, :, :], r.p[:, :, :], ACT.Exp).then_inc(r.p_ready, 1)
                            act.wait_ge(r.shifted, i * 2 + 2)
                            nc.scalar.activation(r.m[:, :, 3], r.m[:, :, 2], ACT.Exp).then_inc(r.p_ready, 1)
                        if (what, e) == ("B", 1):
                            act.wait_ge(s.gate_turned, i + 1)
                            nc.scalar.copy(r.gateT[:, :], psC[0:E0, 0:2, :].rearrange("p a c -> p (a c)")).then_inc(s.gateT_ready, 1)
                            act.wait_ge(s.bias_mixed, i + 1)
                            nc.scalar.copy(acc[:, :, :], psW[:, :, :].rearrange("p a c -> p (a c)").rearrange("p (t c) -> p t c", t=BT)).then_inc(s.acc_ready, 1)
                    norm_act(nc, act, g, nm, i, 3, 1)
                    norm_act(nc, act, g, nm, i, 3, 2)
                    act.wait_ge(s.turned, i * 2 + 2)
                    for k in range(DK):
                        ins = nc.scalar.activation(xT[:, k, :], psW[:, k, :], ACT.Identity, bias=vec(g, "ln1_b", k),
                                                   scale=vec(g, "ln1_g", k))
                    ins.then_inc(s.xT_ready, 1)
                    act.wait_ge(s.qkv_ready, i * BT + 2 * BT)
                    nc.scalar.copy(q3[:, :, 0, :], qkv[:, :, 0:D]).then_inc(s.part_made, 1)
                    act.wait_ge(s.rest_made, i + 1)
                    nc.scalar.copy(q3[:, :, 1, :], rest[:, :, :]).then_inc(s.part_made, 1)

            @block.tensor
            def _(pe):
                pe.wait_ge(g.weights0, 16 * 3 * E0)
                pe.wait_ge(g.qkv_loaded, 48)
                with pe.Fori(0, NB) as i:
                    pe.wait_ge(s.xn_ready, i * 2 + 1)
                    turn(nc, g, psW, lambda q: xn[:, q, :]).then_inc(s.turned, 1)
                    pe.wait_ge(s.xT_ready, i * 2 + 1)
                    for k in range(DK):
                        ins = nc.tensor.matmul(psW[:, 0, :], g.rw1[:, k, :], xT[:, k, :], start=(k == 0), stop=(k == DK - 1))
                    ins.then_inc(s.hidden, 1)
                    pe.wait_ge(s.qkv_ready, i * BT + BT)
                    for what, e in order:
                        if what == "A":
                            if e >= 1:
                                pe.wait_ge(s.h1_ready, i * (2 * E0) + 2 * e)
                            for o in range(DK):
                                for k in range(DK):
                                    ins = nc.tensor.matmul(psA[:, o, :], g.w1[:, e, k, o * P:(o + 1) * P], xT[:, k, :],
                                                           start=(k == 0), stop=(k == DK - 1))
                                ins.then_inc(s.a_ready, 1)
                        if what == "B":
                            pe.wait_ge(s.h1_ready, i * (2 * E0) + (2 * e + 2))
                            if e >= 1:
                                pe.wait_ge(s.h2_ready, i * (2 * E0) + 2 * e)
                            for o in range(DK):
                                for k in range(DK):
                                    ins = nc.tensor.matmul(psB[:, o, :], g.w2[:, e, k, o * P:(o + 1) * P], h1[:, e % 2, k, :],
                                                           start=(k == 0), stop=(k == DK - 1))
                                ins.then_inc(s.b_ready, 1)
                        if what == "C":
                            pe.wait_ge(s.h2_ready, i * (2 * E0) + (2 * e + 2))
                            for q in range(BT):
                                if q % 2 == 0:
                                    pe.wait_ge(s.c_used, i * (E0 * BT) + (e * BT + q + 2))
                                for k in range(DK):
                                    ins = nc.tensor.matmul(psC[:, q, :], h2[:, e % 2, k, q * P:(q + 1) * P], g.w3[:, e, k, :],
                                                           start=(k == 0), stop=(k == DK - 1))
                                ins.then_inc(s.c_ready, 1)
                        if (what, e) == ("A", 0):
                            pe.wait_ge(s.rhT_ready, i + 1)
                            for q in range(BT):
                                ins = nc.tensor.matmul(psW[:, 1, q * E0:(q + 1) * E0], rhT[:, q * P:(q + 1) * P], g.rw2[:, :],
                                                       start=True, stop=True)
                            ins.then_inc(s.logits, 1)
                        if (what, e) == ("B", 1):
                            pe.wait_ge(s.gate_ready, i + 1)
                            pe.wait_ge(s.c_used, i * (E0 * BT) + BT)
                            for q in range(BT):
                                ins = nc.tensor.transpose(psC[0:E0, 0:2, :].rearrange("p a c -> p (a c)")[:, q * P:(q + 1) * P],
                                                          r.gate[:, q, :], g.ident[:, :])
                            ins.then_inc(s.gate_turned, 1)
                            pe.wait_ge(s.gateT_ready, i + 1)
                            for q in range(BT):
                                ins = nc.tensor.matmul(psW[:, q // 2, (q % 2) * D:(q % 2 + 1) * D], r.gateT[:, q * P:(q + 1) * P],
                                                       g.b3[:, :], start=True, stop=True)
                            ins.then_inc(s.bias_mixed, 1)
                    pe.wait_ge(s.acc_ready, i + 1)
                    pe.wait_ge(s.xn_ready, i * 2 + 2)
                    turn(nc, g, psW, lambda q: xn[:, q, :]).then_inc(s.turned, 1)
                    pe.wait_ge(s.xT_ready, i * 2 + 2)
                    for q in range(BT):
                        R = psA if q % 2 == 0 else psB
                        if q >= 2:
                            pe.wait_ge(s.qkv_ready, i * BT + (BT + q - 1))
                        for j, (a, b) in enumerate(((0, 512), (512, 768))):
                            for k in range(DK):
                                ins = nc.tensor.matmul(R[:, j, 0:b - a], xT[:, k, q * P:(q + 1) * P], g.wqkv[:, k, a:b],
                                                       start=(k == 0), stop=(k == DK - 1))
                        ins.then_inc(s.qkv_made, 1)

            @block.sync
            def _(sp):
                load_later(sp, d, g, s.stored)
                with sp.Fori(0, NB) as i:
                    sp.wait_ge(s.qkv_ready, i * BT + 2 * BT)
                    for j, table in ((1, d.k), (2, d.v)):
                        sp.dma_start(table[ds(i * BLK, BLK), :].rearrange("(t p) c -> p t c", p=P),
                                     qkv[:, :, j * D:(j + 1) * D]).then_inc(s.stored, 16)
                    sp.wait_ge(s.q3_ready, i + 1)
                    sp.dma_start(d.q3[ds(i * (3 * BLK), 3 * BLK), :].rearrange("(t p s) c -> p t s c", p=P, s=3),
                                 q3[:, :, :, :]).then_inc(s.stored, 16)
                sp.wait_ge(s.stored, 48 * NB + 16)


def load_later(sp, d, g, stored):
    for j, w in enumerate((d.wq, d.wk, d.wv)):
        sp.dma_start(g.wqkv[:, :, j * D:(j + 1) * D], w.rearrange("(k p) o -> p k o", p=P)).then_inc(g.qkv_loaded, 16)
    sp.dma_start(d.q3[3 * NP:3 * ACCW, :], g.none[0:3 * W, :]).then_inc(stored, 16)
    for dst, src in ((g.f1[:, :, :], d.f1.rearrange("(k p) o -> p k o", p=P)), (g.f2[:, :, :], d.f2.rearrange("(k p) o -> p k o", p=P)),
                     (g.rt[:, :, :], d.rt.rearrange("(k p) o -> p k o", p=P)), (g.mb2[:, :], d.mb2), (g.we[0:ED, :], d.we),
                     (g.we[ED:ED + 1, :], d.be), (g.wo[:, 0:2, :], d.wo[0:2 * VG, :].rearrange("(j p) o -> p j o", p=VG)),
                     (g.wo[0:D - 2 * VG, 2, :], d.wo[2 * VG:D, :])):
        sp.dma_start(dst, src).then_inc(g.loaded1, 16)


N_LOADED1 = 8



def stage_scores(nc, d, g):
    with ExitStack() as ctx:
        m = Mem(nc, ctx, "sco")
        ixs = m.sb("ixs", [P, G], I32)
        kg = m.sb("kg", [P, G, D])
        qw = m.sb("qw", [3 * W, G, D], BF16)
        eft = m.sb("eft", [ED + 1, 2, 4 * P])
        epb = m.sb("epb", [P, 2, 4, DH])
        oh3 = m.sb("oh3", [P, 2, 4, 3 * W], BF16)
        ohT = m.sb("ohT", [3 * W, 2, 4 * P], BF16)
        prod = m.sb("prod", [P, 2, 4, D])
        psT = [m.ps(f"psT{h}", [P, 1024], BF16) for h in range(2)]
        psE = m.ps("psE", [P, 512])
        psQ = m.ps("psQ", [P, G, D])
        got = [m.sem(f"got{b}") for b in range(G)]
        qw_got = [m.sem(f"qw_got{b}") for b in range(G)]
        eft_got = [m.sem(f"eft_got{h}") for h in range(2)]
        names = ("copied", "oh3_ready", "turned", "ohT_ready", "ep_made", "ep_ready", "q_ready", "with_ep",
                 "product", "s_ready", "ones")
        s = Names()
        (s.copied, s.oh3_ready, s.turned, s.ohT_ready, s.ep_made, s.ep_ready, s.q_ready, s.with_ep, s.product,
         s.s_ready, s.ones) = (m.sem(n) for n in names)
        with nc.Block() as block:
            @block.scalar
            def _(act):
                first_indices(nc, g, ixs, s.copied)
                nc.scalar.copy(g.spare[0:1, 12:13], g.eps[0:1, 0:1]).then_inc(s.ohT_ready, 1)
                nc.scalar.copy(g.spare[0:1, 13:14], g.eps[0:1, 0:1]).then_inc(s.ep_ready, 1)

                def body(i):
                    for h in range(2):
                        act.wait_ge(s.turned, i * 2 + (h + 3))
                        act.wait_ge(s.q_ready, i * 2 + (h + 1))
                        nc.scalar.copy(ohT[:, h, :], psT[h][0:3 * W, 0:4 * P]).then_inc(s.ohT_ready, 1)
                        act.wait_ge(s.ep_made, i * 2 + (h + 3))
                        act.wait_ge(s.with_ep, i * 2 + (h + 1))
                        nc.scalar.copy(epb[:, h, :, :].rearrange("p t c -> p (t c)"), psE[:, 0:4 * DH]).then_inc(s.ep_ready, 1)
                        index_copies(nc, act, g, ixs, got, s.copied, i, range(4 * h, 4 * h + 4))
                edge_loops(nc, act, g, body)

            @block.gpsimd
            def _(pool):
                edge_loops(nc, pool, g, lambda i: gathers(nc, pool, g, kg, ixs, d.k, got, s.copied, s.with_ep, 4, i))

            @block.sync
            def _(sp):
                def body(i, extra, features):
                    at = windows(nc, mybir.EngineType.SP, g, i)
                    for h in range(2):
                        sp.wait_ge(s.ep_made, i * 2 + (h + 1))
                        settle(sp)
                        if not extra:
                            sp.dma_start(eft[0:ED, h, :], features[:, ds((i * G + 4 * h) * P, 4 * P)]).then_inc(eft_got[h], 64)
                        for j in range(4):
                            b = 4 * h + j
                            if extra:
                                tl = sp.value_load(g.tile[0:1, ds(i * G + b, 1)], min_val=0, max_val=ET - 1)
                                sp.dma_start(eft[0:ED, h, j * P:(j + 1) * P], features[:, ds(tl * P, P)]).then_inc(eft_got[h], 16)
                            if j == 0:
                                sp.wait_ge(s.q_ready, i * 2 + (h + 1))
                                settle(sp)
                            sp.dma_start(qw[:, b, :], d.q3[ds(at[b] * 3, 3 * W), :]).then_inc(qw_got[b], 16)

                def steps(features):
                    with sp.Fori(0, ET // G) as i:
                        body(i, False, features)
                    over = sp.value_load(g.over[0:1, 0:1], min_val=0, max_val=2 * NP)
                    with sp.If(over):
                        with sp.Fori(ET // G, KS // G) as i:
                            body(i, True, features)

                with sp.If(sp.value_load(g.flags[0:1, 1:2], min_val=0, max_val=1)):
                    steps(d.eft)
                with sp.If(sp.value_load(g.flags[0:1, 0:1], min_val=0, max_val=1)):
                    steps(d.efs)

            @block.vector
            def _(dve):
                nc.vector.memset(eft[ED:ED + 1, :, :], 1.0).then_inc(s.ones, 1)
                nc.vector.memset(g.spare[0:1, 1:2], 0.0).then_inc(s.with_ep, 2)
                nc.vector.memset(g.spare[0:1, 2:3], 0.0).then_inc(s.product, 2)
                nc.vector.memset(g.spare[0:1, 3:4], 0.0).then_inc(s.s_ready, 1)

                def build(i, h):
                    dve.wait_ge(s.turned, i * 2 + (h + 1))
                    nc.vector.tensor_tensor(oh3[:, h, :, :], g.iota3[:, :].unsqueeze(1).to_broadcast([P, 4, 3 * W]),
                                            g.dstrel[:, ds(i * G + 4 * h, 4)].unsqueeze(2).to_broadcast([P, 4, 3 * W]),
                                            ALU.is_equal).then_inc(s.oh3_ready, 1)

                def body(i):
                    for h in range(2):
                        for j in range(4):
                            dve.wait_ge(got[4 * h + j], i * 16 + 16)
                        dve.wait_ge(s.ep_ready, i * 2 + (h + 2))
                        dve.wait_ge(s.s_ready, i * 2 + (h + 1))
                        nc.vector.tensor_tensor(prod[:, h, :, :].rearrange("p t (a c) -> p t a c", c=DH),
                                                kg[:, 4 * h:4 * h + 4, :].rearrange("p t (a c) -> p t a c", c=DH),
                                                epb[:, h, :, :].unsqueeze(2).to_broadcast([P, 4, H, DH]), ALU.add).then_inc(s.with_ep, 1)
                        dve.wait_ge(s.with_ep, i * 2 + (h + 3))
                        dve.wait_ge(s.q_ready, i * 2 + (h + 3))
                        nc.vector.tensor_tensor(prod[:, h, :, :], prod[:, h, :, :], psQ[:, 4 * h:4 * h + 4, :], ALU.mult).then_inc(s.product, 1)
                        dve.wait_ge(s.product, i * 2 + (h + 3))
                        nc.vector.tensor_reduce(g.S[:, ds(i * G + 4 * h, 4), :].rearrange("p t a -> p (t a)"),
                                                prod[:, h, :, :].rearrange("p t (a c) -> p (t a) c", c=DH), AX.X, ALU.add).then_inc(s.s_ready, 1)
                        build(i + 1, h)

                for h in range(2):
                    build(0, h)
                with dve.Fori(0, ET // G) as i:
                    body(i)
                dve.wait_ge(s.s_ready, 2 * ET // G + 1)
                over = dve.value_load(g.over[0:1, 0:1], min_val=0, max_val=2 * NP)
                with dve.If(over):
                    with dve.Fori(ET // G, KS // G) as i:
                        body(i)
                    dve.wait_ge(s.s_ready, 2 * KS // G + 1)
                    with dve.Fori(0, XS) as k:
                        tl = dve.value_load(g.tile[0:1, ds(k + ET, 1)], min_val=0, max_val=ET - 1)
                        Sd = g.S[:, ds(tl, 1), :]
                        nc.vector.tensor_tensor(Sd, Sd, g.S[:, ds(k + ET, 1), :], ALU.add).then_inc(s.s_ready, 1)
                        dve.wait_ge(s.s_ready, k + (2 * KS // G + 2))
                S0 = g.S[:, 0:ET, :]
                nc.vector.scalar_tensor_tensor(out=S0, in0=S0, scalar=DH ** -0.5,
                                               in1=g.ew[:, :].unsqueeze(2).to_broadcast([P, ET, H]), op0=ALU.mult, op1=ALU.mult)

            @block.tensor
            def _(pe):
                pe.wait_ge(s.ones, 1)
                pe.wait_ge(g.loaded1, 16 * N_LOADED1)
                free_at_first(nc, g, psE[0:32, 0:32], s.q_ready, 2)
                free_at_first(nc, g, psE[0:32, 32:64], s.turned, 2)
                free_at_first(nc, g, psE[0:32, 64:96], s.ep_made, 2)

                def body(i):
                    for h in range(2):
                        pe.wait_ge(s.oh3_ready, i * 2 + (h + 1))
                        pe.wait_ge(s.ohT_ready, i * 2 + (h + 1))
                        for j in range(4):
                            ins = nc.tensor.transpose(psT[h][0:3 * W, j * P:(j + 1) * P], oh3[:, h, j, :], g.identb[:, :])
                        ins.then_inc(s.turned, 1)
                        pe.wait_ge(eft_got[h], i * 64 + 64)
                        pe.wait_ge(s.ep_ready, i * 2 + (h + 1))
                        for j in range(4):
                            ins = nc.tensor.matmul(psE[:, j * DH:(j + 1) * DH], eft[:, h, j * P:(j + 1) * P], g.we[:, :],
                                                   start=True, stop=True)
                        ins.then_inc(s.ep_made, 1)
                        pe.wait_ge(s.ohT_ready, i * 2 + (h + 2))
                        pe.wait_ge(s.product, i * 2 + (h + 1))
                        for j in range(4):
                            b = 4 * h + j
                            pe.wait_ge(qw_got[b], i * 16 + 16)
                            ins = nc.tensor.matmul(psQ[:, b, :], ohT[:, h, j * P:(j + 1) * P], qw[:, b, :], start=True, stop=True)
                        ins.then_inc(s.q_ready, 1)
                edge_loops(nc, pe, g, body)



def stage_maximum(nc, d, g):
    NG = -(-ET // P)
    GT = [min(P, ET - P * j) for j in range(NG)]
    L = NG * H * P
    with ExitStack() as ctx:
        m = Mem(nc, ctx, "max")
        R = m.sb("R", [P, NG, H, P])
        M1 = m.sb("M1", [P, NG, H, P])
        flags = m.sb("flags", [P, L + 1])
        dT = m.sb("dT", [P, NG, P])
        end = m.sb("end", [H, ET])
        tot = m.sb("tot", [H, ET])
        same = m.sb("same", [H, ET])
        cont = m.sb("cont", [H, ET])
        carry = m.sb("carry", [H, NG * P])
        first = m.sb("first", [H, ET])
        last = m.sb("last", [H, ET])
        pick = m.sb("pick", [P, 2, H])
        ps = m.ps("ps", [P, 6, 512])
        psS = m.ps("psS", [P, 512])
        psR = m.ps("psR", [P, 512])
        ch, tn, pk, bk = m.sem("chain"), m.sem("turned"), m.sem("picked"), m.sem("back")

        def rows_of(X):
            return X[:, :, :, :].rearrange("p g a c -> p (g a c)")

        flatps = ps[:, :, :].rearrange("p b (a c) -> p (b a) c", c=P)
        with nc.Block() as block:
            @block.tensor
            def _(pe):
                pe.wait_ge(pk, 1)
                for j in range(NG):
                    nc.tensor.transpose(psS[0:GT[j], j * P:(j + 1) * P], g.dstF[:, j * P:j * P + GT[j]], g.ident[:, :])
                nc.tensor.matmul(psR[0:H, 0:ET], pick[:, 0, :], g.dstF[:, :], start=True, stop=True)
                for a in range(H):
                    for j in range(NG):
                        ins = nc.tensor.transpose(flatps[0:GT[j], j * H + a, :], g.S[:, j * P:j * P + GT[j], a], g.ident[:, :])
                ins.then_inc(tn, 1)
                pe.wait_ge(bk, 1)
                nc.tensor.matmul(psR[0:H, 0:ET], pick[:, 1, :], g.dstF[:, :], start=True, stop=True).then_inc(tn, 1)
                for way in range(2):
                    pe.wait_ge(bk, 2 + 2 * way)
                    X, c = (M1, P - 1) if way == 0 else (M1, 0)
                    for j in range(NG):
                        ins = nc.tensor.transpose(psS[0:H, j * P:j * P + GT[j]], X[0:GT[j], j, :, c], g.ident[0:GT[j], 0:GT[j]])
                    ins.then_inc(tn, 1)
                    pe.wait_ge(bk, 3 + 2 * way)
                    for j in range(NG):
                        ins = nc.tensor.transpose(psR[:, j * H:(j + 1) * H], carry[:, j * P:(j + 1) * P], g.ident[0:H, 0:H])
                    ins.then_inc(tn, 1)
                pe.wait_ge(bk, 6)
                for a in range(H):
                    for j in range(NG):
                        ins = nc.tensor.transpose(flatps[:, j * H + a, 0:GT[j]], M1[0:GT[j], j, a, :], g.ident[0:GT[j], 0:GT[j]])
                ins.then_inc(tn, 1)

            @block.vector
            def _(dve):
                t = Tally(ch)
                T = [0]

                def turned(n=1):
                    T[0] += n
                    dve.wait_ge(tn, T[0])

                def go(ins):
                    t.mark(ins)
                    t.wait(dve)

                nc.vector.memset(carry[:, :], 0.0)
                nc.vector.memset(R[:, NG - 1, :, :], 0.0)
                nc.vector.memset(dT[:, NG - 1, :], 0.0)
                nc.vector.tensor_copy(pick[:, 0, :], g.ident[:, 0:1].to_broadcast([P, H]))
                nc.vector.tensor_copy(pick[:, 1, :], g.ident[:, P - 1:P].to_broadcast([P, H])).then_inc(pk, 1)
                nc.vector.memset(flags[:, :], -BIG)
                turned()
                nc.vector.tensor_copy(first[:, :], psR[0:H, 0:ET]).then_inc(bk, 1)
                for j in range(NG):
                    nc.vector.tensor_copy(R[0:GT[j], j, :, :], flatps[0:GT[j], j * H:(j + 1) * H, :])
                    ins = nc.vector.tensor_copy(dT[0:GT[j], j, :], psS[0:GT[j], j * P:(j + 1) * P])
                go(ins)
                turned()
                go(nc.vector.tensor_copy(last[:, :], psR[0:H, 0:ET]))
                go(nc.vector.tensor_tensor(M1[:, :, 0, 1:P], dT[:, :, 1:P], dT[:, :, 0:P - 1], ALU.is_equal))
                go(nc.vector.tensor_scalar(M1[:, :, 0, 1:P], M1[:, :, 0, 1:P], 2.0, -1.0, ALU.mult, ALU.add))
                for a in range(H):
                    f = flags[:, 0:L].rearrange("p (g a c) -> p g a c", g=NG, a=H)[:, :, a, 1:P]
                    ins = nc.vector.tensor_scalar(f, M1[:, :, 0, 1:P], BIG, None, ALU.mult)
                go(ins)
                for way in range(2):
                    def rev(ap):
                        return ap[:, ::-1] if way else ap
                    fl = flags[:, way:L + way]
                    ins = nc.vector.tensor_tensor_scan(rev(rows_of(M1)), rev(fl), rev(rows_of(R)), -BIG, ALU.min, ALU.max)
                    ins.then_inc(bk, 1)
                    turned()
                    go(nc.vector.tensor_copy(end[:, :], psS[0:H, 0:ET]))
                    go(nc.vector.memset(same[:, :], 0.0))
                    go(nc.vector.memset(cont[:, :], 0.0))
                    if way == 0:
                        nc.vector.tensor_tensor(same[:, 1:ET], last[:, 1:ET], last[:, 0:ET - 1], ALU.is_equal)
                        go(nc.vector.tensor_tensor(cont[:, 1:ET], first[:, 1:ET], last[:, 0:ET - 1], ALU.is_equal))
                    else:
                        nc.vector.tensor_tensor(same[:, 0:ET - 1], first[:, 1:ET], first[:, 0:ET - 1], ALU.is_equal)
                        go(nc.vector.tensor_tensor(cont[:, 0:ET - 1], first[:, 1:ET], last[:, 0:ET - 1], ALU.is_equal))
                    for f in (same, cont):
                        go(nc.vector.tensor_scalar(f[:, :], f[:, :], 2.0, -1.0, ALU.mult, ALU.add))
                        go(nc.vector.tensor_scalar(f[:, :], f[:, :], BIG, None, ALU.mult))
                    go(nc.vector.tensor_tensor_scan(rev(tot[:, :]), rev(same[:, :]), rev(end[:, :]), -BIG, ALU.min, ALU.max))
                    go(nc.vector.tensor_copy(carry[:, 0:ET], cont[:, :]))
                    if way == 0:
                        go(nc.vector.tensor_tensor(carry[:, 1:ET], tot[:, 0:ET - 1], cont[:, 1:ET], ALU.min))
                    else:
                        go(nc.vector.tensor_tensor(carry[:, 0:ET - 1], tot[:, 1:ET], cont[:, 0:ET - 1], ALU.min))
                    nc.vector.tensor_scalar(carry[:, 0:ET], carry[:, 0:ET], -BIG, None, ALU.max).then_inc(bk, 1)
                    turned()
                    c = P - 1 if way else 0
                    src = R[:, :, :, c]
                    go(nc.vector.tensor_tensor(src, src, psR[:, 0:NG * H].rearrange("p (j a) -> p j a", a=H), ALU.max))
                    ins = nc.vector.tensor_tensor_scan(rev(rows_of(M1)), rev(fl), rev(rows_of(R)), -BIG, ALU.min, ALU.max)
                    if way == 0:
                        go(ins)
                        go(nc.vector.tensor_copy(rows_of(R), rows_of(M1)))
                    else:
                        ins.then_inc(bk, 1)
                turned()
                for j in range(NG):
                    Sj = g.S[:, j * P:j * P + GT[j], :]
                    ins = nc.vector.tensor_tensor(Sj, Sj, flatps[:, j * H:(j + 1) * H, 0:GT[j]].rearrange("p a t -> p t a"), ALU.subtract)
                ins.then_inc(bk, 1)

            @block.scalar
            def _(act):
                act.wait_ge(bk, 7)
                nc.scalar.activation(g.S[:, 0:ET, :], g.S[:, 0:ET, :], ACT.Exp)



def stage_gather1(nc, d, g):
    with ExitStack() as ctx:
        m = Mem(nc, ctx, "ga1")
        ixs = m.sb("ixs", [P, G], I32)
        vg = m.sb("vg", [P, G, D])
        oh = m.sb("oh", [P, 2, 4, W])
        pv = m.sb("pv", [P, 2, 4, 3 * VG])
        psO = m.ps("psO", [P, 4, 512])
        got = [m.sem(f"got{b}") for b in range(G)]
        names = ("copied", "oh_ready", "pv_ready", "o_ready", "o_added", "cleared", "moved")
        s = Names()
        (s.copied, s.oh_ready, s.pv_ready, s.o_ready, s.o_added, s.cleared, s.moved) = (m.sem(n) for n in names)
        with nc.Block() as block:
            @block.scalar
            def _(act):
                first_indices(nc, g, ixs, s.copied)
                edge_loops(nc, act, g, lambda i: index_copies(nc, act, g, ixs, got, s.copied, i))

            @block.gpsimd
            def _(pool):
                edge_loops(nc, pool, g, lambda i: gathers(nc, pool, g, vg, ixs, d.v, got, s.copied, s.pv_ready, 4, i))

            @block.vector
            def _(dve):
                nc.vector.memset(g.spare[0:1, 4:5], 0.0).then_inc(s.pv_ready, 2)
                nc.vector.memset(g.spare[0:1, 5:6], 0.0).then_inc(s.o_added, 1)
                nc.vector.memset(g.oacc[:, :, :], 0.0).then_inc(s.cleared, 1)
                dve.wait_ge(s.cleared, 1)
                over = dve.value_load(g.over[0:1, 0:1], min_val=0, max_val=2 * NP)
                with dve.If(over):
                    with dve.Fori(0, XS) as k:
                        tl = dve.value_load(g.tile[0:1, ds(k + ET, 1)], min_val=0, max_val=ET - 1)
                        nc.vector.tensor_copy(g.S[:, ds(k + ET, 1), :], g.S[:, ds(tl, 1), :]).then_inc(s.moved, 1)
                    dve.wait_ge(s.moved, XS)

                def build(i, h):
                    dve.wait_ge(s.o_ready, i * 2 + (h + 1))
                    nc.vector.tensor_tensor(oh[:, h, :, :], g.iota[:, :].unsqueeze(1).to_broadcast([P, 4, W]),
                                            g.dstrel[:, ds(i * G + 4 * h, 4)].unsqueeze(2).to_broadcast([P, 4, W]),
                                            ALU.is_equal).then_inc(s.oh_ready, 1)

                def weigh(i, h):
                    for j in range(4):
                        dve.wait_ge(got[4 * h + j], i * 16 + 16)
                    dve.wait_ge(s.o_ready, i * 2 + (h + 1))
                    p8 = g.S[:, ds(i * G + 4 * h, 4), :]
                    nc.vector.tensor_copy(pv[:, h, :, D:D + H], p8)
                    nc.vector.tensor_tensor(pv[:, h, :, 0:D].rearrange("p t (a c) -> p t a c", c=DH),
                                            vg[:, 4 * h:4 * h + 4, :].rearrange("p t (a c) -> p t a c", c=DH),
                                            p8.unsqueeze(3).to_broadcast([P, 4, H, DH]), ALU.mult).then_inc(s.pv_ready, 1)

                def add(i, h, at):
                    dve.wait_ge(s.o_ready, i * 2 + (h + 3))
                    for j in range(4):
                        dve.wait_ge(s.o_added, i * G + (4 * h + j + 1))
                        o = g.oacc[:, :, ds(at[j], W)]
                        nc.vector.tensor_tensor(o, psO[0:VG, h, j * 3 * W:(j + 1) * 3 * W].rearrange("p (c w) -> p c w", c=3),
                                                o, ALU.add).then_inc(s.o_added, 1)
                    build(i + 1, h)

                for h in range(2):
                    build(0, h)
                at = windows(nc, mybir.EngineType.DVE, g, 0)
                weigh(0, 0)
                weigh(0, 1)
                add(0, 0, at[0:4])
                with dve.Fori(1, ET // G) as i:
                    at = windows(nc, mybir.EngineType.DVE, g, i, -4)
                    weigh(i, 0)
                    add(i - 1, 1, at[0:4])
                    weigh(i, 1)
                    add(i, 0, at[4:8])
                at = windows(nc, mybir.EngineType.DVE, g, ET // G - 1)
                add(ET // G - 1, 1, at[4:8])
                over = dve.value_load(g.over[0:1, 0:1], min_val=0, max_val=2 * NP)
                with dve.If(over):
                    with dve.Fori(ET // G, KS // G) as i:
                        at = windows(nc, mybir.EngineType.DVE, g, i)
                        for h in range(2):
                            weigh(i, h)
                        for h in range(2):
                            add(i, h, at[4 * h:4 * h + 4])

            @block.tensor
            def _(pe):
                free_at_first(nc, g, psO[0:32, 3, 0:32], s.o_ready, 2)

                def body(i):
                    for h in range(2):
                        pe.wait_ge(s.oh_ready, i * 2 + (h + 1))
                        pe.wait_ge(s.pv_ready, i * 2 + (h + 3))
                        pe.wait_ge(s.o_added, i * G + (4 * h + 1))
                        for j in range(4):
                            for c in range(3):
                                ins = nc.tensor.matmul(psO[0:VG, h, (j * 3 + c) * W:(j * 3 + c + 1) * W], pv[:, h, j, c * VG:(c + 1) * VG],
                                                       oh[:, h, j, :], start=True, stop=True)
                        ins.then_inc(s.o_ready, 1)
                edge_loops(nc, pe, g, body)





def stage_feed_forward(nc, d, g):
    with ExitStack() as ctx:
        m = Mem(nc, ctx, "ff")
        nm = Norm(m, 0, 1)
        head = m.sb("head", [VG, 3, VG])
        ab = m.sb("ab", [P, DK])
        den = m.sb("den", [VG, 3, BLK])
        aT = m.sb("aT", [P, DK, BLK])
        xn = m.sb("xn", [P, BT, D])
        xT = m.sb("xT", [P, DK, BLK])
        h = m.sb("h", [P, FK, BLK])
        y = m.sb("y", [P, BT, D])
        ps3 = m.ps("ps3", [P, 4, 512])
        psW = m.ps("psW", [P, 2, 512])
        psY = m.ps("psY", [P, BT, D])
        names = ("chain", "ab_ready", "head_ready", "den_made", "den_used", "o_ready", "a_made", "aT_ready", "a_turned", "xn_ready", "turned",
                 "xT_ready", "h_made", "h_ready", "y_made", "y_read")
        s = Names()
        (s.chain, s.ab_ready, s.head_ready, s.den_made, s.den_used, s.o_ready, s.a_made, s.aT_ready, s.a_turned,
         s.xn_ready, s.turned, s.xT_ready, s.h_made, s.h_ready, s.y_made, s.y_read) = (m.sem(n) for n in names)
        with nc.Block() as block:
            @block.gpsimd
            def _(pool):
                nc.gpsimd.memset(head[:, :, :], 1.0).then_inc(s.head_ready, 1)
                pool.wait_ge(s.head_ready, 1)
                first = DH * (D - 2 * VG)
                nc.gpsimd.affine_select(out=head[:, :, :], in_=head[:, :, :], compare_op=ALU.is_ge, fill=0.0, base=first,
                                        pattern=[[VG, 3], [1, VG]], channel_multiplier=-DH).then_inc(s.head_ready, 1)
                pool.wait_ge(s.head_ready, 2)
                nc.gpsimd.affine_select(out=head[:, :, :], in_=head[:, :, :], compare_op=ALU.is_ge, fill=0.0, base=DH - 1 - first,
                                        pattern=[[-VG, 3], [-1, VG]], channel_multiplier=DH).then_inc(s.head_ready, 1)

            @block.sync
            def _(sp):
                for w_sb, w in ((g.mw1, d.mw1), (g.mw2, d.mw2)):
                    for e in range(E1):
                        sp.dma_start(w_sb[:, e, :, :], w[e].rearrange("(k p) o -> p k o", p=P)).then_inc(g.weights1, 16)

            @block.vector
            def _(dve):
                nc.vector.tensor_scalar(ab[:, :], g.cols[:, COL["bo"][0]:COL["bo"][1]], row(g, "alpha"), None, ALU.mult).then_inc(s.ab_ready, 1)
                nc.vector.memset(g.spare[0:1, 1:2], 0.0).then_inc(s.chain, 1)
                with dve.Fori(0, NB) as i:
                    t = Tally(s.chain, i, 8, 1)
                    for j in range(3):
                        dve.wait_ge(s.den_made, i * 3 + (j + 1))
                        ins = nc.vector.tensor_scalar(den[:, j, :], ps3[0:VG, j, :], 0.5, None, ALU.max)
                    t.mark(ins)
                    t.wait(dve)
                    t.mark(nc.vector.reciprocal(den[:, :, :], den[:, :, :]))
                    t.wait(dve)
                    nc.vector.tensor_tensor(den[:, :, :], den[:, :, :], g.oacc[:, :, ds(i * BLK, BLK)], ALU.mult).then_inc(s.o_ready, 1)
                    dve.wait_ge(s.a_turned, i + 1)
                    ub = g.u[:, ds(i * BT, BT), :]
                    t.mark(nc.vector.tensor_tensor(ub, psY[:, :, :], ub, ALU.add))
                    norm_dve(nc, dve, g, nm, t, i, 1, 0, lambda q: g.u[:, ds(i * BT + q, 1), :].rearrange("p a c -> p (a c)"),
                             lambda q: xn[:, q, :], s.xn_ready)
                    dve.wait_ge(s.y_made, i + 1)
                    b2 = row(g, "b2").unsqueeze(1).to_broadcast([P, BT, D])
                    t.mark(nc.vector.tensor_tensor(y[:, :, :], psY[:, :, :], b2, ALU.add))
                    t.wait(dve)
                    t.mark(nc.vector.scalar_tensor_tensor(out=ub, in0=y[:, :, :], scalar=row(g, "beta"), in1=ub, op0=ALU.mult, op1=ALU.add))
                    t.wait(dve)
                    xb = g.x[:, ds(i * BT, BT), :]
                    t.mark(nc.vector.tensor_tensor(xb, xb, ub, ALU.add))
                    t.close()

            @block.scalar
            def _(act):
                act.wait_ge(s.ab_ready, 1)
                nc.scalar.copy(g.spare[0:1, 14:15], g.eps[0:1, 0:1]).then_inc(s.h_ready, 1)
                with act.Fori(0, NB) as i:
                    for o in range(DK):
                        act.wait_ge(s.a_made, i * 2 + (o + 1))
                        nc.scalar.activation(aT[:, o, :], psW[:, o, :], ACT.Identity, bias=ab[:, o:o + 1],
                                             scale=row(g, "alpha")).then_inc(s.aT_ready, 1)
                    norm_act(nc, act, g, nm, i, 1, 0)
                    act.wait_ge(s.turned, i + 1)
                    for k in range(DK):
                        ins = nc.scalar.activation(xT[:, k, :], psW[:, k, :], ACT.Identity, bias=vec(g, "ln2_b", k),
                                                   scale=vec(g, "ln2_g", k))
                    ins.then_inc(s.xT_ready, 1)
                    for f in range(FK):
                        act.wait_ge(s.h_made, i * FK + (f + 1))
                        nc.scalar.activation(h[:, f, :], ps3[:, f % 4, :], ACT.Gelu, bias=vec(g, "gb1", f)).then_inc(s.h_ready, 1)

            @block.tensor
            def _(pe):
                pe.wait_ge(s.head_ready, 3)
                with pe.Fori(0, NB) as i:
                    pe.wait_ge(s.h_ready, i * FK + 1)
                    for j in range(3):
                        nc.tensor.matmul(ps3[0:VG, j, :], head[:, j, :], g.oacc[:, 2, ds(i * BLK, BLK)], start=True,
                                         stop=True).then_inc(s.den_made, 1)
                    pe.wait_ge(s.o_ready, i + 1)
                    for o in range(DK):
                        for j in range(3):
                            K = VG if j < 2 else D - 2 * VG
                            ins = nc.tensor.matmul(psW[:, o, :], g.wo[0:K, j, o * P:(o + 1) * P], den[0:K, j, :],
                                                   start=(j == 0), stop=(j == 2))
                        ins.then_inc(s.a_made, 1)
                    pe.wait_ge(s.aT_ready, i * 2 + 2)
                    pe.wait_ge(s.chain, i * 8 + 1)
                    for q in range(BT):
                        for k in range(DK):
                            ins = nc.tensor.transpose(psY[:, q, k * P:(k + 1) * P], aT[:, k, q * P:(q + 1) * P], g.ident[:, :])
                    ins.then_inc(s.a_turned, 1)
                    pe.wait_ge(s.xn_ready, i + 1)
                    turn(nc, g, psW, lambda q: xn[:, q, :]).then_inc(s.turned, 1)
                    pe.wait_ge(s.xT_ready, i + 1)
                    for f in range(FK):
                        if f >= 4:
                            pe.wait_ge(s.h_ready, i * FK + (f - 2))
                        for k in range(DK):
                            ins = nc.tensor.matmul(ps3[:, f % 4, :], g.f1[:, k, f * P:(f + 1) * P], xT[:, k, :],
                                                   start=(k == 0), stop=(k == DK - 1))
                        ins.then_inc(s.h_made, 1)
                    pe.wait_ge(s.h_ready, i * FK + (FK + 1))
                    for q in range(BT):
                        for f in range(FK):
                            ins = nc.tensor.matmul(psY[:, q, :], h[:, f, q * P:(q + 1) * P], g.f2[:, f, :],
                                                   start=(f == 0), stop=(f == FK - 1))
                    ins.then_inc(s.y_made, 1)



def stage_experts1(nc, d, g):
    order = []
    for e in range(E1 + 1):
        order += [(s, x) for s, x in (("A", e), ("C", e - 1)) if 0 <= x < E1]
    with ExitStack() as ctx:
        m = Mem(nc, ctx, "ex1")
        nm = Norm(m, 0, 1)
        r = Router(m, E1)
        xn = m.sb("xn", [P, BT, D])
        xT = m.sb("xT", [P, DK, BLK])
        h1 = m.sb("h1", [P, 2, DK, BLK])
        spare = m.sb("spare", [1, DH])
        acc = m.sb("acc", [P, BT, D])
        psW = m.ps("psW", [P, 2, 512])
        psA = m.ps("psA", [P, 2, 2, 512])
        psC = m.ps("psC", [P, BT, D])
        names = ("chain", "xn_ready", "turned", "xT_ready", "logits", "gate_ready", "gate_turned", "gateT_ready", "bias_mixed",
                 "acc_ready", "a_ready", "h1_ready", "c_ready", "c_used", "out_ready", "stored")
        s = Names()
        (s.chain, s.xn_ready, s.turned, s.xT_ready, s.logits, s.gate_ready, s.gate_turned, s.gateT_ready,
         s.bias_mixed, s.acc_ready, s.a_ready, s.h1_ready, s.c_ready, s.c_used, s.out_ready, s.stored) = (m.sem(n) for n in names)
        with nc.Block() as block:
            @block.vector
            def _(dve):
                nc.vector.memset(g.spare[0:1, 2:3], 0.0).then_inc(s.c_used, BT)
                nc.vector.memset(g.spare[0:1, 3:4], 0.0).then_inc(s.chain, 1)
                nc.vector.memset(g.spare[0:1, 4:5], 0.0).then_inc(s.acc_ready, 1)
                with dve.Fori(0, NB) as i:
                    t = Tally(s.chain, i, 23, 1)
                    norm_dve(nc, dve, g, nm, t, i, 1, 0, lambda q: g.x[:, ds(i * BT + q, 1), :].rearrange("p a c -> p (a c)"),
                             lambda q: xn[:, q, :], s.xn_ready)
                    dve.wait_ge(s.logits, i + 1)
                    gates_dve(nc, dve, g, r, t, i, E1, psW[:, 1, 0:BT * E1].rearrange("p (t e) -> p t e", t=BT), None, 1)
                    t.mark(nc.vector.tensor_tensor(r.m[:, :, 2], r.m[:, :, 0], r.m[:, :, 1], ALU.add))
                    t.wait(dve)
                    t.mark(nc.vector.tensor_scalar(r.m[:, :, 2], r.m[:, :, 2], 1e-12, None, ALU.max))
                    t.wait(dve)
                    t.mark(nc.vector.reciprocal(r.m[:, :, 3], r.m[:, :, 2]))
                    t.wait(dve)
                    nc.vector.tensor_tensor(r.m[:, :, 0], r.m[:, :, 0], r.m[:, :, 3], ALU.mult)
                    t.mark(nc.vector.tensor_tensor(r.m[:, :, 1], r.m[:, :, 1], r.m[:, :, 3], ALU.mult))
                    t.wait(dve)
                    mix_dve(nc, dve, r, t, E1, r.m[:, :, 0], r.m[:, :, 1], s.gate_ready)
                    dve.wait_ge(s.gate_ready, i + 1)
                    dve.wait_ge(s.bias_mixed, i + 1)
                    dve.wait_ge(s.stored, i * 16 + 16)
                    nc.vector.tensor_tensor(acc[:, :, :], psW[:, :, :].rearrange("p a c -> p (a c)").rearrange("p (t c) -> p t c", t=BT),
                                            xn[:, :, :], ALU.add).then_inc(s.acc_ready, 1)
                    dve.wait_ge(s.acc_ready, i + 2)
                    for e in range(E1):
                        for q in range(BT):
                            if q % 2 == 0:
                                dve.wait_ge(s.c_ready, i * (E1 * BT) + (e * BT + q + 2))
                            dve.wait_ge(s.c_used, i * (E1 * BT) + (e * BT + q + 1))
                            nc.vector.scalar_tensor_tensor(out=acc[:, q, :], in0=psC[:, q, :], scalar=r.gate[:, q, e:e + 1],
                                                           in1=acc[:, q, :], op0=ALU.mult, op1=ALU.add).then_inc(s.c_used, 1)
                    dve.wait_ge(s.c_used, i * (E1 * BT) + (E1 * BT + BT))
                    nc.vector.tensor_tensor(acc[:, :, :], acc[:, :, :], g.x[:, ds(i * BT, BT), :], ALU.add).then_inc(s.out_ready, 1)
                    t.close()

            @block.scalar
            def _(act):
                with act.Fori(0, NB) as i:
                    norm_act(nc, act, g, nm, i, 1, 0)
                    act.wait_ge(s.turned, i + 1)
                    nc.scalar.copy(xT[:, :, :], psW[:, :, :]).then_inc(s.xT_ready, 1)
                    act.wait_ge(r.shifted, i + 1)
                    nc.scalar.activation(r.p[:, :, :], r.p[:, :, :], ACT.Exp).then_inc(r.p_ready, 1)
                    for e in range(E1):
                        for o in range(DK):
                            act.wait_ge(s.a_ready, i * (2 * E1) + (2 * e + o + 1))
                            nc.scalar.activation(h1[:, e % 2, o, :], psA[:, e % 2, o, :], ACT.Gelu,
                                                 bias=vec(g, "mb1", 2 * e + o)).then_inc(s.h1_ready, 1)
                        if e == 1:
                            act.wait_ge(s.gate_turned, i + 1)
                            nc.scalar.copy(r.gateT[:, :], psC[0:E1, 0:2, :].rearrange("p a c -> p (a c)")).then_inc(s.gateT_ready, 1)

            @block.tensor
            def _(pe):
                pe.wait_ge(g.weights1, 16 * 2 * E1)
                with pe.Fori(0, NB) as i:
                    pe.wait_ge(s.acc_ready, i + 1)
                    pe.wait_ge(s.xn_ready, i + 1)
                    turn(nc, g, psW, lambda q: xn[:, q, :]).then_inc(s.turned, 1)
                    pe.wait_ge(s.xT_ready, i + 1)
                    for q in range(BT):
                        for k in range(DK):
                            ins = nc.tensor.matmul(psW[:, 1, q * E1:(q + 1) * E1], xT[:, k, q * P:(q + 1) * P], g.rt[:, k, :],
                                                   start=(k == 0), stop=(k == DK - 1))
                    ins.then_inc(s.logits, 1)
                    for what, e in order:
                        if what == "A":
                            if e >= 2:
                                pe.wait_ge(s.h1_ready, i * (2 * E1) + (2 * e - 2))
                            for o in range(DK):
                                for k in range(DK):
                                    ins = nc.tensor.matmul(psA[:, e % 2, o, :], g.mw1[:, e, k, o * P:(o + 1) * P], xT[:, k, :],
                                                           start=(k == 0), stop=(k == DK - 1))
                                ins.then_inc(s.a_ready, 1)
                        if what == "A" and e == 1:
                            pe.wait_ge(s.gate_ready, i + 1)
                            pe.wait_ge(s.c_used, i * (E1 * BT) + BT)
                            for q in range(BT):
                                ins = nc.tensor.transpose(psC[0:E1, 0:2, :].rearrange("p a c -> p (a c)")[:, q * P:(q + 1) * P],
                                                          r.gate[:, q, :], g.ident[:, :])
                            ins.then_inc(s.gate_turned, 1)
                            pe.wait_ge(s.gateT_ready, i + 1)
                            for q in range(BT):
                                ins = nc.tensor.matmul(psW[:, q // 2, (q % 2) * D:(q % 2 + 1) * D], r.gateT[:, q * P:(q + 1) * P],
                                                       g.mb2[:, :], start=True, stop=True)
                            ins.then_inc(s.bias_mixed, 1)
                        if what == "C":
                            pe.wait_ge(s.h1_ready, i * (2 * E1) + (2 * e + 2))
                            for q in range(BT):
                                if q % 2 == 0:
                                    pe.wait_ge(s.c_used, i * (E1 * BT) + (e * BT + q + 2))
                                for k in range(DK):
                                    ins = nc.tensor.matmul(psC[:, q, :], h1[:, e % 2, k, q * P:(q + 1) * P], g.mw2[:, e, k, :],
                                                           start=(k == 0), stop=(k == DK - 1))
                                ins.then_inc(s.c_ready, 1)

            @block.sync
            def _(sp):
                sp.dma_start(spare[:, :], d.be).then_inc(s.stored, 16)
                with sp.Fori(0, NB) as i:
                    sp.wait_ge(s.out_ready, i + 1)
                    sp.dma_start(d.out[ds(i * BLK, BLK), :].rearrange("(t p) c -> p t c", p=P), acc[:, :, :]).then_inc(s.stored, 16)
                sp.wait_ge(s.stored, 16 * NB + 16)



class Names:
    pass


IN = {
    "x": ([NP, D], F32), "src": ([P, ET], I32), "dst": ([P, ET], I32), "typ": ([P, ET], I32), "ew": ([P, ET], F32),
    "line": ([P, LINE + 1], I32), "ef": ([EP, ED], F32), "eft": ([ED, EP], F32), "cols": ([P, NCOL], F32), "rows": ([1, NROW], F32),
    "basis": ([NBASE, D, D], F32), "loopw": ([D, D], F32), "rw1": ([D, RH], F32), "rw2": ([RH, E0], F32),
    "w1": ([E0, D, D], F32), "w2": ([E0, D, D], F32), "w3": ([E0, D, D], F32), "b3": ([E0, D], F32),
    "wq": ([D, D], F32), "wk": ([D, D], F32), "wv": ([D, D], F32), "we": ([ED, DH], F32), "be": ([1, DH], F32),
    "wo": ([D, D], F32), "f1": ([D, FF], F32), "f2": ([FF, D], F32), "rt": ([D, E1], F32),
    "mw1": ([E1, D, D], F32), "mw2": ([E1, D, D], F32), "mb2": ([E1, D], F32),
}


def program(nc, stages=99):
    d, g = Names(), Names()
    (d.x, d.src, d.dst, d.typ, d.ew, d.line, d.ef, d.eft, d.cols, d.rows, d.basis, d.loopw, d.rw1, d.rw2, d.w1, d.w2, d.w3, d.b3,
     d.wq, d.wk, d.wv, d.we, d.be, d.wo, d.f1, d.f2, d.rt, d.mw1, d.mw2, d.mb2) = \
        (nc.dram_tensor(f"in_{name}", shape, dt, kind="ExternalInput").ap() for name, (shape, dt) in IN.items())
    d.out = nc.dram_tensor("out_0", [NP, D], F32, kind="ExternalOutput").ap()
    d.xn, d.k, d.v = (nc.dram_tensor(f"table_{name}", [NP, D], F32).ap() for name in ("xn", "k", "v"))
    d.q3 = nc.dram_tensor("table_q3", [3 * ACCW, D], BF16).ap()
    d.sorted = nc.dram_tensor("sorted_edges", [EP, 4 + ED], F32).ap()
    d.efs = nc.dram_tensor("sorted_features", [ED, EP], F32).ap()
    with ExitStack() as ctx:
        m = Mem(nc, ctx, "g")
        g.ident = m.sb("ident", [P, P])
        g.identb = m.sb("identb", [P, P], BF16)
        g.iota = m.sb("iota", [P, W])
        g.iota3 = m.sb("iota3", [P, 3 * W])
        g.rev = m.sb("rev", [P, E1])
        g.eps = m.sb("eps", [P, 1])
        g.spare = m.sb("spare", [1, 16])
        g.none = m.sb("none", [P, D], BF16)
        g.cols = m.sb("cols", [P, NCOL])
        g.rows = m.sb("rows", [P, NROW])
        g.x = m.sb("x", [P, NT, D])
        g.srcI = m.sb("srcI", [P, KS + G], I32)
        g.ew = m.sb("ew", [P, ET])
        g.dstF = m.sb("dstF", [P, ET])
        g.dstrel = m.sb("dstrel", [P, KS + G])
        g.win = m.sb("win", [1, KS], I32)
        g.tile = m.sb("tile", [1, KS], I32)
        g.over = m.sb("over", [1, 1], I32)
        g.flags = m.sb("flags", [1, 2], I32)
        g.weights0 = m.sem("weights0")
        g.rw1 = m.sb("rw1", [P, DK, RH])
        g.rw2 = m.sb("rw2", [P, E0])
        g.b3 = m.sb("b3", [E0, D])
        g.experts = m.sb("experts", [P, 3 * E0, DK, D])
        g.w1, g.w2, g.w3 = (g.experts[:, j * E0:(j + 1) * E0, :, :] for j in range(3))
        g.mw1, g.mw2 = (g.experts[:, j * E1:(j + 1) * E1, :, :] for j in range(2))
        with ExitStack() as sums:
            ms = Mem(nc, sums, "z0")
            g.coef = ms.sb("coef", [P, KS + G, NBASE])
            g.basis = ms.sb("basis", [P, NBASE, DK, D])
            g.loopw = ms.sb("loopw", [P, DK, D])
            g.dstI = ms.sb("dstI", [P, ET], I32)
            g.typI = ms.sb("typI", [P, ET], I32)
            stage_load(nc, d, g)
            stage_sort(nc, d, g)
            stage_tables(nc, d, g)
            stage_self_loop(nc, d, g)
            g.ZT = ms.sb("ZT", [P, DK, NBASE, ACCW])
            if stages >= 2:
                stage_gather0(nc, d, g)
                stage_bases(nc, d, g)
        if stages < 3:
            debug_out(nc, d, g, stages)
            return
        g.u = m.sb("u", [P, NT, D])
        g.wqkv = m.sb("wqkv", [P, DK, 3 * D])
        g.f1 = m.sb("f1", [P, DK, FF])
        g.f2 = m.sb("f2", [P, FK, D])
        g.rt = m.sb("rt", [P, DK, E1])
        g.mb2 = m.sb("mb2", [E1, D])
        g.we = m.sb("we", [ED + 1, DH])
        g.wo = m.sb("wo", [VG, 3, D])
        g.loaded1 = m.sem("loaded1")
        g.qkv_loaded = m.sem("qkv_loaded")
        stage_experts0(nc, d, g)
        later_stages(nc, d, g, stages)


def later_stages(nc, d, g, stages):
    if stages < 4:
        debug_out(nc, d, g, stages, g.u if stages == 3.5 else None)
        return
    with ExitStack() as ctx:
        m = Mem(nc, ctx, "g1")
        g.weights1 = m.sem("weights1")
        g.S = m.sb("S", [P, KS, H])
        stage_scores(nc, d, g)
        stage_maximum(nc, d, g)
        if stages == 4:
            debug_out(nc, d, g, stages, g.S[:, 0:ET, :].rearrange("p t a -> p (t a)").rearrange("p (t c) -> p t c", c=D), NT // 2)
            return
        g.oacc = m.sb("oacc", [VG, 3, ACCW])
        stage_gather1(nc, d, g)
        stage_feed_forward(nc, d, g)
        if stages == 5:
            debug_out(nc, d, g, stages, g.u)
            return
        stage_experts1(nc, d, g)


def debug_out(nc, d, g, stages, what=None, tiles=NT):
    with ExitStack() as ctx:
        s = ctx.enter_context(nc.semaphore("dbg"))
        with nc.Block() as block:
            @block.sync
            def _(sp):
                sp.dma_start(d.out[0:tiles * P, :].rearrange("(t p) c -> p t c", p=P), (g.x if what is None else what)[:, 0:tiles, :]).then_inc(s, 16)
                sp.wait_ge(s, 16)
                sp.wait_ge(g.weights0, 16 * 3 * E0)
                if stages >= 3:
                    sp.wait_ge(g.loaded1, 16 * N_LOADED1)
                if stages == 5:
                    sp.wait_ge(g.weights1, 16 * 2 * E1)



def edge_columns(a, pad):
    import numpy as np
    return np.ascontiguousarray(np.concatenate([a, np.full(EP - E, pad, a.dtype)]).reshape(ET, P).T)


def layout(i):
    import numpy as np

    def cat(names, shape):
        return np.concatenate([np.asarray(i[n]).reshape(shape) for n in names], axis=1)

    x = np.asarray(i["x"])
    out = {
        "x": np.concatenate([x, np.zeros((NP - N, D), x.dtype)]),
        "src": edge_columns(np.asarray(i["src"]), 0), "dst": edge_columns(np.asarray(i["dst"]), N),
        "typ": edge_columns(np.asarray(i["edge_type_8"]), 0), "ew": edge_columns(np.asarray(i["edge_weight"]), 0),
    }
    ef = np.asarray(i["edge_attr_64"])
    out["ef"] = np.concatenate([ef, np.zeros((EP - E, ED), ef.dtype)])
    out["eft"] = np.ascontiguousarray(out["ef"].T)
    dst = np.asarray(i["dst"])
    line = np.concatenate([dst, np.full(EP + 1 - E, N, dst.dtype)])
    out["line"] = np.ascontiguousarray(np.concatenate([line[:EP].reshape(P, LINE), line[LINE:][::LINE].reshape(P, 1)], axis=1))
    col = {"rb1": "L0_ffn_router_b1", "eb1": "L0_ffn_expert_b1", "eb2": "L0_ffn_expert_b2", "ln1_g": "L1_gnn_ln1_g",
           "ln1_b": "L1_gnn_ln1_b", "ln2_g": "L1_gnn_ln2_g", "ln2_b": "L1_gnn_ln2_b", "bo": "L1_gnn_bo",
           "gb1": "L1_gnn_b1", "mb1": "L1_ffn_b1"}
    out["cols"] = np.ascontiguousarray(np.concatenate([np.asarray(i[col[n]]).reshape(-1, P) for n in COLS]).T)
    row = {"bias0": ["L0_gnn_bias_param"], "rb2": ["L0_ffn_router_b2"], "qkvb": ["L1_gnn_bq", "L1_gnn_bk", "L1_gnn_bv"],
           "b2": ["L1_gnn_b2"], "alpha": ["L1_gnn_alpha"], "beta": ["L1_gnn_beta"], "comp": ["L0_gnn_comp"]}
    out["rows"] = np.concatenate([cat(row[n], (1, -1)) for n in ROWS], axis=1)
    for name, source in {"basis": "L0_gnn_basis", "loopw": "L0_gnn_loop_weight", "rw1": "L0_ffn_router_w1", "rw2": "L0_ffn_router_w2",
                         "w1": "L0_ffn_expert_w1", "w2": "L0_ffn_expert_w2", "w3": "L0_ffn_expert_w3", "b3": "L0_ffn_expert_b3",
                         "wq": "L1_gnn_Wq", "wk": "L1_gnn_Wk", "wv": "L1_gnn_Wv", "we": "L1_gnn_We", "wo": "L1_gnn_Wo",
                         "f1": "L1_gnn_W1", "f2": "L1_gnn_W2", "mw1": "L1_ffn_w1", "mw2": "L1_ffn_w2", "mb2": "L1_ffn_b2"}.items():
        out[name] = np.asarray(i[source])
    out["be"] = np.asarray(i["L1_gnn_be"]).reshape(1, DH)
    out["rt"] = np.ascontiguousarray(np.asarray(i["L1_ffn_router_w"]).T)
    return {f"in_{n}": a for n, a in out.items()}


def kernel(**inputs):
    import concourse.bacc as _bacc
    from concourse.bass_utils import run_bass_kernel_spmd as _run

    nc = _bacc.Bacc("TRN2", target_bir_lowering=False, num_devices=1)
    program(nc)
    r = _run(nc, [layout(inputs)], core_ids=[0])
    return r.results[0]["out_0"][:N]
```

```python
from contextlib import ExitStack

import concourse.bass as bass
from concourse import mybir

P = 128
N = 2500
NT = -(-N // P)
NP = NT * P
BT = 4
BLK = BT * P
NB = NP // BLK
D = 256
DK = D // P
E = 40000
G = 8
ET = -(-E // (P * G)) * G
EP = ET * P
W = 32
XS = NP // W
KS = ET + XS
ACCW = NP + W
NBASE = 4
NREL = 8
RH = 128
E0 = 6
E1 = 8
H = 8
DH = D // H
ED = 64
FF = 4 * D
FK = FF // P
EPS = 1e-5
VG = 88
BIG = 3.0e38
LINE = EP // P
N_WEIGHTS0 = 3 * E0 + 5

F32 = mybir.dt.float32
BF16 = mybir.dt.bfloat16
I32 = mybir.dt.int32
ALU = mybir.AluOpType
ACT = mybir.ActivationFunctionType
AX = mybir.AxisListType

COLS = {"bias0": 2, "rb1": 1, "eb1": 2 * E0, "eb2": 2 * E0, "ln1_g": 2, "ln1_b": 2, "ln2_g": 2, "ln2_b": 2,
        "bo": 2, "gb1": FK, "mb1": 2 * E1}
ROWS = {"rb2": E0, "qkvb": 3 * D, "b2": D, "alpha": 1, "beta": 1, "comp": NREL * NBASE}


def places(widths):
    at, out = 0, {}
    for name, w in widths.items():
        out[name] = (at, at + w)
        at += w
    return out, at


COL, NCOL = places(COLS)
ROW, NROW = places(ROWS)


class Tally:

    def __init__(self, sem, i=0, per=0, base=0):
        self.sem, self.i, self.per, self.n, self.base = sem, i, per, 0, base

    def at(self, n):
        return self.i * self.per + (self.base + n)

    def mark(self, ins):
        ins.then_inc(self.sem, 1)
        self.n += 1

    def wait(self, eng):
        eng.wait_ge(self.sem, self.at(self.n))

    def close(self):
        assert self.n == self.per, (self.n, self.per)


def settle(eng):
    eng.nop(nofuse=True)


def windows(nc, engine, g, i, first=0):
    _, at = nc.values_load_multi_w_load_instructions(
        g.win[0:1, ds(i * G + first, G)], engines=[engine], min_val=0, max_val=NP,
        skip_runtime_bounds_check_because="a window starts at an edge's node, or at NP")
    return at


def ds(a, n):
    return bass.ds(a, n)


class Mem:

    def __init__(self, nc, ctx, prefix):
        self.nc, self.ctx, self.prefix, self.cleared = nc, ctx, prefix, []

    def sb(self, name, shape, dt=F32):
        return self.ctx.enter_context(self.nc.sbuf_tensor(f"{self.prefix}_{name}", list(shape), dt))

    def ps(self, name, shape, dt=F32):
        return self.ctx.enter_context(self.nc.psum_tensor(f"{self.prefix}_{name}", list(shape), dt))

    def cleared_sem(self, name):
        self.cleared.append(self.nc.alloc_semaphore(name=f"{self.prefix}_{name}"))
        return self.cleared[-1]

    def clear(self):
        self.nc.clear_and_free_semaphores(self.cleared)

    def sem(self, name):
        return self.ctx.enter_context(self.nc.semaphore(f"{self.prefix}_{name}"))



def stage_load(nc, d, g):
    with ExitStack() as ctx:
        m = Mem(nc, ctx, "load")
        ahead = m.sb("ahead", [P, LINE + 1], I32)
        down = m.sb("down", [P, LINE])
        downs = m.sb("downs", [P, 1])
        ones = m.sb("ones", [P, 1])
        count = m.sb("count", [1, 1])
        diag = m.sb("diag", [P, P])
        psC = m.ps("psC", [P, 512])
        loaded, line_loaded, chain = m.cleared_sem("loaded"), m.cleared_sem("line_loaded"), m.cleared_sem("chain")
        diag_ready, downs_ready, counted = m.cleared_sem("diag_ready"), m.cleared_sem("downs_ready"), m.cleared_sem("counted")
        with nc.Block() as block:
            @block.sync
            def _(sp):
                sp.dma_start(ahead[:, :], d.line).then_inc(line_loaded, 16)
                for dst, src in ((g.dstI[:, :], d.dst), (g.typI[:, :], d.typ), (g.srcI[:, 0:ET], d.src),
                                 (g.ew[:, :], d.ew), (g.cols[:, :], d.cols),
                                 (g.rows[:, :], d.rows.to_broadcast([P, NROW]))):
                    sp.dma_start(dst, src).then_inc(loaded, 16)
                for b in range(NB):
                    sp.dma_start(g.x[:, b * BT:(b + 1) * BT, :],
                                 d.x[b * BLK:(b + 1) * BLK, :].rearrange("(t p) c -> p t c", p=P)).then_inc(loaded, 16)
                sp.dma_start(g.basis[:, :, :, :], d.basis.rearrange("b (k p) o -> p b k o", p=P)).then_inc(g.weights0, 16)
                sp.dma_start(g.loopw[:, :, :], d.loopw.rearrange("(k p) o -> p k o", p=P)).then_inc(g.weights0, 16)
                sp.dma_start(g.rw1[:, :, :], d.rw1.rearrange("(k p) o -> p k o", p=P)).then_inc(g.weights0, 16)
                sp.dma_start(g.rw2[:, :], d.rw2).then_inc(g.weights0, 16)
                sp.dma_start(g.b3[:, :], d.b3).then_inc(g.weights0, 16)
                for w_sb, w in ((g.w1, d.w1), (g.w2, d.w2), (g.w3, d.w3)):
                    for e in range(E0):
                        sp.dma_start(w_sb[:, e, :, :], w[e].rearrange("(k p) o -> p k o", p=P)).then_inc(g.weights0, 16)
                sp.wait_ge(line_loaded, 16)
                sp.wait_ge(loaded, 16 * (6 + NB))

            @block.gpsimd
            def _(pool):
                nc.gpsimd.iota(diag[:, :], [[-1, P]], base=0, channel_multiplier=1,
                               allow_small_or_imprecise_dtypes=True).then_inc(diag_ready, 1)

            @block.vector
            def _(dve):
                t = Tally(chain)
                nc.vector.memset(ones[:, :], 1.0)
                nc.vector.memset(g.eps[:, :], EPS)
                dve.wait_ge(diag_ready, 1)
                nc.vector.tensor_scalar(g.ident[:, :], diag[:, :], 0.0, None, ALU.is_equal)
                nc.vector.tensor_scalar(g.identb[:, :], diag[:, :], 0.0, None, ALU.is_equal)
                dve.wait_ge(line_loaded, 16)
                t.mark(nc.vector.tensor_tensor(down[:, :], ahead[:, 0:LINE], ahead[:, 1:LINE + 1], ALU.is_gt))
                t.wait(dve)
                nc.vector.tensor_reduce(downs[:, :], down[:, :], AX.X, ALU.add).then_inc(downs_ready, 1)
                dve.wait_ge(counted, 1)
                t.mark(nc.vector.tensor_copy(count[:, :], psC[0:1, 0:1]))
                t.wait(dve)
                nc.vector.tensor_scalar(g.flags[:, 0:1], count[:, :], 0.0, None, ALU.is_gt)
                nc.vector.tensor_scalar(g.flags[:, 1:2], count[:, :], 0.0, None, ALU.is_equal)

            @block.tensor
            def _(pe):
                pe.wait_ge(downs_ready, 1)
                nc.tensor.matmul(psC[0:1, 0:1], downs[:, :], ones[:, :], start=True, stop=True).then_inc(counted, 1)
        m.clear()
        nc.all_engine_barrier()



def stage_sort(nc, d, g):
    RN = 512
    with ExitStack() as ctx:
        m = Mem(nc, ctx, "sort")
        nodes = m.sb("nodes", [P, NP])
        oh = m.sb("oh", [P, NP], BF16)
        junk = m.sb("junk", [P, NP])
        base = m.sb("base", [P, NP])
        hist = m.sb("hist", [P, NP])
        onesb = m.sb("onesb", [P, P], BF16)
        below = m.sb("below", [P, P])
        same = m.sb("same", [P, P])
        wide = m.sb("wide", [P, P])
        dstF = m.sb("dstF", [P, ET])
        col = m.sb("col", [P, 1])
        part = m.sb("part", [P, 3])
        rank = m.sb("rank", [P, ET])
        place = m.sb("place", [P, 1], I32)
        rec = m.sb("rec", [P, 4 + P])
        efT = m.sb("efT", [ED, P])
        psR = m.ps("psR", [P, NP])
        psD = m.ps("psD", [P, 512])
        shapes_ready, chain, zeroed = m.cleared_sem("shapes_ready"), m.cleared_sem("chain"), m.cleared_sem("zeroed")
        wide_ready, spread, seen, counted = m.cleared_sem("wide_ready"), m.cleared_sem("spread"), m.cleared_sem("seen"), m.cleared_sem("counted")
        ef_got, rec_ready, scattered = m.cleared_sem("ef_got"), m.cleared_sem("rec_ready"), m.cleared_sem("scattered")
        chain2, chain3, back, turned, efT_ready, stored = (m.cleared_sem(n) for n in
                                                           ("chain2", "chain3", "back", "turned", "efT_ready", "stored"))
        with nc.Block() as block:
            @block.gpsimd
            def _(pool):
                with pool.If(pool.value_load(g.flags[0:1, 0:1], min_val=0, max_val=1)):
                    kw = dict(allow_small_or_imprecise_dtypes=True)
                    nc.gpsimd.iota(nodes[:, :], [[1, NP]], base=0, channel_multiplier=0, **kw)
                    nc.gpsimd.iota(below[:, :], [[-1, P]], base=0, channel_multiplier=1, **kw).then_inc(shapes_ready, 1)
                    with pool.Fori(0, ET) as t:
                        pool.wait_ge(rec_ready, t + 1)
                        settle(pool)
                        nc.gpsimd.indirect_dma_start(d.sorted[:, :], bass.IndirectOffsetOnAxis(ap=place[:, 0:1], axis=0),
                                                     rec[:, 0:4 + ED], None).then_inc(scattered, 16)
                    pool.wait_ge(scattered, 16 * ET)

            @block.sync
            def _(sp):
                with sp.If(sp.value_load(g.flags[0:1, 0:1], min_val=0, max_val=1)):
                    sp.wait_ge(zeroed, 1)
                    sp.dma_start(rec[:, 4:4 + ED], d.ef[0:P, :]).then_inc(ef_got, 16)
                    with sp.Fori(1, ET) as t:
                        sp.wait_ge(scattered, t * 16)
                        settle(sp)
                        sp.dma_start(rec[:, 4:4 + ED], d.ef[ds(t * P, P), :]).then_inc(ef_got, 16)
                    sp.wait_ge(ef_got, 16 * ET)
                    sp.wait_ge(scattered, 16 * ET)
                    with sp.Fori(0, ET) as t:
                        sp.wait_ge(chain3, t + 1)
                        settle(sp)
                        sp.dma_start(rec[:, 0:4 + ED], d.sorted[ds(t * P, P), :]).then_inc(back, 16)
                        sp.wait_ge(efT_ready, t + 1)
                        settle(sp)
                        sp.dma_start(d.efs[:, ds(t * P, P)], efT[:, :]).then_inc(stored, 16)
                    sp.wait_ge(back, 16 * ET)
                    sp.wait_ge(stored, 16 * ET)

            @block.vector
            def _(dve):
                with dve.If(dve.value_load(g.flags[0:1, 0:1], min_val=0, max_val=1)):
                    nc.vector.memset(onesb[:, :], 1.0)
                    nc.vector.memset(rec[:, :], 0.0).then_inc(zeroed, 1)
                    nc.vector.memset(hist[:, :], 0.0)
                    nc.vector.memset(g.spare[0:1, 0:1], 0.0).then_inc(chain, 1)
                    dve.wait_ge(shapes_ready, 1)
                    nc.vector.tensor_scalar(junk[:, 0:P], below[:, :], 0.0, None, ALU.is_gt).then_inc(zeroed, 1)
                    dve.wait_ge(zeroed, 2)
                    nc.vector.tensor_copy(below[:, :], junk[:, 0:P])
                    nc.vector.tensor_copy(dstF[:, :], g.dstI[:, :]).then_inc(zeroed, 1)
                    dve.wait_ge(zeroed, 3)
                    with dve.Fori(0, ET) as i:
                        t = Tally(chain, i, 5, 1)
                        t.wait(dve)
                        t.mark(nc.vector.tensor_copy(col[:, :], dstF[:, ds(i, 1)]))
                        t.wait(dve)
                        nc.vector.tensor_copy(wide[:, :], col[:, :].to_broadcast([P, P])).then_inc(wide_ready, 1)
                        t.mark(nc.vector.tensor_scalar(oh[:, :], nodes[:, :], col[:, 0:1], None, ALU.is_equal))
                        t.wait(dve)
                        nc.vector.scalar_tensor_tensor(out=junk[:, :], in0=nodes[:, :], scalar=col[:, 0:1], in1=hist[:, :],
                                                       op0=ALU.is_equal, op1=ALU.mult, accum_out=part[:, 0:1]).then_inc(seen, 1)
                        dve.wait_ge(spread, i + 1)
                        t.mark(nc.vector.scalar_tensor_tensor(out=same[:, :], in0=psD[:, 0:P], scalar=col[:, 0:1], in1=below[:, :],
                                                              op0=ALU.is_equal, op1=ALU.mult, accum_out=part[:, 1:2]))
                        t.wait(dve)
                        dve.wait_ge(seen, i + 1)
                        t.mark(nc.vector.tensor_tensor(rank[:, ds(i, 1)], part[:, 0:1], part[:, 1:2], ALU.add))
                        dve.wait_ge(counted, i + 1)
                        t.mark(nc.vector.tensor_tensor(hist[:, :], hist[:, :], psR[:, :], ALU.add))
                        t.close()
                    dve.wait_ge(chain, 5 * ET + 1)
                    t = Tally(chain2)
                    t.mark(nc.vector.memset(base[:, :], 0.0))
                    t.wait(dve)
                    t.mark(nc.vector.tensor_tensor_scan(junk[:, :], hist[:, :], base[:, :], 0.0, ALU.add, ALU.add))
                    t.wait(dve)
                    t.mark(nc.vector.tensor_tensor(base[:, :], junk[:, :], hist[:, :], ALU.subtract))
                    with dve.Fori(0, ET) as i:
                        t = Tally(chain2, i, 3, 3)
                        t.wait(dve)
                        t.mark(nc.vector.tensor_copy(col[:, :], dstF[:, ds(i, 1)]))
                        t.wait(dve)
                        t.mark(nc.vector.scalar_tensor_tensor(out=junk[:, :], in0=nodes[:, :], scalar=col[:, 0:1], in1=base[:, :],
                                                              op0=ALU.is_equal, op1=ALU.mult, accum_out=part[:, 0:1]))
                        t.wait(dve)
                        dve.wait_ge(ef_got, i * 16 + 16)
                        nc.vector.tensor_tensor(place[:, :], part[:, 0:1], rank[:, ds(i, 1)], ALU.add)
                        for c, from_ in enumerate((g.srcI, g.dstI, g.typI, g.ew)):
                            ins = nc.vector.tensor_copy(rec[:, c:c + 1], from_[:, ds(i, 1)])
                        ins.then_inc(rec_ready, 1)
                        dve.wait_ge(rec_ready, i + 1)
                        t.mark(nc.vector.tensor_copy(g.spare[0:1, 5:6], g.eps[0:1, 0:1]))
                        t.close()
                    nc.vector.memset(g.spare[0:1, 1:2], 0.0).then_inc(chain3, 1)
                    with dve.Fori(0, ET) as i:
                        dve.wait_ge(back, i * 16 + 16)
                        for c, to in enumerate((g.srcI, g.dstI, g.typI, g.ew)):
                            nc.vector.tensor_copy(to[:, ds(i, 1)], rec[:, c:c + 1])
                        dve.wait_ge(turned, i + 1)
                        nc.vector.tensor_copy(efT[:, :], psD[0:ED, 0:P]).then_inc(efT_ready, 1)
                        dve.wait_ge(stored, i * 16 + 16)
                        nc.vector.memset(g.spare[0:1, 2:3], 0.0).then_inc(chain3, 1)

            @block.tensor
            def _(pe):
                with pe.If(pe.value_load(g.flags[0:1, 0:1], min_val=0, max_val=1)):
                    pe.wait_ge(zeroed, 1)
                    with pe.Fori(0, ET) as i:
                        pe.wait_ge(wide_ready, i + 1)
                        nc.tensor.matmul(psD[:, 0:P], wide[:, :], g.ident[:, :], start=True, stop=True).then_inc(spread, 1)
                        pe.wait_ge(seen, i + 1)
                        for j in range(NP // RN):
                            ins = nc.tensor.matmul(psR[:, j * RN:(j + 1) * RN], onesb[:, :], oh[:, j * RN:(j + 1) * RN],
                                                   start=True, stop=True)
                        ins.then_inc(counted, 1)
                    with pe.Fori(0, ET) as i:
                        pe.wait_ge(back, i * 16 + 16)
                        nc.tensor.transpose(psD[:, 0:P], rec[:, 4:4 + P], g.ident[:, :]).then_inc(turned, 1)
        m.clear()
        nc.all_engine_barrier()



class Norm:

    def __init__(self, m):
        self.stat = m.sb("stat", [P, BT, 6])
        self.mv = m.sb("mv", [P, BT, 2])
        self.std = m.sb("std", [P, BT])
        self.rstd = m.sb("rstd", [P, BT])
        self.var_ready = m.sem("var_ready")
        self.std_ready = m.sem("std_ready")


def norm_dve(nc, dve, g, nm, t, i, per, k, src, dst, done=None):
    t.wait(dve)
    settle(dve)
    for q in range(BT):
        ins = nc.vector.bn_stats(nm.stat[:, q, :], src(q))
    t.mark(ins)
    t.wait(dve)
    settle(dve)
    for q in range(BT):
        ins = nc.vector.bn_aggr(nm.mv[:, q, :], nm.stat[:, q, :])
    ins.then_inc(nm.var_ready, 1)
    dve.wait_ge(nm.std_ready, i * per + k + 1)
    t.mark(nc.vector.reciprocal(nm.rstd[:, :], nm.std[:, :]))
    t.wait(dve)
    for q in range(BT):
        ins = nc.vector.tensor_scalar(dst(q), src(q), nm.mv[:, q, 0:1], nm.rstd[:, q:q + 1], ALU.subtract, ALU.mult)
    if done is None:
        t.mark(ins)
    else:
        ins.then_inc(done, 1)


def norm_act(nc, act, g, nm, i, per, k):
    act.wait_ge(nm.var_ready, i * per + k + 1)
    nc.scalar.activation(nm.std[:, :], nm.mv[:, :, 1], ACT.Sqrt, bias=g.eps[:, 0:1]).then_inc(nm.std_ready, 1)


def turn(nc, g, out, src):
    for q in range(BT):
        for k in range(DK):
            ins = nc.tensor.transpose(out[:, k, q * P:(q + 1) * P], src(q)[:, k * P:(k + 1) * P], g.ident[:, :])
    return ins


def free_at_first(nc, g, out, sem, n):
    nc.tensor.transpose(out, g.ident[0:32, 0:32], g.ident[0:32, 0:32]).then_inc(sem, n)



ON_DVE = 3


def stage_tables(nc, d, g):
    with ExitStack() as ctx:
        m = Mem(nc, ctx, "tab")
        nm = Norm(m)
        xn = m.sb("xn", [P, NT, D])
        psT = m.ps("psT", [P, DK, BLK])
        dstF = g.dstF
        typF = m.sb("typF", [P, ET])
        hit = m.sb("hit", [P, ET])
        term = m.sb("term", [P, ET, NBASE])
        pick0 = m.sb("pick0", [P, P])
        pickl = m.sb("pickl", [P, P])
        firstS = m.sb("firstS", [P, ET])
        lastS = m.sb("lastS", [P, ET])
        spanF = m.sb("spanF", [P, ET])
        spanI = m.sb("spanI", [P, ET], I32)
        moreI = m.sb("moreI", [P, ET], I32)
        more = m.sb("more", [P, ET])
        upto = m.sb("upto", [P, ET])
        past = m.sb("past", [P, ET])
        sel = m.sb("sel", [P, ET])
        pidx = m.sb("pidx", [P, 1])
        tidx = m.sb("tidx", [P, ET])
        xt = m.sb("xt", [P, 8])
        winx = m.sb("winx", [P, XS])
        psF = m.ps("psF", [P, 512])
        psL = m.ps("psL", [P, 512])
        psX = m.ps("psX", [P, 512])
        shapes_ready = m.cleared_sem("shapes_ready")
        ch = m.cleared_sem("chain")
        norm_chain = m.cleared_sem("norm_chain")
        coef_chain = m.cleared_sem("coef_chain")
        coef_ready = m.cleared_sem("coef_ready")
        xn_ready = m.cleared_sem("xn_ready")
        turned = m.cleared_sem("turned")
        xnT_ready = m.cleared_sem("xnT_ready")
        stored = m.cleared_sem("stored")
        picks_ready = m.cleared_sem("picks_ready")
        ends_ready = m.cleared_sem("ends_ready")
        extra_ready = m.cleared_sem("extra_ready")
        extra_turned = m.cleared_sem("extra_turned")
        dst_ready = m.cleared_sem("dst_ready")
        moved = m.cleared_sem("moved")
        with nc.Block() as block:
            @block.gpsimd
            def _(pool):
                kw = dict(allow_small_or_imprecise_dtypes=True)
                nc.gpsimd.iota(g.iota[:, :], [[1, W]], base=0, channel_multiplier=0, **kw)
                nc.gpsimd.iota(g.iota3[:, :], [[1, W], [0, 3]], base=0, channel_multiplier=0, **kw)
                nc.gpsimd.iota(pidx[:, :], [[0, 1]], base=0, channel_multiplier=1, **kw)
                nc.gpsimd.iota(tidx[:, :], [[1, ET]], base=0, channel_multiplier=0, **kw)
                nc.gpsimd.iota(g.rev[:, :], [[-1, E1]], base=E1, channel_multiplier=0, **kw)
                nc.gpsimd.iota(g.tile[:, 0:ET], [[1, ET]], base=0, channel_multiplier=0)
                nc.gpsimd.memset(g.srcI[:, ET:KS + G], 0).then_inc(shapes_ready, 1)
                t = Tally(coef_chain)
                nc.gpsimd.memset(g.coef[:, :, :], 0.0)
                t.mark(nc.gpsimd.tensor_copy(typF[:, :], g.typI[:, :]))
                t.wait(pool)
                for r in range(NREL - ON_DVE):
                    t.mark(nc.gpsimd.tensor_scalar(hit[:, :], typF[:, :], float(r), None, ALU.is_equal))
                    t.wait(pool)
                    c = ROW["comp"][0] + r * NBASE
                    t.mark(nc.gpsimd.tensor_tensor(term[:, :, :], hit[:, :].unsqueeze(2).to_broadcast([P, ET, NBASE]),
                                                   g.rows[:, c:c + NBASE].unsqueeze(1).to_broadcast([P, ET, NBASE]), ALU.mult))
                    t.wait(pool)
                    ins = nc.gpsimd.tensor_tensor(g.coef[:, 0:ET, :], g.coef[:, 0:ET, :], term[:, :, :], ALU.add)
                    t.mark(ins)
                    t.wait(pool)
                nc.gpsimd.memset(g.spare[0:1, 9:10], 0.0).then_inc(coef_ready, 1)

            @block.vector
            def _(dve):
                nc.vector.memset(g.spare[0:1, 1:2], 0.0).then_inc(norm_chain, 1)
                with dve.Fori(0, NB) as i:
                    t = Tally(norm_chain, i, 2, 1)
                    norm_dve(nc, dve, g, nm, t, i, 1, 0, lambda q: g.x[:, ds(i * BT + q, 1), :].rearrange("p a c -> p (a c)"),
                             lambda q: xn[:, ds(i * BT + q, 1), :].rearrange("p a c -> p (a c)"), xn_ready)
                    t.close()
                t = Tally(ch)
                nc.vector.memset(g.none[:, :], 0.0)
                t.mark(nc.vector.memset(g.dstrel[:, ET:KS + G], -1.0))
                dve.wait_ge(shapes_ready, 1)
                nc.vector.tensor_copy(pick0[:, :], g.ident[:, 0:1].to_broadcast([P, P]))
                nc.vector.tensor_copy(pickl[:, :], g.ident[:, P - 1:P].to_broadcast([P, P])).then_inc(picks_ready, 1)
                nc.vector.tensor_copy(dstF[:, :], g.dstI[:, :]).then_inc(dst_ready, 1)
                dve.wait_ge(ends_ready, 1)
                nc.vector.tensor_copy(firstS[:, :], psF[:, 0:ET])
                nc.vector.tensor_copy(g.win[:, 0:ET], psF[0:1, 0:ET])
                t.mark(nc.vector.tensor_copy(lastS[:, :], psL[:, 0:ET]))
                t.wait(dve)
                nc.vector.tensor_tensor(g.dstrel[:, 0:ET], dstF[:, :], firstS[:, :], ALU.subtract)
                t.mark(nc.vector.tensor_tensor(spanI[:, :], lastS[:, :], firstS[:, :], ALU.subtract))
                t.wait(dve)
                t.mark(nc.vector.tensor_scalar(moreI[:, :], spanI[:, :], 5, None, ALU.arith_shift_right))
                t.wait(dve)
                t.mark(nc.vector.tensor_scalar(more[:, :], moreI[:, :], 0.0, None, ALU.max))
                t.wait(dve)
                nc.vector.memset(past[:, :], 0.0)
                t.mark(nc.vector.memset(xt[:, :], 0.0))
                t.wait(dve)
                t.mark(nc.vector.tensor_tensor_scan(upto[:, :], more[:, :], past[:, :], 0.0, ALU.add, ALU.add))
                t.wait(dve)
                t.mark(nc.vector.tensor_scalar(past[:, :], upto[:, :], pidx[:, 0:1], None, ALU.is_le))
                t.wait(dve)
                nc.vector.tensor_reduce(xt[:, 0:1], past[:, :], AX.X, ALU.add)
                t.mark(nc.vector.tensor_tensor(sel[:, :], past[:, :], more[:, :], ALU.mult))
                t.wait(dve)
                nc.vector.tensor_reduce(xt[:, 1:2], sel[:, :], AX.X, ALU.add)
                t.mark(nc.vector.tensor_scalar(spanF[:, :], tidx[:, :], xt[:, 0:1], None, ALU.is_equal))
                t.wait(dve)
                t.mark(nc.vector.tensor_tensor(sel[:, :], spanF[:, :], firstS[:, :], ALU.mult))
                t.wait(dve)
                t.mark(nc.vector.tensor_reduce(xt[:, 2:3], sel[:, :], AX.X, ALU.add))
                t.wait(dve)
                t.mark(nc.vector.tensor_scalar(xt[:, 3:4], pidx[:, :], xt[:, 1:2], 1.0, ALU.subtract, ALU.add))
                t.wait(dve)
                t.mark(nc.vector.tensor_scalar(xt[:, 3:4], xt[:, 3:4], float(W), xt[:, 2:3], ALU.mult, ALU.add))
                t.wait(dve)
                t.mark(nc.vector.tensor_scalar(xt[:, 4:5], xt[:, 0:1], float(ET), None, ALU.is_ge))
                t.wait(dve)
                t.mark(nc.vector.tensor_scalar(xt[:, 5:6], xt[:, 4:5], float(2 * NP), xt[:, 3:4], ALU.mult, ALU.add))
                t.wait(dve)
                nc.vector.tensor_scalar(xt[:, 6:7], xt[:, 5:6], float(NP), None, ALU.min)
                t.mark(nc.vector.tensor_scalar(xt[:, 7:8], xt[:, 0:1], float(ET - 1), None, ALU.min))
                t.wait(dve)
                nc.vector.tensor_copy(pick0[:, :], xt[:, 6:7].to_broadcast([P, P]))
                nc.vector.tensor_copy(pickl[:, :], xt[:, 7:8].to_broadcast([P, P])).then_inc(extra_ready, 1)
                dve.wait_ge(extra_turned, 1)
                nc.vector.tensor_copy(winx[:, :], psX[:, 0:XS])
                nc.vector.tensor_copy(g.win[:, ET:KS], psX[0:1, 0:XS])
                nc.vector.tensor_copy(g.tile[:, ET:KS], psX[0:1, P:P + XS])
                t.mark(nc.vector.tensor_copy(g.over[:, :], upto[0:1, ET - 1:ET]))
                t.wait(dve)
                over = dve.value_load(g.over[0:1, 0:1], min_val=0, max_val=2 * NP)
                dve.wait_ge(coef_ready, 1)
                for r in range(NREL - ON_DVE, NREL):
                    t.mark(nc.vector.tensor_scalar(hit[:, :], typF[:, :], float(r), None, ALU.is_equal))
                    t.wait(dve)
                    for b in range(NBASE):
                        c = ROW["comp"][0] + r * NBASE + b
                        ins = nc.vector.scalar_tensor_tensor(out=g.coef[:, 0:ET, b], in0=hit[:, :], scalar=g.rows[:, c:c + 1],
                                                             in1=g.coef[:, 0:ET, b], op0=ALU.mult, op1=ALU.add)
                    t.mark(ins)
                    t.wait(dve)
                with dve.If(over):
                    with dve.Fori(0, XS) as k:
                        tl = dve.value_load(g.tile[0:1, ds(k + ET, 1)], min_val=0, max_val=ET - 1)
                        nc.vector.tensor_tensor(g.dstrel[:, ds(k + ET, 1)], dstF[:, ds(tl, 1)], winx[:, ds(k, 1)], ALU.subtract)
                        nc.vector.tensor_copy(g.coef[:, ds(k + ET, 1), :], g.coef[:, ds(tl, 1), :])
                        nc.vector.tensor_copy(g.srcI[:, ds(k + ET, 1)], g.srcI[:, ds(tl, 1)]).then_inc(moved, 1)
                    dve.wait_ge(moved, XS)

            @block.tensor
            def _(pe):
                free_at_first(nc, g, psT[0:32, 0, 0:32], turned, 1)
                for i in range(NB):
                    pe.wait_ge(xn_ready, i + 1)
                    pe.wait_ge(xnT_ready, i + 1)
                    turn(nc, g, psT, lambda q: xn[:, i * BT + q, :]).then_inc(turned, 1)
                pe.wait_ge(picks_ready, 1)
                pe.wait_ge(dst_ready, 1)
                nc.tensor.matmul(psF[:, 0:ET], pick0[:, :], dstF[:, :], start=True, stop=True)
                nc.tensor.matmul(psL[:, 0:ET], pickl[:, :], dstF[:, :], start=True, stop=True).then_inc(ends_ready, 1)
                pe.wait_ge(extra_ready, 1)
                nc.tensor.matmul(psX[:, 0:P], pick0[:, :], g.ident[:, :], start=True, stop=True)
                nc.tensor.matmul(psX[:, P:2 * P], pickl[:, :], g.ident[:, :], start=True, stop=True).then_inc(extra_turned, 1)

            @block.scalar
            def _(act):
                nc.scalar.copy(g.spare[0:1, 12:13], g.eps[0:1, 0:1]).then_inc(xnT_ready, 1)
                with act.Fori(0, NB) as i:
                    norm_act(nc, act, g, nm, i, 1, 0)
                    act.wait_ge(turned, i + 2)
                    nc.scalar.copy(g.xnT[:, :, ds(i * BLK, BLK)], psT[:, :, :]).then_inc(xnT_ready, 1)

            @block.sync
            def _(sp):
                with sp.Fori(0, NB) as i:
                    sp.wait_ge(xn_ready, i + 1)
                    sp.dma_start(d.xn[ds(i * BLK, BLK), :].rearrange("(t p) c -> p t c", p=P),
                                 xn[:, ds(i * BT, BT), :]).then_inc(stored, 16)
                sp.wait_ge(stored, 16 * NB)
        m.clear()
        nc.all_engine_barrier()



def index_copies(nc, act, g, ixs, got, copied, i, slots=range(G)):
    for b in slots:
        act.wait_ge(got[b], i * 16 + 16)
        settle(act)
        nc.scalar.copy(ixs[:, b:b + 1], g.srcI[:, ds(i * G + (G + b), 1)]).then_inc(copied, 1)


def first_indices(nc, g, ixs, copied):
    for b in range(G):
        nc.scalar.copy(ixs[:, b:b + 1], g.srcI[:, b:b + 1]).then_inc(copied, 1)


def gathers(nc, pool, g, ring, ixs, table, got, copied, free, per, i):
    for b in range(G):
        pool.wait_ge(copied, i * G + (b + 1))
        pool.wait_ge(free, i * (G // per) + (b // per + 1))
        settle(pool)
        nc.gpsimd.indirect_dma_start(ring[:, b, :], None, table[:, :],
                                     bass.IndirectOffsetOnAxis(ap=ixs[:, b:b + 1], axis=0)).then_inc(got[b], 16)


def edge_loops(nc, eng, g, body):
    with eng.Fori(0, ET // G) as i:
        body(i)
    over = eng.value_load(g.over[0:1, 0:1], min_val=0, max_val=2 * NP)
    with eng.If(over):
        with eng.Fori(ET // G, KS // G) as i:
            body(i)


def stage_gather0(nc, d, g):
    with ExitStack() as ctx:
        m = Mem(nc, ctx, "ga0")
        ixs = m.sb("ixs", [P, G], I32)
        xg = m.sb("xg", [P, G, D])
        oh = m.sb("oh", [P, 2, 4, W])
        M = m.sb("M", [P, 2, 4, NBASE, W])
        psZ = m.ps("psZ", [P, 4, 512])
        got = [m.sem(f"got{b}") for b in range(G)]
        copied = m.sem("copied")
        oh_ready = m.sem("oh_ready")
        M_ready = m.sem("M_ready")
        z_ready = m.sem("z_ready")
        z_added = m.sem("z_added")
        cleared = m.sem("cleared")
        cleared1 = m.sem("cleared1")
        zero_ready = m.sem("zero_ready")
        zero = m.sb("zero", [P, NBASE])
        with nc.Block() as block:
            @block.scalar
            def _(act):
                first_indices(nc, g, ixs, copied)
                act.wait_ge(zero_ready, 1)
                nc.scalar.copy(g.ZT[:, 1, :, :], zero[:, :].unsqueeze(2).to_broadcast([P, NBASE, ACCW])).then_inc(cleared1, 1)
                edge_loops(nc, act, g, lambda i: index_copies(nc, act, g, ixs, got, copied, i))

            @block.gpsimd
            def _(pool):
                edge_loops(nc, pool, g, lambda i: gathers(nc, pool, g, xg, ixs, d.xn, got, copied, z_ready, 1, i))

            @block.vector
            def _(dve):
                nc.vector.memset(zero[:, :], 0.0).then_inc(zero_ready, 1)
                nc.vector.memset(g.spare[0:1, 0:1], 0.0).then_inc(z_added, 4)

                def build(i, h):
                    dve.wait_ge(z_ready, i * G + 4 * (h + 1))
                    at = ds(i * G + 4 * h, 4)
                    nc.vector.tensor_tensor(oh[:, h, :, :], g.iota[:, :].unsqueeze(1).to_broadcast([P, 4, W]),
                                            g.dstrel[:, at].unsqueeze(2).to_broadcast([P, 4, W]),
                                            ALU.is_equal).then_inc(oh_ready, 1)
                    dve.wait_ge(oh_ready, i * 2 + (h + 1))
                    nc.vector.tensor_tensor(M[:, h, :, :, :],
                                            oh[:, h, :, :].unsqueeze(2).to_broadcast([P, 4, NBASE, W]),
                                            g.coef[:, at, :].unsqueeze(3).to_broadcast([P, 4, NBASE, W]),
                                            ALU.mult).then_inc(M_ready, 1)

                def body(i):
                    at = windows(nc, mybir.EngineType.DVE, g, i)
                    for b in range(G):
                        dve.wait_ge(z_ready, i * G + (G + b + 1))
                        dve.wait_ge(z_added, i * G + (b + 4))
                        z = g.ZT[:, :, :, ds(at[b], W)]
                        nc.vector.tensor_tensor(z, psZ[:, b % 4, 0:DK * NBASE * W].rearrange("p (k b w) -> p k b w", k=DK, b=NBASE),
                                                z, ALU.add).then_inc(z_added, 1)
                        if b % 4 == 3:
                            build(i + 1, b // 4)

                for h in range(2):
                    build(0, h)
                nc.vector.memset(g.ZT[:, 0, :, :], 0.0).then_inc(cleared, 1)
                dve.wait_ge(cleared, 1)
                dve.wait_ge(cleared1, 1)
                edge_loops(nc, dve, g, body)

            @block.tensor
            def _(pe):
                free_at_first(nc, g, psZ[0:32, 0, 0:32], z_ready, G)

                def body(i):
                    for h in range(2):
                        pe.wait_ge(M_ready, i * 2 + (h + 1))
                        for j in range(4):
                            b = 4 * h + j
                            pe.wait_ge(got[b], i * 16 + 16)
                            pe.wait_ge(z_added, i * G + (b + 1))
                            for k in range(DK):
                                ins = nc.tensor.matmul(psZ[:, j, k * NBASE * W:(k + 1) * NBASE * W],
                                                       xg[:, b, k * P:(k + 1) * P],
                                                       M[:, h, j, :, :].rearrange("p b w -> p (b w)"), start=True, stop=True)
                            ins.then_inc(z_ready, 1)

                edge_loops(nc, pe, g, body)




def stage_bases(nc, d, g):
    with ExitStack() as ctx:
        m = Mem(nc, ctx, "bas")
        aT = m.sb("aT", [P, DK, BLK])
        psA = m.ps("psA", [P, DK, BLK])
        psB = m.ps("psB", [P, BT, D])
        sums_ready = m.sem("sums_ready")
        aT_ready = m.sem("aT_ready")
        turned = m.sem("turned")
        added = m.sem("added")
        with nc.Block() as block:
            @block.tensor
            def _(pe):
                pe.wait_ge(g.weights0, 16 * N_WEIGHTS0)
                free_at_first(nc, g, psA[0:32, 0, 0:32], turned, 1)
                with pe.Fori(0, NB) as i:
                    pe.wait_ge(turned, i + 1)
                    for o in range(DK):
                        for k in range(DK):
                            nc.tensor.matmul(psA[:, o, :], g.loopw[:, k, o * P:(o + 1) * P], g.xnT[:, k, ds(i * BLK, BLK)],
                                             start=(k == 0), stop=False)
                        for b in range(NBASE):
                            for k in range(DK):
                                ins = nc.tensor.matmul(psA[:, o, :], g.basis[:, b, k, o * P:(o + 1) * P],
                                                       g.ZT[:, k, b, ds(i * BLK, BLK)],
                                                       start=False, stop=(b == NBASE - 1 and k == DK - 1))
                        ins.then_inc(sums_ready, 1)
                    pe.wait_ge(aT_ready, i * 2 + 2)
                    pe.wait_ge(added, i + 1)
                    for q in range(BT):
                        for k in range(DK):
                            ins = nc.tensor.transpose(psB[:, q, k * P:(k + 1) * P], aT[:, k, q * P:(q + 1) * P], g.ident[:, :])
                    ins.then_inc(turned, 1)

            @block.scalar
            def _(act):
                with act.Fori(0, NB) as i:
                    for o in range(DK):
                        act.wait_ge(sums_ready, i * 2 + (o + 1))
                        act.wait_ge(turned, i + 1)
                        nc.scalar.activation(aT[:, o, :], psA[:, o, :], ACT.Identity, bias=vec(g, "bias0", o)).then_inc(aT_ready, 1)

            @block.vector
            def _(dve):
                nc.vector.memset(g.spare[0:1, 2:3], 0.0).then_inc(added, 1)
                with dve.Fori(0, NB) as i:
                    dve.wait_ge(turned, i + 2)
                    xb = g.x[:, ds(i * BT, BT), :]
                    nc.vector.tensor_tensor(xb, psB[:, :, :], xb, ALU.add).then_inc(added, 1)



def gates_dve(nc, dve, g, r, t, i, n, psL, bias, last):
    def red(out, op):
        t.mark(nc.vector.tensor_reduce(out, r.p[:, :, 0:n], AX.X, op))
        t.wait(dve)

    def spread(v):
        return v.unsqueeze(2).to_broadcast([P, BT, n])

    if bias is None:
        t.mark(nc.vector.tensor_copy(r.p[:, :, :], psL))
    else:
        t.mark(nc.vector.tensor_tensor(r.p[:, :, :], psL, bias.unsqueeze(1).to_broadcast([P, BT, n]), ALU.add))
    t.wait(dve)
    red(r.m[:, :, 0], ALU.max)
    nc.vector.tensor_tensor(r.p[:, :, :], r.p[:, :, :], spread(r.m[:, :, 0]), ALU.subtract).then_inc(r.shifted, 1)
    dve.wait_ge(r.p_ready, last * i + 1)
    red(r.m[:, :, 0], ALU.add)
    t.mark(nc.vector.reciprocal(r.m[:, :, 1], r.m[:, :, 0]))
    t.wait(dve)
    t.mark(nc.vector.tensor_tensor(r.p[:, :, :], r.p[:, :, :], spread(r.m[:, :, 1]), ALU.mult))
    t.wait(dve)
    for j in range(2):
        red(r.m[:, :, j], ALU.max)
        t.mark(nc.vector.tensor_tensor(r.k[:, j, :, :], r.p[:, :, :], spread(r.m[:, :, j]), ALU.is_equal))
        t.wait(dve)
        t.mark(nc.vector.tensor_tensor(r.k[:, j, :, :], r.k[:, j, :, :], g.rev[:, 0:n].unsqueeze(1).to_broadcast([P, BT, n]), ALU.mult))
        t.wait(dve)
        t.mark(nc.vector.tensor_reduce(r.m[:, :, 2], r.k[:, j, :, :], AX.X, ALU.max))
        t.wait(dve)
        t.mark(nc.vector.tensor_tensor(r.k[:, j, :, :], r.k[:, j, :, :], spread(r.m[:, :, 2]), ALU.is_equal))
        t.wait(dve)
        if j == 0:
            t.mark(nc.vector.scalar_tensor_tensor(out=r.p[:, :, :], in0=r.k[:, 0, :, :], scalar=-2.0, in1=r.p[:, :, :],
                                                  op0=ALU.mult, op1=ALU.add))
            t.wait(dve)


def mix_dve(nc, dve, r, t, n, g1, g2, done):
    def spread(v):
        return v.unsqueeze(2).to_broadcast([P, BT, n])
    nc.vector.tensor_tensor(r.k[:, 0, :, :], r.k[:, 0, :, :], spread(g1), ALU.mult)
    t.mark(nc.vector.tensor_tensor(r.k[:, 1, :, :], r.k[:, 1, :, :], spread(g2), ALU.mult))
    t.wait(dve)
    nc.vector.tensor_tensor(r.gate[:, :, :], r.k[:, 0, :, :], r.k[:, 1, :, :], ALU.add).then_inc(done, 1)


class Router:
    def __init__(self, m, n):
        self.p = m.sb("r_p", [P, BT, n])
        self.m = m.sb("r_m", [P, BT, 4])
        self.k = m.sb("r_k", [P, 2, BT, n])
        self.gate = m.sb("gate", [P, BT, n])
        self.gateT = m.sb("gateT", [n, BLK])
        self.shifted = m.sem("shifted")
        self.p_ready = m.sem("p_ready")


def vec(g, name, k=0):
    c = COL[name][0] + k
    return g.cols[:, c:c + 1]


def row(g, name):
    return g.rows[:, ROW[name][0]:ROW[name][1]]


ORDER0 = (("A", 0), ("logits", 0), ("A", 1), ("B", 0), ("A", 2), ("B", 1), ("mix", 0), ("C", 0), ("A", 3), ("B", 2), ("C", 1),
          ("turn2", 0), ("A", 4), ("B", 3), ("q", 0), ("C", 2), ("q", 1), ("A", 5), ("B", 4), ("q", 2), ("C", 3), ("q", 3),
          ("B", 5), ("C", 4), ("turn", 0), ("C", 5))


def block_loop(eng, body, after):
    body(0, False, True)
    with eng.Fori(1, NB - 1) as i:
        body(i, True, True)
    body(NB - 1, True, False)
    after(NB)


def stage_experts0(nc, d, g):
    with ExitStack() as ctx:
        m = Mem(nc, ctx, "ex0")
        mp = Mem(nc, ctx, "ex0p")
        nm = Norm(m)
        post_norm = Norm(mp)
        r = Router(m, E0)
        xn = m.sb("xn", [P, BT, D])
        g.wqkv = m.sb("wqkv", [P, DK, 3 * D])
        xn2 = m.sb("xn2", [P, BT, D])
        xT = m.sb("xT", [P, DK, BLK])
        x2T = m.sb("x2T", [P, DK, BLK])
        rhT = m.sb("rhT", [P, BLK])
        h1 = m.sb("h1", [P, 2, DK, BLK])
        h2 = m.sb("h2", [P, 2, DK, BLK])
        acc = m.sb("acc", [P, BT, D])
        qkv = m.sb("qkv", [P, BT, 3 * D])
        q3 = m.sb("q3", [P, BT, 3, D], BF16)
        rest = m.sb("rest", [P, BT, D])
        psW = m.ps("psW", [P, 2, 512])
        psA = m.ps("psA", [P, 2, 512])
        psB = m.ps("psB", [P, 2, 512])
        psC = m.ps("psC", [P, BT, D])
        names = ("norm_chain", "gate_chain", "post_chain", "xn_ready", "xn2_ready", "turned", "turned2", "xT_ready", "x2T_ready",
                 "hidden", "rhT_ready", "logits", "gate_ready", "gate_turned", "gateT_ready", "bias_mixed", "acc_ready",
                 "acc_free", "a_ready", "h1_ready", "b_ready", "h2_ready", "c_ready", "c_used", "qkv_made", "qkv_ready",
                 "part_made", "q3_ready", "stored")
        s = Names()
        (s.norm_chain, s.gate_chain, s.post_chain, s.xn_ready, s.xn2_ready, s.turned, s.turned2, s.xT_ready, s.x2T_ready,
         s.hidden, s.rhT_ready, s.logits, s.gate_ready, s.gate_turned, s.gateT_ready, s.bias_mixed, s.acc_ready,
         s.acc_free, s.a_ready, s.h1_ready, s.b_ready, s.h2_ready, s.c_ready, s.c_used, s.qkv_made, s.qkv_ready,
         s.part_made, s.q3_ready, s.stored) = (m.sem(n) for n in names)
        sums = psW[:, :, :].rearrange("p a c -> p (a c)").rearrange("p (t c) -> p t c", t=BT)
        with nc.Block() as block:
            @block.vector
            def _(dve):
                nc.vector.memset(g.spare[0:1, 1:2], 0.0).then_inc(s.c_used, BT)
                nc.vector.memset(g.spare[0:1, 3:4], 0.0).then_inc(s.norm_chain, 1)
                nc.vector.memset(g.spare[0:1, 4:5], 0.0).then_inc(s.gate_chain, 1)
                nc.vector.memset(g.spare[0:1, 5:6], 0.0).then_inc(s.post_chain, 1)
                dve.wait_ge(g.weights0, 16 * N_WEIGHTS0)

                def norm(i):
                    t = Tally(s.norm_chain, i, 2, 1)
                    norm_dve(nc, dve, g, nm, t, i, 1, 0, lambda q: g.x[:, ds(i * BT + q, 1), :].rearrange("p a c -> p (a c)"),
                             lambda q: xn[:, q, :], s.xn_ready)
                    t.close()

                def gates(i):
                    t = Tally(s.gate_chain, i, 20, 1)
                    t.wait(dve)
                    dve.wait_ge(s.logits, i + 1)
                    gates_dve(nc, dve, g, r, t, i, E0, psW[:, 1, 0:BT * E0].rearrange("p (t e) -> p t e", t=BT), row(g, "rb2"), 2)
                    nc.vector.tensor_tensor(r.m[:, :, 2], r.m[:, :, 1], r.m[:, :, 0], ALU.subtract).then_inc(r.shifted, 1)
                    dve.wait_ge(r.p_ready, i * 2 + 2)
                    t.mark(nc.vector.tensor_scalar(r.m[:, :, 2], r.m[:, :, 3], 1.0, None, ALU.add))
                    t.wait(dve)
                    t.mark(nc.vector.reciprocal(r.m[:, :, 0], r.m[:, :, 2]))
                    t.wait(dve)
                    t.mark(nc.vector.tensor_tensor(r.m[:, :, 1], r.m[:, :, 3], r.m[:, :, 0], ALU.mult))
                    t.wait(dve)
                    mix_dve(nc, dve, r, t, E0, r.m[:, :, 0], r.m[:, :, 1], s.gate_ready)
                    dve.wait_ge(s.gate_ready, i + 1)
                    t.close()

                def add_x(j):
                    dve.wait_ge(s.c_used, j * (E0 * BT) + (E0 * BT + BT))
                    xb = g.x[:, ds(j * BT, BT), :]
                    nc.vector.tensor_tensor(xb, xb, acc[:, :, :], ALU.add).then_inc(s.acc_free, 1)

                def post(j):
                    dve.wait_ge(s.acc_free, j + 1)
                    t = Tally(s.post_chain, j, 5, 1)
                    ub = lambda q: g.u[:, ds(j * BT + q, 1), :].rearrange("p a c -> p (a c)")
                    norm_dve(nc, dve, g, post_norm, t, j, 2, 0, lambda q: g.x[:, ds(j * BT + q, 1), :].rearrange("p a c -> p (a c)"), ub)
                    norm_dve(nc, dve, g, post_norm, t, j, 2, 1, ub, lambda q: xn2[:, q, :], s.xn2_ready)
                    t.close()

                def sum_expert(i, e):
                    if e == 0:
                        dve.wait_ge(s.acc_ready, i + 1)
                    for q in range(BT):
                        if q % 2 == 0:
                            dve.wait_ge(s.c_ready, i * (E0 * BT) + (e * BT + q + 2))
                        dve.wait_ge(s.c_used, i * (E0 * BT) + (e * BT + q + 1))
                        nc.vector.scalar_tensor_tensor(out=acc[:, q, :], in0=psC[:, q, :], scalar=r.gate[:, q, e:e + 1],
                                                       in1=acc[:, q, :], op0=ALU.mult, op1=ALU.add).then_inc(s.c_used, 1)

                def take_qkv(j, q, banks=psW):
                    if q == 0:
                        dve.wait_ge(s.stored, j * 48 + 16)
                    dve.wait_ge(s.qkv_made, j * BT + (q + 1))
                    nc.vector.tensor_tensor(qkv[:, q, :], banks[:, :, :].rearrange("p a c -> p (a c)")[:, 0:3 * D],
                                            row(g, "qkvb"), ALU.add).then_inc(s.qkv_ready, 1)

                norm(0)

                def body(i, prev, next_):
                    gates(i)
                    if prev:
                        add_x(i - 1)
                    sum_expert(i, 0)
                    if prev:
                        post(i - 1)
                    sum_expert(i, 1)
                    if prev:
                        take_qkv(i - 1, 0)
                    sum_expert(i, 2)
                    if prev:
                        take_qkv(i - 1, 1)
                        take_qkv(i - 1, 2)
                    sum_expert(i, 3)
                    if prev:
                        take_qkv(i - 1, 3)
                    if next_:
                        norm(i + 1)
                    sum_expert(i, 4)
                    sum_expert(i, 5)

                def after(i):
                    add_x(i - 1)
                    post(i - 1)
                    for q in range(BT):
                        take_qkv(i - 1, q, (psA, psB)[q % 2])

                block_loop(dve, body, after)

            @block.scalar
            def _(act):
                def take_turned(i):
                    act.wait_ge(s.turned, i + 1)
                    nc.scalar.copy(xT[:, :, :], psW[:, :, :]).then_inc(s.xT_ready, 1)

                def take_turned2(j):
                    act.wait_ge(s.turned2, j + 1)
                    for k in range(DK):
                        ins = nc.scalar.activation(x2T[:, k, :], psW[:, k, :], ACT.Identity, bias=vec(g, "ln1_b", k),
                                                   scale=vec(g, "ln1_g", k))
                    ins.then_inc(s.x2T_ready, 1)

                norm_act(nc, act, g, nm, 0, 1, 0)
                take_turned(0)

                def body(i, prev, next_):
                    act.wait_ge(s.hidden, i + 1)
                    nc.scalar.activation(rhT[:, :], psW[:, 0, :], ACT.Relu, bias=vec(g, "rb1")).then_inc(s.rhT_ready, 1)
                    for what, e in ORDER0:
                        if what in ("A", "B"):
                            for o in range(DK):
                                src, ready, h, done, b = (psA, s.a_ready, h1, s.h1_ready, "eb1") if what == "A" else \
                                                         (psB, s.b_ready, h2, s.h2_ready, "eb2")
                                act.wait_ge(ready, i * (2 * E0) + (2 * e + o + 1))
                                nc.scalar.activation(h[:, e % 2, o, :], src[:, o, :], ACT.Relu, bias=vec(g, b, 2 * e + o)).then_inc(done, 1)
                        if (what, e) == ("A", 1):
                            act.wait_ge(r.shifted, i * 2 + 1)
                            nc.scalar.activation(r.p[:, :, :], r.p[:, :, :], ACT.Exp).then_inc(r.p_ready, 1)
                        if (what, e) == ("B", 0):
                            act.wait_ge(r.shifted, i * 2 + 2)
                            nc.scalar.activation(r.m[:, :, 3], r.m[:, :, 2], ACT.Exp).then_inc(r.p_ready, 1)
                        if what == "mix":
                            act.wait_ge(s.gate_turned, i + 1)
                            nc.scalar.copy(r.gateT[:, :], psC[0:E0, 0:2, :].rearrange("p a c -> p (a c)")).then_inc(s.gateT_ready, 1)
                            act.wait_ge(s.bias_mixed, i + 1)
                            if prev:
                                act.wait_ge(s.acc_free, i)
                            nc.scalar.copy(acc[:, :, :], sums).then_inc(s.acc_ready, 1)
                        if prev and (what, e) in (("A", 3), ("B", 2)):
                            norm_act(nc, act, g, post_norm, i - 1, 2, int(what == "B"))
                        if prev and what == "turn2":
                            take_turned2(i - 1)
                        if next_ and (what, e) == ("B", 5):
                            norm_act(nc, act, g, nm, i + 1, 1, 0)
                        if next_ and what == "turn":
                            take_turned(i + 1)

                def after(i):
                    norm_act(nc, act, g, post_norm, i - 1, 2, 0)
                    norm_act(nc, act, g, post_norm, i - 1, 2, 1)
                    take_turned2(i - 1)

                block_loop(act, body, after)

            @block.gpsimd
            def _(pool):
                with pool.Fori(0, NB) as i:
                    for q in range(BT):
                        pool.wait_ge(s.qkv_ready, i * BT + (q + 1))
                        if q == 0:
                            pool.wait_ge(s.stored, i * 48 + 16)
                        settle(pool)
                        nc.gpsimd.tensor_copy(q3[:, q, 0, :], qkv[:, q, 0:D]).then_inc(s.part_made, 1)
                        pool.wait_ge(s.part_made, i * (3 * BT) + (3 * q + 1))
                        nc.gpsimd.tensor_tensor(rest[:, q, :], qkv[:, q, 0:D], q3[:, q, 0, :], ALU.subtract).then_inc(s.part_made, 1)
                        pool.wait_ge(s.part_made, i * (3 * BT) + (3 * q + 2))
                        settle(pool)
                        nc.gpsimd.tensor_copy(q3[:, q, 1, :], rest[:, q, :]).then_inc(s.part_made, 1)
                        pool.wait_ge(s.part_made, i * (3 * BT) + (3 * q + 3))
                        nc.gpsimd.tensor_tensor(q3[:, q, 2, :], rest[:, q, :], q3[:, q, 1, :], ALU.subtract).then_inc(s.q3_ready, 1)

            @block.tensor
            def _(pe):
                pe.wait_ge(g.weights0, 16 * N_WEIGHTS0)
                pe.wait_ge(g.qkv_loaded, 48)

                def project(j, q, banks=psW, ahead=0):
                    if q == 0:
                        pe.wait_ge(s.x2T_ready, j + 1)
                    elif q > ahead:
                        pe.wait_ge(s.qkv_ready, j * BT + (q - ahead))
                    for o, (a, b) in enumerate(((0, 512), (512, 768))):
                        for k in range(DK):
                            ins = nc.tensor.matmul(banks[:, o, 0:b - a], x2T[:, k, q * P:(q + 1) * P], g.wqkv[:, k, a:b],
                                                   start=(k == 0), stop=(k == DK - 1))
                    ins.then_inc(s.qkv_made, 1)

                def turn2(j):
                    pe.wait_ge(s.xn2_ready, j + 1)
                    turn(nc, g, psW, lambda q: xn2[:, q, :]).then_inc(s.turned2, 1)

                pe.wait_ge(s.xn_ready, 1)
                turn(nc, g, psW, lambda q: xn[:, q, :]).then_inc(s.turned, 1)

                def body(i, prev, next_):
                    pe.wait_ge(s.xT_ready, i + 1)
                    for k in range(DK):
                        ins = nc.tensor.matmul(psW[:, 0, :], g.rw1[:, k, :], xT[:, k, :], start=(k == 0), stop=(k == DK - 1))
                    ins.then_inc(s.hidden, 1)
                    for what, e in ORDER0:
                        if what == "A":
                            if e >= 1:
                                pe.wait_ge(s.h1_ready, i * (2 * E0) + 2 * e)
                            for o in range(DK):
                                for k in range(DK):
                                    ins = nc.tensor.matmul(psA[:, o, :], g.w1[:, e, k, o * P:(o + 1) * P], xT[:, k, :],
                                                           start=(k == 0), stop=(k == DK - 1))
                                ins.then_inc(s.a_ready, 1)
                        if what == "B":
                            pe.wait_ge(s.h1_ready, i * (2 * E0) + (2 * e + 2))
                            if e >= 1:
                                pe.wait_ge(s.h2_ready, i * (2 * E0) + 2 * e)
                            for o in range(DK):
                                for k in range(DK):
                                    ins = nc.tensor.matmul(psB[:, o, :], g.w2[:, e, k, o * P:(o + 1) * P], h1[:, e % 2, k, :],
                                                           start=(k == 0), stop=(k == DK - 1))
                                ins.then_inc(s.b_ready, 1)
                        if what == "C":
                            pe.wait_ge(s.h2_ready, i * (2 * E0) + (2 * e + 2))
                            for q in range(BT):
                                if q % 2 == 0:
                                    pe.wait_ge(s.c_used, i * (E0 * BT) + (e * BT + q + 2))
                                for k in range(DK):
                                    ins = nc.tensor.matmul(psC[:, q, :], h2[:, e % 2, k, q * P:(q + 1) * P], g.w3[:, e, k, :],
                                                           start=(k == 0), stop=(k == DK - 1))
                                ins.then_inc(s.c_ready, 1)
                        if what == "logits":
                            pe.wait_ge(s.rhT_ready, i + 1)
                            for q in range(BT):
                                ins = nc.tensor.matmul(psW[:, 1, q * E0:(q + 1) * E0], rhT[:, q * P:(q + 1) * P], g.rw2[:, :],
                                                       start=True, stop=True)
                            ins.then_inc(s.logits, 1)
                        if what == "mix":
                            pe.wait_ge(s.gate_ready, i + 1)
                            pe.wait_ge(s.c_used, i * (E0 * BT) + BT)
                            for q in range(BT):
                                ins = nc.tensor.transpose(psC[0:E0, 0:2, :].rearrange("p a c -> p (a c)")[:, q * P:(q + 1) * P],
                                                          r.gate[:, q, :], g.ident[:, :])
                            ins.then_inc(s.gate_turned, 1)
                            pe.wait_ge(s.gateT_ready, i + 1)
                            for q in range(BT):
                                ins = nc.tensor.matmul(psW[:, q // 2, (q % 2) * D:(q % 2 + 1) * D], r.gateT[:, q * P:(q + 1) * P],
                                                       g.b3[:, :], start=True, stop=True)
                            ins.then_inc(s.bias_mixed, 1)
                        if prev and what == "turn2":
                            pe.wait_ge(s.acc_ready, i + 1)
                            turn2(i - 1)
                        if prev and what == "q":
                            project(i - 1, e)
                        if next_ and what == "turn":
                            if prev:
                                pe.wait_ge(s.qkv_ready, i * BT)
                            else:
                                pe.wait_ge(s.acc_ready, i + 1)
                            pe.wait_ge(s.xn_ready, i + 2)
                            turn(nc, g, psW, lambda q: xn[:, q, :]).then_inc(s.turned, 1)

                def after(i):
                    turn2(i - 1)
                    for q in range(BT):
                        project(i - 1, q, (psA, psB)[q % 2], 1)

                block_loop(pe, body, after)

            @block.sync
            def _(sp):
                load_later(sp, d, g, s.stored)
                with sp.Fori(0, NB) as i:
                    sp.wait_ge(s.qkv_ready, i * BT + BT)
                    for j, table in ((1, d.k), (2, d.v)):
                        sp.dma_start(table[ds(i * BLK, BLK), :].rearrange("(t p) c -> p t c", p=P),
                                     qkv[:, :, j * D:(j + 1) * D]).then_inc(s.stored, 16)
                    sp.wait_ge(s.q3_ready, i * BT + BT)
                    sp.dma_start(d.q3[ds(i * (3 * BLK), 3 * BLK), :].rearrange("(t p s) c -> p t s c", p=P, s=3),
                                 q3[:, :, :, :]).then_inc(s.stored, 16)
                sp.wait_ge(s.stored, 48 * NB + 16)


def load_later(sp, d, g, stored):
    for j, w in enumerate((d.wq, d.wk, d.wv)):
        sp.dma_start(g.wqkv[:, :, j * D:(j + 1) * D], w.rearrange("(k p) o -> p k o", p=P)).then_inc(g.qkv_loaded, 16)
    sp.dma_start(d.q3[3 * NP:3 * ACCW, :], g.none[0:3 * W, :]).then_inc(stored, 16)
    for dst, src in ((g.f1[:, :, :], d.f1.rearrange("(k p) o -> p k o", p=P)), (g.f2[:, :, :], d.f2.rearrange("(k p) o -> p k o", p=P)),
                     (g.rt[:, :, :], d.rt.rearrange("(k p) o -> p k o", p=P)), (g.mb2[:, :], d.mb2), (g.we[0:ED, :], d.we),
                     (g.we[ED:ED + 1, :], d.be), (g.wo[:, 0:2, :], d.wo[0:2 * VG, :].rearrange("(j p) o -> p j o", p=VG)),
                     (g.wo[0:D - 2 * VG, 2, :], d.wo[2 * VG:D, :])):
        sp.dma_start(dst, src).then_inc(g.loaded1, 16)


N_LOADED1 = 8



def stage_scores(nc, d, g):
    with ExitStack() as ctx:
        m = Mem(nc, ctx, "sco")
        ixs = m.sb("ixs", [P, G], I32)
        kg = m.sb("kg", [P, G, D])
        qw = m.sb("qw", [3 * W, G, D], BF16)
        eft = m.sb("eft", [ED + 1, 2, 4 * P])
        epb = m.sb("epb", [P, 2, 4, DH])
        oh3 = m.sb("oh3", [P, 2, 4, 3 * W], BF16)
        ohT = m.sb("ohT", [3 * W, 2, 4 * P], BF16)
        prod = m.sb("prod", [P, 2, 4, D])
        psT = [m.ps(f"psT{h}", [P, 1024], BF16) for h in range(2)]
        psE = m.ps("psE", [P, 512])
        psQ = m.ps("psQ", [P, G, D])
        got = [m.sem(f"got{b}") for b in range(G)]
        qw_got = [m.sem(f"qw_got{b}") for b in range(G)]
        eft_got = [m.sem(f"eft_got{h}") for h in range(2)]
        names = ("copied", "oh3_ready", "turned", "ohT_ready", "ep_made", "ep_ready", "q_ready", "with_ep",
                 "product", "s_ready", "ones")
        s = Names()
        (s.copied, s.oh3_ready, s.turned, s.ohT_ready, s.ep_made, s.ep_ready, s.q_ready, s.with_ep, s.product,
         s.s_ready, s.ones) = (m.sem(n) for n in names)
        with nc.Block() as block:
            @block.scalar
            def _(act):
                first_indices(nc, g, ixs, s.copied)
                nc.scalar.copy(g.spare[0:1, 12:13], g.eps[0:1, 0:1]).then_inc(s.ohT_ready, 1)
                nc.scalar.copy(g.spare[0:1, 13:14], g.eps[0:1, 0:1]).then_inc(s.ep_ready, 1)

                def body(i):
                    for h in range(2):
                        act.wait_ge(s.turned, i * 2 + (h + 3))
                        act.wait_ge(s.q_ready, i * 2 + (h + 1))
                        nc.scalar.copy(ohT[:, h, :], psT[h][0:3 * W, 0:4 * P]).then_inc(s.ohT_ready, 1)
                        act.wait_ge(s.ep_made, i * 2 + (h + 3))
                        act.wait_ge(s.with_ep, i * 2 + (h + 1))
                        nc.scalar.copy(epb[:, h, :, :].rearrange("p t c -> p (t c)"), psE[:, 0:4 * DH]).then_inc(s.ep_ready, 1)
                        index_copies(nc, act, g, ixs, got, s.copied, i, range(4 * h, 4 * h + 4))
                edge_loops(nc, act, g, body)

            @block.gpsimd
            def _(pool):
                edge_loops(nc, pool, g, lambda i: gathers(nc, pool, g, kg, ixs, d.k, got, s.copied, s.with_ep, 4, i))

            @block.sync
            def _(sp):
                def body(i, extra, features):
                    at = windows(nc, mybir.EngineType.SP, g, i)
                    for h in range(2):
                        sp.wait_ge(s.ep_made, i * 2 + (h + 1))
                        settle(sp)
                        if not extra:
                            sp.dma_start(eft[0:ED, h, :], features[:, ds((i * G + 4 * h) * P, 4 * P)]).then_inc(eft_got[h], 64)
                        for j in range(4):
                            b = 4 * h + j
                            if extra:
                                tl = sp.value_load(g.tile[0:1, ds(i * G + b, 1)], min_val=0, max_val=ET - 1)
                                sp.dma_start(eft[0:ED, h, j * P:(j + 1) * P], features[:, ds(tl * P, P)]).then_inc(eft_got[h], 16)
                            if j == 0:
                                sp.wait_ge(s.q_ready, i * 2 + (h + 1))
                                settle(sp)
                            sp.dma_start(qw[:, b, :], d.q3[ds(at[b] * 3, 3 * W), :]).then_inc(qw_got[b], 16)

                def steps(features):
                    with sp.Fori(0, ET // G) as i:
                        body(i, False, features)
                    over = sp.value_load(g.over[0:1, 0:1], min_val=0, max_val=2 * NP)
                    with sp.If(over):
                        with sp.Fori(ET // G, KS // G) as i:
                            body(i, True, features)

                with sp.If(sp.value_load(g.flags[0:1, 1:2], min_val=0, max_val=1)):
                    steps(d.eft)
                with sp.If(sp.value_load(g.flags[0:1, 0:1], min_val=0, max_val=1)):
                    steps(d.efs)

            @block.vector
            def _(dve):
                nc.vector.memset(eft[ED:ED + 1, :, :], 1.0).then_inc(s.ones, 1)
                nc.vector.memset(g.spare[0:1, 1:2], 0.0).then_inc(s.with_ep, 2)
                nc.vector.memset(g.spare[0:1, 2:3], 0.0).then_inc(s.product, 2)
                nc.vector.memset(g.spare[0:1, 3:4], 0.0).then_inc(s.s_ready, 1)

                def build(i, h):
                    dve.wait_ge(s.turned, i * 2 + (h + 1))
                    nc.vector.tensor_tensor(oh3[:, h, :, :], g.iota3[:, :].unsqueeze(1).to_broadcast([P, 4, 3 * W]),
                                            g.dstrel[:, ds(i * G + 4 * h, 4)].unsqueeze(2).to_broadcast([P, 4, 3 * W]),
                                            ALU.is_equal).then_inc(s.oh3_ready, 1)

                def body(i):
                    for h in range(2):
                        for j in range(4):
                            dve.wait_ge(got[4 * h + j], i * 16 + 16)
                        dve.wait_ge(s.ep_ready, i * 2 + (h + 2))
                        dve.wait_ge(s.s_ready, i * 2 + (h + 1))
                        nc.vector.tensor_tensor(prod[:, h, :, :].rearrange("p t (a c) -> p t a c", c=DH),
                                                kg[:, 4 * h:4 * h + 4, :].rearrange("p t (a c) -> p t a c", c=DH),
                                                epb[:, h, :, :].unsqueeze(2).to_broadcast([P, 4, H, DH]), ALU.add).then_inc(s.with_ep, 1)
                        dve.wait_ge(s.with_ep, i * 2 + (h + 3))
                        dve.wait_ge(s.q_ready, i * 2 + (h + 3))
                        nc.vector.tensor_tensor(prod[:, h, :, :], prod[:, h, :, :], psQ[:, 4 * h:4 * h + 4, :], ALU.mult).then_inc(s.product, 1)
                        dve.wait_ge(s.product, i * 2 + (h + 3))
                        nc.vector.tensor_reduce(g.S[:, ds(i * G + 4 * h, 4), :].rearrange("p t a -> p (t a)"),
                                                prod[:, h, :, :].rearrange("p t (a c) -> p (t a) c", c=DH), AX.X, ALU.add).then_inc(s.s_ready, 1)
                        build(i + 1, h)

                for h in range(2):
                    build(0, h)
                with dve.Fori(0, ET // G) as i:
                    body(i)
                dve.wait_ge(s.s_ready, 2 * ET // G + 1)
                over = dve.value_load(g.over[0:1, 0:1], min_val=0, max_val=2 * NP)
                with dve.If(over):
                    with dve.Fori(ET // G, KS // G) as i:
                        body(i)
                    dve.wait_ge(s.s_ready, 2 * KS // G + 1)
                    with dve.Fori(0, XS) as k:
                        tl = dve.value_load(g.tile[0:1, ds(k + ET, 1)], min_val=0, max_val=ET - 1)
                        Sd = g.S[:, ds(tl, 1), :]
                        nc.vector.tensor_tensor(Sd, Sd, g.S[:, ds(k + ET, 1), :], ALU.add).then_inc(s.s_ready, 1)
                        dve.wait_ge(s.s_ready, k + (2 * KS // G + 2))
                S0 = g.S[:, 0:ET, :]
                nc.vector.scalar_tensor_tensor(out=S0, in0=S0, scalar=DH ** -0.5,
                                               in1=g.ew[:, :].unsqueeze(2).to_broadcast([P, ET, H]), op0=ALU.mult, op1=ALU.mult)

            @block.tensor
            def _(pe):
                pe.wait_ge(s.ones, 1)
                pe.wait_ge(g.loaded1, 16 * N_LOADED1)
                free_at_first(nc, g, psE[0:32, 0:32], s.q_ready, 2)
                free_at_first(nc, g, psE[0:32, 32:64], s.turned, 2)
                free_at_first(nc, g, psE[0:32, 64:96], s.ep_made, 2)

                def body(i):
                    for h in range(2):
                        pe.wait_ge(s.oh3_ready, i * 2 + (h + 1))
                        pe.wait_ge(s.ohT_ready, i * 2 + (h + 1))
                        for j in range(4):
                            ins = nc.tensor.transpose(psT[h][0:3 * W, j * P:(j + 1) * P], oh3[:, h, j, :], g.identb[:, :])
                        ins.then_inc(s.turned, 1)
                        pe.wait_ge(eft_got[h], i * 64 + 64)
                        pe.wait_ge(s.ep_ready, i * 2 + (h + 1))
                        for j in range(4):
                            ins = nc.tensor.matmul(psE[:, j * DH:(j + 1) * DH], eft[:, h, j * P:(j + 1) * P], g.we[:, :],
                                                   start=True, stop=True)
                        ins.then_inc(s.ep_made, 1)
                        pe.wait_ge(s.ohT_ready, i * 2 + (h + 2))
                        pe.wait_ge(s.product, i * 2 + (h + 1))
                        for j in range(4):
                            b = 4 * h + j
                            pe.wait_ge(qw_got[b], i * 16 + 16)
                            ins = nc.tensor.matmul(psQ[:, b, :], ohT[:, h, j * P:(j + 1) * P], qw[:, b, :], start=True, stop=True)
                        ins.then_inc(s.q_ready, 1)
                edge_loops(nc, pe, g, body)



def stage_maximum(nc, d, g):
    NG = -(-ET // P)
    GT = [min(P, ET - P * j) for j in range(NG)]
    L = NG * H * P
    with ExitStack() as ctx:
        m = Mem(nc, ctx, "max")
        R = m.sb("R", [P, NG, H, P])
        M1 = m.sb("M1", [P, NG, H, P])
        flags = m.sb("flags", [P, L + 1])
        dT = m.sb("dT", [P, NG, P])
        end = m.sb("end", [H, ET])
        tot = m.sb("tot", [H, ET])
        same = m.sb("same", [H, ET])
        cont = m.sb("cont", [H, ET])
        carry = m.sb("carry", [H, NG * P])
        first = m.sb("first", [H, ET])
        last = m.sb("last", [H, ET])
        pick = m.sb("pick", [P, 2, H])
        ps = m.ps("ps", [P, 6, 512])
        psS = m.ps("psS", [P, 512])
        psR = m.ps("psR", [P, 512])
        filled = m.sem("filled")
        ch, tn, pk, bk = m.sem("chain"), m.sem("turned"), m.sem("picked"), m.sem("back")

        def rows_of(X):
            return X[:, :, :, :].rearrange("p g a c -> p (g a c)")

        flatps = ps[:, :, :].rearrange("p b (a c) -> p (b a) c", c=P)
        with nc.Block() as block:
            @block.gpsimd
            def _(pool):
                nc.gpsimd.memset(R[:, NG - 1, :, :], 0.0)
                nc.gpsimd.memset(dT[:, NG - 1, :], 0.0)
                nc.gpsimd.memset(carry[:, :], 0.0)
                nc.gpsimd.memset(flags[:, :], -BIG).then_inc(filled, 1)
                nc.gpsimd.memset(g.oacc[:, :, :], 0.0)

            @block.tensor
            def _(pe):
                pe.wait_ge(pk, 1)
                for j in range(NG):
                    nc.tensor.transpose(psS[0:GT[j], j * P:(j + 1) * P], g.dstF[:, j * P:j * P + GT[j]], g.ident[:, :])
                nc.tensor.matmul(psR[0:H, 0:ET], pick[:, 0, :], g.dstF[:, :], start=True, stop=True)
                for a in range(H):
                    for j in range(NG):
                        ins = nc.tensor.transpose(flatps[0:GT[j], j * H + a, :], g.S[:, j * P:j * P + GT[j], a], g.ident[:, :])
                ins.then_inc(tn, 1)
                pe.wait_ge(bk, 1)
                nc.tensor.matmul(psR[0:H, 0:ET], pick[:, 1, :], g.dstF[:, :], start=True, stop=True).then_inc(tn, 1)
                for way in range(2):
                    pe.wait_ge(bk, 2 + 2 * way)
                    X, c = (M1, P - 1) if way == 0 else (M1, 0)
                    for j in range(NG):
                        ins = nc.tensor.transpose(psS[0:H, j * P:j * P + GT[j]], X[0:GT[j], j, :, c], g.ident[0:GT[j], 0:GT[j]])
                    ins.then_inc(tn, 1)
                    pe.wait_ge(bk, 3 + 2 * way)
                    for j in range(NG):
                        ins = nc.tensor.transpose(psR[:, j * H:(j + 1) * H], carry[:, j * P:(j + 1) * P], g.ident[0:H, 0:H])
                    ins.then_inc(tn, 1)
                pe.wait_ge(bk, 6)
                for a in range(H):
                    for j in range(NG):
                        ins = nc.tensor.transpose(flatps[:, j * H + a, 0:GT[j]], M1[0:GT[j], j, a, :], g.ident[0:GT[j], 0:GT[j]])
                ins.then_inc(tn, 1)

            @block.vector
            def _(dve):
                t = Tally(ch)
                T = [0]

                def turned(n=1):
                    T[0] += n
                    dve.wait_ge(tn, T[0])

                def go(ins):
                    t.mark(ins)
                    t.wait(dve)

                nc.vector.tensor_copy(pick[:, 0, :], g.ident[:, 0:1].to_broadcast([P, H]))
                nc.vector.tensor_copy(pick[:, 1, :], g.ident[:, P - 1:P].to_broadcast([P, H])).then_inc(pk, 1)
                turned()
                nc.vector.tensor_copy(first[:, :], psR[0:H, 0:ET]).then_inc(bk, 1)
                dve.wait_ge(filled, 1)
                for j in range(NG):
                    nc.vector.tensor_copy(R[0:GT[j], j, :, :], flatps[0:GT[j], j * H:(j + 1) * H, :])
                    ins = nc.vector.tensor_copy(dT[0:GT[j], j, :], psS[0:GT[j], j * P:(j + 1) * P])
                go(ins)
                turned()
                go(nc.vector.tensor_copy(last[:, :], psR[0:H, 0:ET]))
                go(nc.vector.tensor_tensor(M1[:, :, 0, 1:P], dT[:, :, 1:P], dT[:, :, 0:P - 1], ALU.is_equal))
                go(nc.vector.tensor_scalar(M1[:, :, 0, 1:P], M1[:, :, 0, 1:P], 2.0, -1.0, ALU.mult, ALU.add))
                for a in range(H):
                    f = flags[:, 0:L].rearrange("p (g a c) -> p g a c", g=NG, a=H)[:, :, a, 1:P]
                    ins = nc.vector.tensor_scalar(f, M1[:, :, 0, 1:P], BIG, None, ALU.mult)
                go(ins)
                for way in range(2):
                    def rev(ap):
                        return ap[:, ::-1] if way else ap
                    fl = flags[:, way:L + way]
                    ins = nc.vector.tensor_tensor_scan(rev(rows_of(M1)), rev(fl), rev(rows_of(R)), -BIG, ALU.min, ALU.max)
                    ins.then_inc(bk, 1)
                    turned()
                    go(nc.vector.tensor_copy(end[:, :], psS[0:H, 0:ET]))
                    go(nc.vector.memset(same[:, :], 0.0))
                    go(nc.vector.memset(cont[:, :], 0.0))
                    if way == 0:
                        nc.vector.tensor_tensor(same[:, 1:ET], last[:, 1:ET], last[:, 0:ET - 1], ALU.is_equal)
                        go(nc.vector.tensor_tensor(cont[:, 1:ET], first[:, 1:ET], last[:, 0:ET - 1], ALU.is_equal))
                    else:
                        nc.vector.tensor_tensor(same[:, 0:ET - 1], first[:, 1:ET], first[:, 0:ET - 1], ALU.is_equal)
                        go(nc.vector.tensor_tensor(cont[:, 0:ET - 1], first[:, 1:ET], last[:, 0:ET - 1], ALU.is_equal))
                    for f in (same, cont):
                        go(nc.vector.tensor_scalar(f[:, :], f[:, :], 2.0, -1.0, ALU.mult, ALU.add))
                        go(nc.vector.tensor_scalar(f[:, :], f[:, :], BIG, None, ALU.mult))
                    go(nc.vector.tensor_tensor_scan(rev(tot[:, :]), rev(same[:, :]), rev(end[:, :]), -BIG, ALU.min, ALU.max))
                    go(nc.vector.tensor_copy(carry[:, 0:ET], cont[:, :]))
                    if way == 0:
                        go(nc.vector.tensor_tensor(carry[:, 1:ET], tot[:, 0:ET - 1], cont[:, 1:ET], ALU.min))
                    else:
                        go(nc.vector.tensor_tensor(carry[:, 0:ET - 1], tot[:, 1:ET], cont[:, 0:ET - 1], ALU.min))
                    nc.vector.tensor_scalar(carry[:, 0:ET], carry[:, 0:ET], -BIG, None, ALU.max).then_inc(bk, 1)
                    turned()
                    c = P - 1 if way else 0
                    src = R[:, :, :, c]
                    go(nc.vector.tensor_tensor(src, src, psR[:, 0:NG * H].rearrange("p (j a) -> p j a", a=H), ALU.max))
                    ins = nc.vector.tensor_tensor_scan(rev(rows_of(M1)), rev(fl), rev(rows_of(R)), -BIG, ALU.min, ALU.max)
                    if way == 0:
                        go(ins)
                        go(nc.vector.tensor_copy(rows_of(R), rows_of(M1)))
                    else:
                        ins.then_inc(bk, 1)
                turned()
                for j in range(NG):
                    Sj = g.S[:, j * P:j * P + GT[j], :]
                    ins = nc.vector.tensor_tensor(Sj, Sj, flatps[:, j * H:(j + 1) * H, 0:GT[j]].rearrange("p a t -> p t a"), ALU.subtract)
                ins.then_inc(bk, 1)

            @block.scalar
            def _(act):
                act.wait_ge(bk, 7)
                nc.scalar.activation(g.S[:, 0:ET, :], g.S[:, 0:ET, :], ACT.Exp)



def stage_gather1(nc, d, g):
    with ExitStack() as ctx:
        m = Mem(nc, ctx, "ga1")
        ixs = m.sb("ixs", [P, G], I32)
        vg = m.sb("vg", [P, G, D])
        oh = m.sb("oh", [P, 2, 4, W])
        pv = m.sb("pv", [P, 2, 4, 3 * VG])
        psO = m.ps("psO", [P, 4, 512])
        got = [m.sem(f"got{b}") for b in range(G)]
        names = ("copied", "oh_ready", "pv_ready", "o_ready", "o_added", "moved")
        s = Names()
        (s.copied, s.oh_ready, s.pv_ready, s.o_ready, s.o_added, s.moved) = (m.sem(n) for n in names)
        with nc.Block() as block:
            @block.scalar
            def _(act):
                first_indices(nc, g, ixs, s.copied)
                edge_loops(nc, act, g, lambda i: index_copies(nc, act, g, ixs, got, s.copied, i))

            @block.gpsimd
            def _(pool):
                edge_loops(nc, pool, g, lambda i: gathers(nc, pool, g, vg, ixs, d.v, got, s.copied, s.pv_ready, 4, i))

            @block.vector
            def _(dve):
                nc.vector.memset(g.spare[0:1, 4:5], 0.0).then_inc(s.pv_ready, 2)
                nc.vector.memset(g.spare[0:1, 5:6], 0.0).then_inc(s.o_added, 5)
                over = dve.value_load(g.over[0:1, 0:1], min_val=0, max_val=2 * NP)
                with dve.If(over):
                    with dve.Fori(0, XS) as k:
                        tl = dve.value_load(g.tile[0:1, ds(k + ET, 1)], min_val=0, max_val=ET - 1)
                        nc.vector.tensor_copy(g.S[:, ds(k + ET, 1), :], g.S[:, ds(tl, 1), :]).then_inc(s.moved, 1)
                    dve.wait_ge(s.moved, XS)

                def build(i, h):
                    dve.wait_ge(s.o_ready, i * 2 + (h + 1))
                    nc.vector.tensor_tensor(oh[:, h, :, :], g.iota[:, :].unsqueeze(1).to_broadcast([P, 4, W]),
                                            g.dstrel[:, ds(i * G + 4 * h, 4)].unsqueeze(2).to_broadcast([P, 4, W]),
                                            ALU.is_equal).then_inc(s.oh_ready, 1)

                def weigh(i, h):
                    for j in range(4):
                        dve.wait_ge(got[4 * h + j], i * 16 + 16)
                    dve.wait_ge(s.o_ready, i * 2 + (h + 1))
                    p8 = g.S[:, ds(i * G + 4 * h, 4), :]
                    nc.vector.tensor_copy(pv[:, h, :, D:D + H], p8)
                    nc.vector.tensor_tensor(pv[:, h, :, 0:D].rearrange("p t (a c) -> p t a c", c=DH),
                                            vg[:, 4 * h:4 * h + 4, :].rearrange("p t (a c) -> p t a c", c=DH),
                                            p8.unsqueeze(3).to_broadcast([P, 4, H, DH]), ALU.mult).then_inc(s.pv_ready, 1)

                def add(i, h, at):
                    dve.wait_ge(s.o_ready, i * 2 + (h + 3))
                    for j in range(4):
                        dve.wait_ge(s.o_added, i * G + (4 * h + j + 5))
                        o = g.oacc[:, :, ds(at[j], W)]
                        nc.vector.tensor_tensor(o, psO[0:VG, h, j * 3 * W:(j + 1) * 3 * W].rearrange("p (c w) -> p c w", c=3),
                                                o, ALU.add).then_inc(s.o_added, 1)
                    build(i + 1, h)

                for h in range(2):
                    build(0, h)
                at = windows(nc, mybir.EngineType.DVE, g, 0)
                weigh(0, 0)
                weigh(0, 1)
                add(0, 0, at[0:4])
                with dve.Fori(1, ET // G) as i:
                    at = windows(nc, mybir.EngineType.DVE, g, i, -4)
                    weigh(i, 0)
                    add(i - 1, 1, at[0:4])
                    weigh(i, 1)
                    add(i, 0, at[4:8])
                at = windows(nc, mybir.EngineType.DVE, g, ET // G - 1)
                add(ET // G - 1, 1, at[4:8])
                over = dve.value_load(g.over[0:1, 0:1], min_val=0, max_val=2 * NP)
                with dve.If(over):
                    with dve.Fori(ET // G, KS // G) as i:
                        at = windows(nc, mybir.EngineType.DVE, g, i)
                        for h in range(2):
                            weigh(i, h)
                        for h in range(2):
                            add(i, h, at[4 * h:4 * h + 4])

            @block.tensor
            def _(pe):
                free_at_first(nc, g, psO[0:32, 3, 0:32], s.o_ready, 2)

                def body(i):
                    for h in range(2):
                        pe.wait_ge(s.oh_ready, i * 2 + (h + 1))
                        pe.wait_ge(s.pv_ready, i * 2 + (h + 3))
                        pe.wait_ge(s.o_added, i * G + (4 * h + 1))
                        for j in range(4):
                            for c in range(3):
                                ins = nc.tensor.matmul(psO[0:VG, h, (j * 3 + c) * W:(j * 3 + c + 1) * W], pv[:, h, j, c * VG:(c + 1) * VG],
                                                       oh[:, h, j, :], start=True, stop=True)
                        ins.then_inc(s.o_ready, 1)
                edge_loops(nc, pe, g, body)





ORDER_FF = (("f", 0), ("f", 1), ("f", 2), ("spread", 0), ("f", 3), ("spread", 1), ("f", 4), ("f", 5), ("wo", 0), ("f", 6), ("f", 7),
            ("back", 0), ("y", 0), ("y", 1), ("y", 2), ("turn", 0), ("y", 3))


def stage_feed_forward(nc, d, g):
    D0 = 64
    with ExitStack() as ctx:
        m = Mem(nc, ctx, "ff")
        nm = Norm(m)
        head = m.sb("head", [VG, 3, VG])
        ab = m.sb("ab", [P, DK])
        rden = m.sb("rden", [VG, BLK])
        att = m.sb("att", [VG, 3, BLK])
        aT = m.sb("aT", [P, DK, BLK])
        xn = m.sb("xn", [P, BT, D])
        xT = m.sb("xT", [P, DK, BLK])
        h = m.sb("h", [P, FK, BLK])
        y = m.sb("y", [P, BT, D])
        psS = m.ps("psS", [P, BT, D])
        psH = m.ps("psH", [P, 2, 512])
        psW = m.ps("psW", [P, 2, 512])
        psY = m.ps("psY", [P, BT, D])
        names = ("att_chain", "y_chain", "ab_ready", "head_ready", "rden_ready", "spread", "att_ready", "a_made", "aT_ready",
                 "a_back", "u_ready", "xn_ready", "turned", "xT_ready", "h_made", "h_ready", "y_made")
        s = Names()
        (s.att_chain, s.y_chain, s.ab_ready, s.head_ready, s.rden_ready, s.spread, s.att_ready, s.a_made, s.aT_ready,
         s.a_back, s.u_ready, s.xn_ready, s.turned, s.xT_ready, s.h_made, s.h_ready, s.y_made) = (m.sem(n) for n in names)
        with nc.Block() as block:
            @block.gpsimd
            def _(pool):
                nc.gpsimd.memset(head[:, :, :], 1.0).then_inc(s.head_ready, 1)
                pool.wait_ge(s.head_ready, 1)
                first = DH * (D - 2 * VG)
                nc.gpsimd.affine_select(out=head[:, :, :], in_=head[:, :, :], compare_op=ALU.is_ge, fill=0.0, base=first,
                                        pattern=[[VG, 3], [1, VG]], channel_multiplier=-DH).then_inc(s.head_ready, 1)
                pool.wait_ge(s.head_ready, 2)
                nc.gpsimd.affine_select(out=head[:, :, :], in_=head[:, :, :], compare_op=ALU.is_ge, fill=0.0, base=DH - 1 - first,
                                        pattern=[[-VG, 3], [-1, VG]], channel_multiplier=DH).then_inc(s.head_ready, 1)

            @block.sync
            def _(sp):
                for w_sb, w in ((g.mw1, d.mw1), (g.mw2, d.mw2)):
                    for e in range(E1):
                        sp.dma_start(w_sb[:, e, :, :], w[e].rearrange("(k p) o -> p k o", p=P)).then_inc(g.weights1, 16)

            @block.vector
            def _(dve):
                nc.vector.tensor_scalar(ab[:, :], g.cols[:, COL["bo"][0]:COL["bo"][1]], row(g, "alpha"), None, ALU.mult).then_inc(s.ab_ready, 1)
                nc.vector.memset(g.spare[0:1, 1:2], 0.0).then_inc(s.att_chain, 1)
                nc.vector.memset(g.spare[0:1, 2:3], 0.0).then_inc(s.y_chain, 1)

                def attention(j):
                    t = Tally(s.att_chain, j, 3, 1)
                    t.wait(dve)
                    t.mark(nc.vector.tensor_scalar(rden[D0:VG, :], g.oacc[D0:VG, 2, ds(j * BLK, BLK)], 0.5, None, ALU.max))
                    t.wait(dve)
                    nc.vector.reciprocal(rden[D0:VG, :], rden[D0:VG, :]).then_inc(s.rden_ready, 1)
                    for c in range(3):
                        dve.wait_ge(s.spread, j * 3 + (c + 1))
                        o = g.oacc[:, c, ds(j * BLK, BLK)]
                        nc.vector.tensor_tensor(att[:, c, :], psS[0:VG, 2 * (c % 2):2 * (c % 2) + 2, :].rearrange("p a c -> p (a c)"), o,
                                                ALU.mult).then_inc(s.att_ready, 1)
                    dve.wait_ge(s.a_back, j + 1)
                    ub = g.u[:, ds(j * BT, BT), :]
                    nc.vector.tensor_tensor(ub, psS[:, :, :], ub, ALU.add).then_inc(s.u_ready, 1)
                    dve.wait_ge(s.u_ready, j + 1)
                    norm_dve(nc, dve, g, nm, t, j, 1, 0, lambda q: g.u[:, ds(j * BT + q, 1), :].rearrange("p a c -> p (a c)"),
                             lambda q: xn[:, q, :], s.xn_ready)
                    t.close()

                def finish(i):
                    t = Tally(s.y_chain, i, 3, 1)
                    t.wait(dve)
                    dve.wait_ge(s.y_made, i + 1)
                    ub = g.u[:, ds(i * BT, BT), :]
                    t.mark(nc.vector.tensor_tensor(y[:, :, :], psY[:, :, :], row(g, "b2").unsqueeze(1).to_broadcast([P, BT, D]), ALU.add))
                    t.wait(dve)
                    t.mark(nc.vector.scalar_tensor_tensor(out=ub, in0=y[:, :, :], scalar=row(g, "beta"), in1=ub, op0=ALU.mult, op1=ALU.add))
                    t.wait(dve)
                    xb = g.x[:, ds(i * BT, BT), :]
                    t.mark(nc.vector.tensor_tensor(xb, xb, ub, ALU.add))
                    t.close()

                attention(0)
                with dve.Fori(0, NB - 1) as i:
                    attention(i + 1)
                    finish(i)
                finish(NB - 1)

            @block.scalar
            def _(act):
                act.wait_ge(s.ab_ready, 1)
                nc.scalar.copy(g.spare[0:1, 14:15], g.eps[0:1, 0:1]).then_inc(s.h_ready, 1)

                def output(j):
                    for o in range(DK):
                        act.wait_ge(s.a_made, j * 2 + (o + 1))
                        nc.scalar.activation(aT[:, o, :], psW[:, o, :], ACT.Identity, bias=ab[:, o:o + 1],
                                             scale=row(g, "alpha")).then_inc(s.aT_ready, 1)

                def take_turned(j):
                    act.wait_ge(s.turned, j + 1)
                    for k in range(DK):
                        ins = nc.scalar.activation(xT[:, k, :], psW[:, k, :], ACT.Identity, bias=vec(g, "ln2_b", k),
                                                   scale=vec(g, "ln2_g", k))
                    ins.then_inc(s.xT_ready, 1)

                def body(i, next_):
                    for what, n in ORDER_FF:
                        if what == "f":
                            act.wait_ge(s.h_made, i * FK + (n + 1))
                            nc.scalar.activation(h[:, n, :], psH[:, n % 2, :], ACT.Gelu, bias=vec(g, "gb1", n)).then_inc(s.h_ready, 1)
                        if next_ and what == "wo":
                            output(i + 1)
                        if next_ and (what, n) == ("y", 0):
                            norm_act(nc, act, g, nm, i + 1, 1, 0)
                        if next_ and what == "turn":
                            take_turned(i + 1)

                output(0)
                norm_act(nc, act, g, nm, 0, 1, 0)
                take_turned(0)
                with act.Fori(0, NB - 1) as i:
                    body(i, True)
                body(NB - 1, False)

            @block.tensor
            def _(pe):
                pe.wait_ge(s.head_ready, 3)

                def spread(j, part):
                    for c in ((0, 1), (2,))[part]:
                        if c == 0:
                            pe.wait_ge(s.rden_ready, j + 1)
                        if c == 2:
                            pe.wait_ge(s.att_ready, j * 3 + 1)
                        nc.tensor.matmul(psS[0:VG, 2 * (c % 2):2 * (c % 2) + 2, :].rearrange("p a c -> p (a c)"), head[D0:VG, c, :],
                                         rden[D0:VG, :], start=True, stop=True).then_inc(s.spread, 1)

                def output(j):
                    pe.wait_ge(s.att_ready, j * 3 + 3)
                    for o in range(DK):
                        for c in range(3):
                            K = VG if c < 2 else D - 2 * VG
                            ins = nc.tensor.matmul(psW[:, o, :], g.wo[0:K, c, o * P:(o + 1) * P], att[0:K, c, :],
                                                   start=(c == 0), stop=(c == 2))
                        ins.then_inc(s.a_made, 1)

                def back(j):
                    pe.wait_ge(s.aT_ready, j * 2 + 2)
                    for q in range(BT):
                        for k in range(DK):
                            ins = nc.tensor.transpose(psS[:, q, k * P:(k + 1) * P], aT[:, k, q * P:(q + 1) * P], g.ident[:, :])
                    ins.then_inc(s.a_back, 1)

                def turn_norm(j):
                    pe.wait_ge(s.xn_ready, j + 1)
                    turn(nc, g, psW, lambda q: xn[:, q, :]).then_inc(s.turned, 1)

                def body(i, next_):
                    pe.wait_ge(s.xT_ready, i + 1)
                    for what, n in ORDER_FF:
                        if what == "f":
                            pe.wait_ge(s.h_ready, i * FK + (n if n >= 1 else 1))
                            for k in range(DK):
                                ins = nc.tensor.matmul(psH[:, n % 2, :], g.f1[:, k, n * P:(n + 1) * P], xT[:, k, :],
                                                       start=(k == 0), stop=(k == DK - 1))
                            ins.then_inc(s.h_made, 1)
                        if what == "y":
                            if n == 0:
                                pe.wait_ge(s.h_ready, i * FK + (FK + 1))
                                pe.wait_ge(s.y_chain, i * 3 + 1)
                            for f in range(FK):
                                ins = nc.tensor.matmul(psY[:, n, :], h[:, f, n * P:(n + 1) * P], g.f2[:, f, :],
                                                       start=(f == 0), stop=(f == FK - 1))
                            if n == BT - 1:
                                ins.then_inc(s.y_made, 1)
                        if next_ and what == "spread":
                            spread(i + 1, n)
                        if next_ and what == "wo":
                            output(i + 1)
                        if next_ and what == "back":
                            back(i + 1)
                        if next_ and what == "turn":
                            turn_norm(i + 1)

                spread(0, 0)
                spread(0, 1)
                output(0)
                back(0)
                turn_norm(0)
                with pe.Fori(0, NB - 1) as i:
                    body(i, True)
                body(NB - 1, False)



def stage_experts1(nc, d, g):
    order = [("A", 0), ("logits", 0), ("A", 1), ("C", 0), ("A", 2), ("mix", 0), ("A", 3)]
    for e in range(1, E1 - 3):
        order += [("C", e), ("A", e + 3)]
    order += [("C", E1 - 3), ("turn", 0), ("C", E1 - 2), ("C", E1 - 1)]
    HS = 3
    with ExitStack() as ctx:
        m = Mem(nc, ctx, "ex1")
        nm = Norm(m)
        r = Router(m, E1)
        xn = m.sb("xn", [P, BT, D])
        xT = m.sb("xT", [P, DK, BLK])
        h1 = m.sb("h1", [P, HS, DK, BLK])
        spare = m.sb("spare", [1, DH])
        acc = m.sb("acc", [P, BT, D])
        psW = m.ps("psW", [P, 2, 512])
        psA = m.ps("psA", [P, 2, 2, 512])
        psC = m.ps("psC", [P, BT, D])
        names = ("norm_chain", "chain", "xn_ready", "turned", "xT_ready", "logits", "gate_ready", "gate_turned", "gateT_ready", "bias_mixed",
                 "acc_ready", "a_ready", "h1_ready", "c_ready", "c_used", "out_ready", "stored")
        s = Names()
        (s.norm_chain, s.chain, s.xn_ready, s.turned, s.xT_ready, s.logits, s.gate_ready, s.gate_turned, s.gateT_ready,
         s.bias_mixed, s.acc_ready, s.a_ready, s.h1_ready, s.c_ready, s.c_used, s.out_ready, s.stored) = (m.sem(n) for n in names)
        with nc.Block() as block:
            @block.vector
            def _(dve):
                nc.vector.memset(g.spare[0:1, 2:3], 0.0).then_inc(s.c_used, BT)
                nc.vector.memset(g.spare[0:1, 3:4], 0.0).then_inc(s.chain, 1)
                nc.vector.memset(g.spare[0:1, 5:6], 0.0).then_inc(s.norm_chain, 1)
                nc.vector.memset(g.spare[0:1, 4:5], 0.0).then_inc(s.acc_ready, 1)
                def norm(i):
                    t = Tally(s.norm_chain, i, 2, 1)
                    norm_dve(nc, dve, g, nm, t, i, 1, 0, lambda q: g.x[:, ds(i * BT + q, 1), :].rearrange("p a c -> p (a c)"),
                             lambda q: xn[:, q, :], s.xn_ready)
                    t.close()

                def body(i, next_):
                    t = Tally(s.chain, i, 21, 1)
                    t.wait(dve)
                    dve.wait_ge(s.logits, i + 1)
                    gates_dve(nc, dve, g, r, t, i, E1, psW[:, 1, 0:BT * E1].rearrange("p (t e) -> p t e", t=BT), None, 1)
                    t.mark(nc.vector.tensor_tensor(r.m[:, :, 2], r.m[:, :, 0], r.m[:, :, 1], ALU.add))
                    t.wait(dve)
                    t.mark(nc.vector.tensor_scalar(r.m[:, :, 2], r.m[:, :, 2], 1e-12, None, ALU.max))
                    t.wait(dve)
                    t.mark(nc.vector.reciprocal(r.m[:, :, 3], r.m[:, :, 2]))
                    t.wait(dve)
                    nc.vector.tensor_tensor(r.m[:, :, 0], r.m[:, :, 0], r.m[:, :, 3], ALU.mult)
                    t.mark(nc.vector.tensor_tensor(r.m[:, :, 1], r.m[:, :, 1], r.m[:, :, 3], ALU.mult))
                    t.wait(dve)
                    mix_dve(nc, dve, r, t, E1, r.m[:, :, 0], r.m[:, :, 1], s.gate_ready)
                    dve.wait_ge(s.gate_ready, i + 1)
                    dve.wait_ge(s.bias_mixed, i + 1)
                    dve.wait_ge(s.stored, i * 16 + 16)
                    nc.vector.tensor_tensor(acc[:, :, :], psW[:, :, :].rearrange("p a c -> p (a c)").rearrange("p (t c) -> p t c", t=BT),
                                            xn[:, :, :], ALU.add).then_inc(s.acc_ready, 1)
                    dve.wait_ge(s.acc_ready, i + 2)
                    for e in range(E1):
                        if e == E1 - 4 and next_:
                            norm(i + 1)
                        for q in range(BT):
                            if q % 2 == 0:
                                dve.wait_ge(s.c_ready, i * (E1 * BT) + (e * BT + q + 2))
                            dve.wait_ge(s.c_used, i * (E1 * BT) + (e * BT + q + 1))
                            nc.vector.scalar_tensor_tensor(out=acc[:, q, :], in0=psC[:, q, :], scalar=r.gate[:, q, e:e + 1],
                                                           in1=acc[:, q, :], op0=ALU.mult, op1=ALU.add).then_inc(s.c_used, 1)
                    dve.wait_ge(s.c_used, i * (E1 * BT) + (E1 * BT + BT))
                    nc.vector.tensor_tensor(acc[:, :, :], acc[:, :, :], g.x[:, ds(i * BT, BT), :], ALU.add).then_inc(s.out_ready, 1)
                    t.close()

                norm(0)
                with dve.Fori(0, NB - 1) as i:
                    body(i, True)
                body(NB - 1, False)

            @block.scalar
            def _(act):
                def take_turned(i):
                    act.wait_ge(s.turned, i + 1)
                    nc.scalar.copy(xT[:, :, :], psW[:, :, :]).then_inc(s.xT_ready, 1)

                def body(i, next_):
                    for what, e in order:
                        if what == "A":
                            for o in range(DK):
                                act.wait_ge(s.a_ready, i * (2 * E1) + (2 * e + o + 1))
                                nc.scalar.activation(h1[:, e % HS, o, :], psA[:, e % 2, o, :], ACT.Gelu,
                                                     bias=vec(g, "mb1", 2 * e + o)).then_inc(s.h1_ready, 1)
                        if (what, e) == ("A", 1):
                            act.wait_ge(r.shifted, i + 1)
                            nc.scalar.activation(r.p[:, :, :], r.p[:, :, :], ACT.Exp).then_inc(r.p_ready, 1)
                        if what == "mix":
                            act.wait_ge(s.gate_turned, i + 1)
                            nc.scalar.copy(r.gateT[:, :], psW[0:E1, 0, :]).then_inc(s.gateT_ready, 1)
                        if next_ and (what, e) == ("A", E1 - 2):
                            norm_act(nc, act, g, nm, i + 1, 1, 0)
                        if next_ and what == "turn":
                            take_turned(i + 1)

                norm_act(nc, act, g, nm, 0, 1, 0)
                take_turned(0)
                with act.Fori(0, NB - 1) as i:
                    body(i, True)
                body(NB - 1, False)

            @block.tensor
            def _(pe):
                pe.wait_ge(g.weights1, 16 * 2 * E1)

                def turn_norm(i):
                    pe.wait_ge(s.xn_ready, i + 1)
                    turn(nc, g, psW, lambda q: xn[:, q, :]).then_inc(s.turned, 1)

                def body(i, next_):
                    pe.wait_ge(s.xT_ready, i + 1)
                    for what, e in order:
                        if what == "logits":
                            for q in range(BT):
                                for k in range(DK):
                                    ins = nc.tensor.matmul(psW[:, 1, q * E1:(q + 1) * E1], xT[:, k, q * P:(q + 1) * P], g.rt[:, k, :],
                                                           start=(k == 0), stop=(k == DK - 1))
                            ins.then_inc(s.logits, 1)
                        if what == "A":
                            if e >= 2:
                                pe.wait_ge(s.h1_ready, i * (2 * E1) + (2 * e - 2))
                            for o in range(DK):
                                for k in range(DK):
                                    ins = nc.tensor.matmul(psA[:, e % 2, o, :], g.mw1[:, e, k, o * P:(o + 1) * P], xT[:, k, :],
                                                           start=(k == 0), stop=(k == DK - 1))
                                ins.then_inc(s.a_ready, 1)
                        if what == "mix":
                            pe.wait_ge(s.gate_ready, i + 1)
                            for q in range(BT):
                                ins = nc.tensor.transpose(psW[0:E1, 0, q * P:(q + 1) * P], r.gate[:, q, :], g.ident[:, :])
                            ins.then_inc(s.gate_turned, 1)
                            pe.wait_ge(s.gateT_ready, i + 1)
                            for q in range(BT):
                                ins = nc.tensor.matmul(psW[:, q // 2, (q % 2) * D:(q % 2 + 1) * D], r.gateT[:, q * P:(q + 1) * P],
                                                       g.mb2[:, :], start=True, stop=True)
                            ins.then_inc(s.bias_mixed, 1)
                        if what == "C":
                            pe.wait_ge(s.h1_ready, i * (2 * E1) + (2 * e + 2))
                            for q in range(BT):
                                if q % 2 == 0:
                                    pe.wait_ge(s.c_used, i * (E1 * BT) + (e * BT + q + 2))
                                for k in range(DK):
                                    ins = nc.tensor.matmul(psC[:, q, :], h1[:, e % HS, k, q * P:(q + 1) * P], g.mw2[:, e, k, :],
                                                           start=(k == 0), stop=(k == DK - 1))
                                ins.then_inc(s.c_ready, 1)
                        if next_ and what == "turn":
                            pe.wait_ge(s.acc_ready, i + 2)
                            turn_norm(i + 1)

                turn_norm(0)
                with pe.Fori(0, NB - 1) as i:
                    body(i, True)
                body(NB - 1, False)

            @block.sync
            def _(sp):
                sp.dma_start(spare[:, :], d.be).then_inc(s.stored, 16)
                with sp.Fori(0, NB) as i:
                    sp.wait_ge(s.out_ready, i + 1)
                    sp.dma_start(d.out[ds(i * BLK, BLK), :].rearrange("(t p) c -> p t c", p=P), acc[:, :, :]).then_inc(s.stored, 16)
                sp.wait_ge(s.stored, 16 * NB + 16)



class Names:
    pass


IN = {
    "x": ([NP, D], F32), "src": ([P, ET], I32), "dst": ([P, ET], I32), "typ": ([P, ET], I32), "ew": ([P, ET], F32),
    "line": ([P, LINE + 1], I32), "ef": ([EP, ED], F32), "eft": ([ED, EP], F32), "cols": ([P, NCOL], F32), "rows": ([1, NROW], F32),
    "basis": ([NBASE, D, D], F32), "loopw": ([D, D], F32), "rw1": ([D, RH], F32), "rw2": ([RH, E0], F32),
    "w1": ([E0, D, D], F32), "w2": ([E0, D, D], F32), "w3": ([E0, D, D], F32), "b3": ([E0, D], F32),
    "wq": ([D, D], F32), "wk": ([D, D], F32), "wv": ([D, D], F32), "we": ([ED, DH], F32), "be": ([1, DH], F32),
    "wo": ([D, D], F32), "f1": ([D, FF], F32), "f2": ([FF, D], F32), "rt": ([D, E1], F32),
    "mw1": ([E1, D, D], F32), "mw2": ([E1, D, D], F32), "mb2": ([E1, D], F32),
}


def program(nc):
    d, g = Names(), Names()
    (d.x, d.src, d.dst, d.typ, d.ew, d.line, d.ef, d.eft, d.cols, d.rows, d.basis, d.loopw, d.rw1, d.rw2, d.w1, d.w2, d.w3, d.b3,
     d.wq, d.wk, d.wv, d.we, d.be, d.wo, d.f1, d.f2, d.rt, d.mw1, d.mw2, d.mb2) = \
        (nc.dram_tensor(f"in_{name}", shape, dt, kind="ExternalInput").ap() for name, (shape, dt) in IN.items())
    d.out = nc.dram_tensor("out_0", [NP, D], F32, kind="ExternalOutput").ap()
    d.xn, d.k, d.v = (nc.dram_tensor(f"table_{name}", [NP, D], F32).ap() for name in ("xn", "k", "v"))
    d.q3 = nc.dram_tensor("table_q3", [3 * ACCW, D], BF16).ap()
    d.sorted = nc.dram_tensor("sorted_edges", [EP, 4 + ED], F32).ap()
    d.efs = nc.dram_tensor("sorted_features", [ED, EP], F32).ap()
    with ExitStack() as ctx:
        m = Mem(nc, ctx, "g")
        g.ident = m.sb("ident", [P, P])
        g.identb = m.sb("identb", [P, P], BF16)
        g.iota = m.sb("iota", [P, W])
        g.iota3 = m.sb("iota3", [P, 3 * W])
        g.rev = m.sb("rev", [P, E1])
        g.eps = m.sb("eps", [P, 1])
        g.spare = m.sb("spare", [1, 16])
        g.none = m.sb("none", [P, D], BF16)
        g.cols = m.sb("cols", [P, NCOL])
        g.rows = m.sb("rows", [P, NROW])
        g.x = m.sb("x", [P, NT, D])
        g.srcI = m.sb("srcI", [P, KS + G], I32)
        g.ew = m.sb("ew", [P, ET])
        g.dstF = m.sb("dstF", [P, ET])
        g.dstrel = m.sb("dstrel", [P, KS + G])
        g.win = m.sb("win", [1, KS], I32)
        g.tile = m.sb("tile", [1, KS], I32)
        g.over = m.sb("over", [1, 1], I32)
        g.flags = m.sb("flags", [1, 2], I32)
        g.weights0 = m.sem("weights0")
        g.rw1 = m.sb("rw1", [P, DK, RH])
        g.rw2 = m.sb("rw2", [P, E0])
        g.b3 = m.sb("b3", [E0, D])
        g.experts = m.sb("experts", [P, 3 * E0, DK, D])
        g.w1, g.w2, g.w3 = (g.experts[:, j * E0:(j + 1) * E0, :, :] for j in range(3))
        g.mw1, g.mw2 = (g.experts[:, j * E1:(j + 1) * E1, :, :] for j in range(2))
        with ExitStack() as sums:
            ms = Mem(nc, sums, "z0")
            g.coef = ms.sb("coef", [P, KS + G, NBASE])
            g.basis = ms.sb("basis", [P, NBASE, DK, D])
            g.loopw = ms.sb("loopw", [P, DK, D])
            g.xnT = ms.sb("xnT", [P, DK, NP])
            g.dstI = ms.sb("dstI", [P, ET], I32)
            g.typI = ms.sb("typI", [P, ET], I32)
            stage_load(nc, d, g)
            stage_sort(nc, d, g)
            stage_tables(nc, d, g)
            g.ZT = ms.sb("ZT", [P, DK, NBASE, ACCW])
            stage_gather0(nc, d, g)
            stage_bases(nc, d, g)
        g.u = m.sb("u", [P, NT, D])
        g.f1 = m.sb("f1", [P, DK, FF])
        g.f2 = m.sb("f2", [P, FK, D])
        g.rt = m.sb("rt", [P, DK, E1])
        g.mb2 = m.sb("mb2", [E1, D])
        g.we = m.sb("we", [ED + 1, DH])
        g.wo = m.sb("wo", [VG, 3, D])
        g.loaded1 = m.sem("loaded1")
        g.qkv_loaded = m.sem("qkv_loaded")
        stage_experts0(nc, d, g)
        g.weights1 = m.sem("weights1")
        g.S = m.sb("S", [P, KS, H])
        stage_scores(nc, d, g)
        g.oacc = m.sb("oacc", [VG, 3, ACCW])
        stage_maximum(nc, d, g)
        stage_gather1(nc, d, g)
        stage_feed_forward(nc, d, g)
        stage_experts1(nc, d, g)



def edge_columns(a, pad):
    import numpy as np
    return np.ascontiguousarray(np.concatenate([a, np.full(EP - E, pad, a.dtype)]).reshape(ET, P).T)


def layout(i):
    import numpy as np

    def cat(names, shape):
        return np.concatenate([np.asarray(i[n]).reshape(shape) for n in names], axis=1)

    x = np.asarray(i["x"])
    out = {
        "x": np.concatenate([x, np.zeros((NP - N, D), x.dtype)]),
        "src": edge_columns(np.asarray(i["src"]), 0), "dst": edge_columns(np.asarray(i["dst"]), N),
        "typ": edge_columns(np.asarray(i["edge_type_8"]), 0), "ew": edge_columns(np.asarray(i["edge_weight"]), 0),
    }
    ef = np.asarray(i["edge_attr_64"])
    out["ef"] = np.concatenate([ef, np.zeros((EP - E, ED), ef.dtype)])
    out["eft"] = np.ascontiguousarray(out["ef"].T)
    dst = np.asarray(i["dst"])
    line = np.concatenate([dst, np.full(EP + 1 - E, N, dst.dtype)])
    out["line"] = np.ascontiguousarray(np.concatenate([line[:EP].reshape(P, LINE), line[LINE:][::LINE].reshape(P, 1)], axis=1))
    col = {"bias0": "L0_gnn_bias_param", "rb1": "L0_ffn_router_b1", "eb1": "L0_ffn_expert_b1", "eb2": "L0_ffn_expert_b2", "ln1_g": "L1_gnn_ln1_g",
           "ln1_b": "L1_gnn_ln1_b", "ln2_g": "L1_gnn_ln2_g", "ln2_b": "L1_gnn_ln2_b", "bo": "L1_gnn_bo",
           "gb1": "L1_gnn_b1", "mb1": "L1_ffn_b1"}
    out["cols"] = np.ascontiguousarray(np.concatenate([np.asarray(i[col[n]]).reshape(-1, P) for n in COLS]).T)
    row = {"rb2": ["L0_ffn_router_b2"], "qkvb": ["L1_gnn_bq", "L1_gnn_bk", "L1_gnn_bv"],
           "b2": ["L1_gnn_b2"], "alpha": ["L1_gnn_alpha"], "beta": ["L1_gnn_beta"], "comp": ["L0_gnn_comp"]}
    out["rows"] = np.concatenate([cat(row[n], (1, -1)) for n in ROWS], axis=1)
    for name, source in {"basis": "L0_gnn_basis", "loopw": "L0_gnn_loop_weight", "rw1": "L0_ffn_router_w1", "rw2": "L0_ffn_router_w2",
                         "w1": "L0_ffn_expert_w1", "w2": "L0_ffn_expert_w2", "w3": "L0_ffn_expert_w3", "b3": "L0_ffn_expert_b3",
                         "wq": "L1_gnn_Wq", "wk": "L1_gnn_Wk", "wv": "L1_gnn_Wv", "we": "L1_gnn_We", "wo": "L1_gnn_Wo",
                         "f1": "L1_gnn_W1", "f2": "L1_gnn_W2", "mw1": "L1_ffn_w1", "mw2": "L1_ffn_w2", "mb2": "L1_ffn_b2"}.items():
        out[name] = np.asarray(i[source])
    out["be"] = np.asarray(i["L1_gnn_be"]).reshape(1, DH)
    out["rt"] = np.ascontiguousarray(np.asarray(i["L1_ffn_router_w"]).T)
    return {f"in_{n}": a for n, a in out.items()}


def kernel(**inputs):
    import concourse.bacc as _bacc
    from concourse.bass_utils import run_bass_kernel_spmd as _run

    nc = _bacc.Bacc("TRN2", target_bir_lowering=False, num_devices=1)
    program(nc)
    r = _run(nc, [layout(inputs)], core_ids=[0])
    return r.results[0]["out_0"][:N]
```
